# Optimizing a Trainium2 kernel written in Bass

```python
import numpy as np
import jax
import jax.numpy as jnp

def _softmax(x, axis=-1):
    return jax.nn.softmax(x, axis=axis)

def _gelu(x):
    return jax.nn.gelu(x, approximate=True)

def _silu(x):
    return jax.nn.silu(x)

def _sigmoid(x):
    return jax.nn.sigmoid(x)

def _layernorm(x, axis=-1, eps=1e-05):
    m = jnp.mean(x, axis=axis, keepdims=True)
    v = jnp.var(x, axis=axis, keepdims=True)
    return (x - m) / jnp.sqrt(v + eps)

def _scatter_add(tgt, idx, src, axis=0):
    return tgt.at[idx].add(src)

def _segment_sum(src, seg, n):
    return jax.ops.segment_sum(src, seg, n)
kernel_name = 'mk_vit_tower_d2_tok_img256_r4_801280'

def setup_inputs(seed: int=0):
    np.random.seed(seed)
    _w = jnp.asarray

    def _rec_inputs():
        import jax
        import jax.numpy as jnp
        _rk = jax.random.key(seed)
        x = -0.000209053 + 0.999977 * jax.random.normal(jax.random.fold_in(_rk, 1), (8, 64, 56, 56), jnp.float32)
        return x
    x = _rec_inputs()

    def _L0_tok_setup():
        import jax, jax.numpy as jnp
        import numpy as np
        B, EMB, HT, WD = (32, 64, 56, 56)
        NH, WS, SHIFTED = (8, 4, True)

        def _rel_indices(ws):
            coords = np.array([[i, j] for i in range(ws) for j in range(ws)])
            rel = coords[None, :, :] - coords[:, None, :] + ws - 1
            return jnp.asarray(rel)

        def _shift_masks(ws):
            m = np.zeros((ws * ws, ws * ws), np.float32)
            s = ws * (ws // 2)
            m[-s:, :-s] = -np.inf
            m[:-s, -s:] = -np.inf
            col = m.reshape(ws, ws, ws, ws).transpose(1, 0, 3, 2).reshape(ws * ws, ws * ws)
            return (jnp.asarray(m), jnp.asarray(col))
        key = jax.random.key(seed)
        ks = jax.random.split(key, 6)
        x = jax.random.normal(ks[0], (B, EMB, HT, WD), jnp.float32)
        s = 1.0 / np.sqrt(EMB)
        w1 = jax.random.uniform(ks[1], (3 * EMB, EMB), jnp.float32, -s, s)
        b1 = jax.random.uniform(ks[2], (3 * EMB,), jnp.float32, -s, s)
        w2 = jax.random.uniform(ks[3], (EMB, EMB), jnp.float32, -s, s)
        b2 = jax.random.uniform(ks[4], (EMB,), jnp.float32, -s, s)
        pos_emb = jax.random.normal(ks[5], (2 * WS - 1, 2 * WS - 1), jnp.float32)
        return {'x': x, 'w1': w1, 'b1': b1, 'w2': w2, 'b2': b2, 'pos_emb': pos_emb}
    _L0_tok_all = _L0_tok_setup()
    _L0_tok_in = {k: v for k, v in _L0_tok_all.items() if k in ('w1', 'b1', 'w2', 'b2', 'pos_emb')}
    del _L0_tok_all

    def _L0_attn_setup():
        import jax, jax.numpy as jnp
        import numpy as np
        B, T, C = (16, 512, 64)
        TT = T
        LAYER_ID, N_LAYER = (3, 6)
        key = jax.random.key(seed)
        ks = jax.random.split(key, 6)
        ratio_0_to_1 = LAYER_ID / (N_LAYER - 1)
        ratio_1_to_almost0 = 1.0 - LAYER_ID / N_LAYER
        h = np.arange(TT, dtype=np.float32)
        decay_speed = -5.0 + 8.0 * (h / (TT - 1)) ** (0.7 + 1.3 * ratio_0_to_1)
        curve = -(TT - 1 - h)
        time_w = jnp.asarray(np.exp(np.clip(curve * decay_speed, -30.0, 0.0)), dtype=jnp.float32)
        i = np.arange(C, dtype=np.float32) / C
        time_mix_k = jnp.asarray((i ** ratio_1_to_almost0).reshape(1, 1, C), dtype=jnp.float32)
        time_mix_v = jnp.asarray((i ** ratio_1_to_almost0 + 0.3 * ratio_0_to_1).reshape(1, 1, C), dtype=jnp.float32)
        time_mix_r = jnp.asarray((i ** (0.5 * ratio_1_to_almost0)).reshape(1, 1, C), dtype=jnp.float32)
        x = jax.random.normal(ks[0], (B, T, C), dtype=jnp.float32)
        scale = 0.02
        Wk = scale * jax.random.normal(ks[1], (C, C), dtype=jnp.float32)
        Wv = scale * jax.random.normal(ks[2], (C, C), dtype=jnp.float32)
        Wr = scale * jax.random.normal(ks[3], (C, C), dtype=jnp.float32)
        Wo = scale * jax.random.normal(ks[4], (C, C), dtype=jnp.float32)
        return {'x': x, 'time_w': time_w, 'time_mix_k': time_mix_k, 'time_mix_v': time_mix_v, 'time_mix_r': time_mix_r, 'Wk': Wk, 'Wv': Wv, 'Wr': Wr, 'Wo': Wo}
    _L0_attn_all = _L0_attn_setup()
    _L0_attn_in = {k: v for k, v in _L0_attn_all.items() if k in ('time_w', 'time_mix_k', 'time_mix_v', 'time_mix_r', 'Wk', 'Wv', 'Wr', 'Wo')}
    del _L0_attn_all

    def _L0_ffn_setup():
        import jax, jax.numpy as jnp
        import numpy as np
        C = 64
        HID = 256
        E = 8
        TEMP = 1.0
        key = jax.random.key(seed)
        ks = jax.random.split(key, 7)
        x = jax.random.normal(ks[0], (8, 4096, C), dtype=jnp.float32)
        W1 = jax.random.normal(ks[1], (C, HID), dtype=jnp.float32) * 0.02
        b1 = jnp.zeros((HID,), dtype=jnp.float32)
        Wg = jax.random.normal(ks[2], (HID, E), dtype=jnp.float32) * 0.02
        bg = jnp.zeros((E,), dtype=jnp.float32)
        Wd = jax.random.normal(ks[3], (E, HID, C), dtype=jnp.float32) * 0.02
        bd = jnp.zeros((E, C), dtype=jnp.float32)
        return {'x': x, 'W1': W1, 'b1': b1, 'Wg': Wg, 'bg': bg, 'Wd': Wd, 'bd': bd}
    _L0_ffn_all = _L0_ffn_setup()
    _L0_ffn_in = {k: v for k, v in _L0_ffn_all.items() if k in ('W1', 'b1', 'Wg', 'bg', 'Wd', 'bd')}
    del _L0_ffn_all

    def _L1_attn_setup():
        import jax, jax.numpy as jnp
        import numpy as np
        B, S, I, H, O = (64, 128, 64, 256, 64)

        def _rnn_layer(inp, W_ih, W_hh, b_ih, b_hh):
            pre = jnp.einsum('bsi,hi->bsh', inp, W_ih) + (b_ih + b_hh)
            h0 = jnp.zeros((inp.shape[0], W_hh.shape[0]), dtype=inp.dtype)

            def step(h, p_t):
                h = jnp.tanh(p_t + h @ W_hh.T)
                return (h, h)
            _, hs = jax.lax.scan(step, h0, jnp.swapaxes(pre, 0, 1))
            return jnp.swapaxes(hs, 0, 1)
        key = jax.random.key(seed)
        ks = jax.random.split(key, 12)
        s_in = 1.0 / np.sqrt(H)
        inp = {'x': jax.random.normal(ks[0], (B, S, I), dtype=jnp.float32), 'W_ih_0': jax.random.uniform(ks[1], (H, I), jnp.float32, -s_in, s_in), 'W_hh_0': jax.random.uniform(ks[2], (H, H), jnp.float32, -s_in, s_in), 'b_ih_0': jax.random.uniform(ks[3], (H,), jnp.float32, -s_in, s_in), 'b_hh_0': jax.random.uniform(ks[4], (H,), jnp.float32, -s_in, s_in), 'W_ih_1': jax.random.uniform(ks[5], (H, H), jnp.float32, -s_in, s_in), 'W_hh_1': jax.random.uniform(ks[6], (H, H), jnp.float32, -s_in, s_in), 'b_ih_1': jax.random.uniform(ks[7], (H,), jnp.float32, -s_in, s_in), 'b_hh_1': jax.random.uniform(ks[8], (H,), jnp.float32, -s_in, s_in), 'fc_w': jax.random.uniform(ks[9], (O, H), jnp.float32, -s_in, s_in), 'fc_b': jax.random.uniform(ks[10], (O,), jnp.float32, -s_in, s_in)}
        return inp
    _L1_attn_all = _L1_attn_setup()
    _L1_attn_in = {k: v for k, v in _L1_attn_all.items() if k in ('W_ih_0', 'W_hh_0', 'b_ih_0', 'b_hh_0', 'W_ih_1', 'W_hh_1', 'b_ih_1', 'b_hh_1', 'fc_w', 'fc_b')}
    del _L1_attn_all

    def _L1_ffn_setup():
        import jax, jax.numpy as jnp
        import numpy as np
        B, T, D, H, E = (16, 1024, 64, 128, 8)
        key = jax.random.key(seed)
        ks = jax.random.split(key, 5)
        x = jax.random.normal(ks[0], (B, T, D), dtype=jnp.float32)
        gate_w = jax.random.normal(ks[1], (D, E), dtype=jnp.float32) * 0.02
        gate_b = jnp.zeros((E,), dtype=jnp.float32)
        W1 = jax.random.normal(ks[2], (E, D, H), dtype=jnp.float32) * 0.02
        b1 = jnp.zeros((E, H), dtype=jnp.float32)
        W2 = jax.random.normal(ks[3], (E, H, D), dtype=jnp.float32) * 0.02
        b2 = jnp.zeros((E, D), dtype=jnp.float32)
        return {'x': x, 'gate_w': gate_w, 'gate_b': gate_b, 'W1': W1, 'b1': b1, 'W2': W2, 'b2': b2}
    _L1_ffn_all = _L1_ffn_setup()
    _L1_ffn_in = {k: v for k, v in _L1_ffn_all.items() if k in ('gate_w', 'gate_b', 'W1', 'b1', 'W2', 'b2')}
    del _L1_ffn_all
    return {'x': x, 'L0_tok_w1': _L0_tok_in['w1'], 'L0_tok_b1': _L0_tok_in['b1'], 'L0_tok_w2': _L0_tok_in['w2'], 'L0_tok_b2': _L0_tok_in['b2'], 'L0_tok_pos_emb': _L0_tok_in['pos_emb'], 'L0_attn_time_w': _L0_attn_in['time_w'], 'L0_attn_time_mix_k': _L0_attn_in['time_mix_k'], 'L0_attn_time_mix_v': _L0_attn_in['time_mix_v'], 'L0_attn_time_mix_r': _L0_attn_in['time_mix_r'], 'L0_attn_Wk': _L0_attn_in['Wk'], 'L0_attn_Wv': _L0_attn_in['Wv'], 'L0_attn_Wr': _L0_attn_in['Wr'], 'L0_attn_Wo': _L0_attn_in['Wo'], 'L0_ffn_W1': _L0_ffn_in['W1'], 'L0_ffn_b1': _L0_ffn_in['b1'], 'L0_ffn_Wg': _L0_ffn_in['Wg'], 'L0_ffn_bg': _L0_ffn_in['bg'], 'L0_ffn_Wd': _L0_ffn_in['Wd'], 'L0_ffn_bd': _L0_ffn_in['bd'], 'L1_attn_W_ih_0': _L1_attn_in['W_ih_0'], 'L1_attn_W_hh_0': _L1_attn_in['W_hh_0'], 'L1_attn_b_ih_0': _L1_attn_in['b_ih_0'], 'L1_attn_b_hh_0': _L1_attn_in['b_hh_0'], 'L1_attn_W_ih_1': _L1_attn_in['W_ih_1'], 'L1_attn_W_hh_1': _L1_attn_in['W_hh_1'], 'L1_attn_b_ih_1': _L1_attn_in['b_ih_1'], 'L1_attn_b_hh_1': _L1_attn_in['b_hh_1'], 'L1_attn_fc_w': _L1_attn_in['fc_w'], 'L1_attn_fc_b': _L1_attn_in['fc_b'], 'L1_ffn_gate_w': _L1_ffn_in['gate_w'], 'L1_ffn_gate_b': _L1_ffn_in['gate_b'], 'L1_ffn_W1': _L1_ffn_in['W1'], 'L1_ffn_b1': _L1_ffn_in['b1'], 'L1_ffn_W2': _L1_ffn_in['W2'], 'L1_ffn_b2': _L1_ffn_in['b2']}

def reference(x, L0_tok_w1, L0_tok_b1, L0_tok_w2, L0_tok_b2, L0_tok_pos_emb, L0_attn_time_w, L0_attn_time_mix_k, L0_attn_time_mix_v, L0_attn_time_mix_r, L0_attn_Wk, L0_attn_Wv, L0_attn_Wr, L0_attn_Wo, L0_ffn_W1, L0_ffn_b1, L0_ffn_Wg, L0_ffn_bg, L0_ffn_Wd, L0_ffn_bd, L1_attn_W_ih_0, L1_attn_W_hh_0, L1_attn_b_ih_0, L1_attn_b_hh_0, L1_attn_W_ih_1, L1_attn_W_hh_1, L1_attn_b_ih_1, L1_attn_b_hh_1, L1_attn_fc_w, L1_attn_fc_b, L1_ffn_gate_w, L1_ffn_gate_b, L1_ffn_W1, L1_ffn_b1, L1_ffn_W2, L1_ffn_b2):
    import jax
    import jax.numpy as jnp

    def _L0_tok_ref(x, w1, b1, w2, b2, pos_emb):
        import jax, jax.numpy as jnp
        import numpy as np
        B, EMB, HT, WD = (32, 64, 56, 56)
        NH, WS, SHIFTED = (8, 4, True)

        def _rel_indices(ws):
            coords = np.array([[i, j] for i in range(ws) for j in range(ws)])
            rel = coords[None, :, :] - coords[:, None, :] + ws - 1
            return jnp.asarray(rel)

        def _shift_masks(ws):
            m = np.zeros((ws * ws, ws * ws), np.float32)
            s = ws * (ws // 2)
            m[-s:, :-s] = -np.inf
            m[:-s, -s:] = -np.inf
            col = m.reshape(ws, ws, ws, ws).transpose(1, 0, 3, 2).reshape(ws * ws, ws * ws)
            return (jnp.asarray(m), jnp.asarray(col))
        b, c, ht, wd = x.shape
        ws, nh = (WS, NH)
        e = c // nh
        xt = x.reshape(b, c, ht * wd).transpose(0, 2, 1)
        qkv = xt @ w1.T + b1
        qkv = qkv.reshape(b, ht, wd, c, 3)
        if SHIFTED:
            qkv = jnp.roll(qkv, (-ws // 2, -ws // 2), axis=(1, 2))
        Wh, Ww = (ht // ws, wd // ws)
        qkv = qkv.reshape(b, Wh, ws, Ww, ws, e, nh, 3)
        qkv = qkv.transpose(0, 6, 1, 3, 2, 4, 5, 7).reshape(b, nh, Wh, Ww, ws * ws, e, 3)
        Q, K, V = (qkv[..., 0], qkv[..., 1], qkv[..., 2])
        scale = jnp.sqrt(jnp.float32(c / nh))
        wei = jnp.einsum('bhijpe,bhijqe->bhijpq', Q, K) / scale
        rel = _rel_indices(ws)
        wei = wei + pos_emb[rel[..., 0], rel[..., 1]]
        if SHIFTED:
            row_mask, col_mask = _shift_masks(ws)
            wei = wei.at[:, :, -1, :].add(row_mask)
            wei = wei.at[:, :, :, -1].add(col_mask)
        attn = jax.nn.softmax(wei, axis=-1)
        out = jnp.einsum('bhijpq,bhijqe->bhijpe', attn, V)
        out = out.reshape(b, nh, Wh, Ww, ws, ws, e)
        out = out.transpose(0, 2, 4, 3, 5, 1, 6).reshape(b, ht, wd, nh * e)
        out = out.reshape(b, ht * wd, c)
        return out @ w2.T + b2

    def _L0_attn_ref(x, time_w, time_mix_k, time_mix_v, time_mix_r, Wk, Wv, Wr, Wo):
        import jax, jax.numpy as jnp
        import numpy as np
        B, T, C = (16, 512, 64)
        TT = T
        LAYER_ID, N_LAYER = (3, 6)
        Bx, Tx, Cx = x.shape
        maxlen = time_w.shape[0]
        xx = jnp.pad(x, ((0, 0), (1, 0), (0, 0)))[:, :-1]
        xk = x * time_mix_k + xx * (1.0 - time_mix_k)
        xv = x * time_mix_v + xx * (1.0 - time_mix_v)
        xr = x * time_mix_r + xx * (1.0 - time_mix_r)
        k = jnp.exp(jnp.clip(xk @ Wk, -60.0, 30.0))
        v = xv @ Wv
        r = xr @ Wr
        sum_k = jnp.cumsum(k, axis=1)
        kv = k * v
        t_idx = jnp.arange(Tx)
        d = t_idx[:, None] - t_idx[None, :]
        W = jnp.where(d >= 0, time_w[jnp.clip(maxlen - 1 - d, 0, maxlen - 1)], 0.0)
        wkv = jnp.einsum('tu,buc->btc', W, kv)
        rwkv = jax.nn.sigmoid(r) * wkv / sum_k
        return rwkv @ Wo

    def _L0_ffn_ref(x, W1, b1, Wg, bg, Wd, bd):
        import jax, jax.numpy as jnp
        import numpy as np
        C = 64
        HID = 256
        E = 8
        TEMP = 1.0
        orig_shape = x.shape
        xf = x.reshape(-1, orig_shape[-1])
        H = jax.nn.gelu(xf @ W1 + b1, approximate=False)
        probs = jax.nn.softmax((H @ Wg + bg) / TEMP, axis=-1)
        assign = jnp.argmax(probs, axis=-1)
        out = jnp.zeros_like(xf)
        for e in range(Wd.shape[0]):
            y = H @ Wd[e] + bd[e]
            sel = (assign == e)[:, None]
            out = out + jnp.where(sel, probs[:, e:e + 1] * y, 0.0)
        return out.reshape(orig_shape)

    def _L1_attn_ref(x, W_ih_0, W_hh_0, b_ih_0, b_hh_0, W_ih_1, W_hh_1, b_ih_1, b_hh_1, fc_w, fc_b):
        import jax, jax.numpy as jnp
        import numpy as np
        B, S, I, H, O = (64, 128, 64, 256, 64)

        def _rnn_layer(inp, W_ih, W_hh, b_ih, b_hh):
            pre = jnp.einsum('bsi,hi->bsh', inp, W_ih) + (b_ih + b_hh)
            h0 = jnp.zeros((inp.shape[0], W_hh.shape[0]), dtype=inp.dtype)

            def step(h, p_t):
                h = jnp.tanh(p_t + h @ W_hh.T)
                return (h, h)
            _, hs = jax.lax.scan(step, h0, jnp.swapaxes(pre, 0, 1))
            return jnp.swapaxes(hs, 0, 1)
        h = _rnn_layer(x, W_ih_0, W_hh_0, b_ih_0, b_hh_0)
        h = _rnn_layer(h, W_ih_1, W_hh_1, b_ih_1, b_hh_1)
        return h @ fc_w.T + fc_b

    def _L1_ffn_ref(x, gate_w, gate_b, W1, b1, W2, b2):
        import jax, jax.numpy as jnp
        import numpy as np
        B, T, D, H, E = (16, 1024, 64, 128, 8)
        Bb, Tt, Dd = x.shape
        Ee = gate_w.shape[1]
        xf = x.reshape(-1, Dd)
        N = xf.shape[0]
        logits = xf @ gate_w + gate_b
        probs = jax.nn.softmax(logits, axis=-1)
        top2_vals, top2_idx = jax.lax.top_k(probs, 2)
        cw = jnp.zeros((N, Ee), dtype=xf.dtype).at[jnp.arange(N)[:, None], top2_idx].add(top2_vals)

        def step(acc, params):
            w1, bb1, w2, bb2, we = params
            h = jax.nn.gelu(xf @ w1 + bb1, approximate=False)
            y = h @ w2 + bb2
            return (acc + we[:, None] * y, None)
        out, _ = jax.lax.scan(step, jnp.zeros_like(xf), (W1, b1, W2, b2, cw.T))
        return out.reshape(Bb, Tt, Dd)
    h = _L0_tok_ref(x, L0_tok_w1, L0_tok_b1, L0_tok_w2, L0_tok_b2, L0_tok_pos_emb)
    h = h + _L0_attn_ref(_layernorm(h, axis=-1), L0_attn_time_w, L0_attn_time_mix_k, L0_attn_time_mix_v, L0_attn_time_mix_r, L0_attn_Wk, L0_attn_Wv, L0_attn_Wr, L0_attn_Wo)
    h = h + _L0_ffn_ref(_layernorm(h, axis=-1), L0_ffn_W1, L0_ffn_b1, L0_ffn_Wg, L0_ffn_bg, L0_ffn_Wd, L0_ffn_bd)
    h = h + _L1_attn_ref(_layernorm(h, axis=-1), L1_attn_W_ih_0, L1_attn_W_hh_0, L1_attn_b_ih_0, L1_attn_b_hh_0, L1_attn_W_ih_1, L1_attn_W_hh_1, L1_attn_b_ih_1, L1_attn_b_hh_1, L1_attn_fc_w, L1_attn_fc_b)
    h = h + _L1_ffn_ref(_layernorm(h, axis=-1), L1_ffn_gate_w, L1_ffn_gate_b, L1_ffn_W1, L1_ffn_b1, L1_ffn_W2, L1_ffn_b2)
    return h

_drawn_inputs = setup_inputs


def setup_inputs(seed=0):
    import zlib

    import numpy as np

    out = dict(_drawn_inputs(seed))
    spreads = {'L0_ffn_b1': (0.0, 0.378),
     'L0_ffn_bg': (0.0, 0.275),
     'L0_ffn_bd': (0.0, 0.1),
     'L1_ffn_gate_b': (0.0, 0.1),
     'L1_ffn_b1': (0.0, 0.647),
     'L1_ffn_b2': (0.0, 0.1)}
    factors = {'L0_attn_time_w': 5.319,
     'L0_attn_time_mix_k': 8.0,
     'L0_attn_time_mix_v': 8.0,
     'L0_attn_time_mix_r': 8.0,
     'L0_attn_Wk': 8.0,
     'L0_attn_Wr': 8.0,
     'L0_ffn_Wg': 8.0,
     'L1_ffn_W1': 2.953}
    for name, (base, spread) in spreads.items():
        noise = np.random.default_rng([zlib.crc32(name.encode()), seed]).standard_normal(out[name].shape)
        drawn = base * np.exp(spread * noise) if base else spread * noise
        out[name] = jnp.asarray(drawn.astype(out[name].dtype))
    for name, factor in factors.items():
        out[name] = (out[name] * factor).astype(out[name].dtype)
    return out
```

```python
from contextlib import ExitStack

import numpy as np

import concourse.bass as bass
from concourse import mybir

F32 = mybir.dt.float32
ALU = mybir.AluOpType
ACT = mybir.ActivationFunctionType
X = mybir.AxisListType.X

B, C, HT, WD = 8, 64, 56, 56
TOKENS = HT * WD
WS, NH = 4, 8
HEAD = C // NH
STRIPS = HT // WS
WCOLS = WD // WS
WINDOWS = B * WCOLS
WTOK = WS * WS
TB = 2 * WD
NBLK = TOKENS // TB
BC = B * C
PAIRS = B // 2
PW = 2 * C
MAXLEN = 512
BAND = (MAXLEN - 2 + TB) // TB + 1
HID = 256
EXPERTS = 8
MHID = 128
HALF_TOK = PAIRS * TB
STEP_LOOP = 64
XCHUNK = 16
QUAD = 32
EPS = 1e-5
NEG = -1.0e30


def pipeline(eng, stages, n, tail=0):
    head, most = 4, max(lag for lag, _ in stages)

    def step(t, n_blocks):
        for lag, stage in stages:
            if 0 <= t - lag < n_blocks:
                stage(t - lag, (t - lag) % 2)

    for t in range(head):
        step(t, n)
    with eng.Fori(head // 2, (n - tail) // 2) as pair:
        first = eng.snap(pair * 2)
        for par in range(2):
            for lag, stage in stages:
                stage(first + (par - lag), (par - lag) % 2)
    for t in range(n - tail, n + most):
        step(t, n)


def wait_count(eng, sem, i, per, offset):
    if isinstance(i, int) and i * per + offset <= 0:
        return
    eng.wait_ge(sem, i * per + offset)


def wait_former(eng, sem, i, per=1, ago=2):
    wait_count(eng, sem, i, per, (1 - ago) * per)


def wait_load(eng, sems, i, par):
    eng.wait_ge(sems[par], i * 8 + (16 - 8 * par))


def block_cols(t, i, width=BC):
    return t[:, bass.ds(i * width, width)]


def by_batch(ap, n=B):
    return ap.rearrange("p (b c) -> p b c", b=n)


class Norm:

    def __init__(self, nc, ctx, hidden, name):
        sb = lambda n, s: ctx.enter_context(nc.sbuf_tensor(f"{name}_{n}", s, F32))
        sem = lambda n: ctx.enter_context(nc.semaphore(f"{name}_{n}"))
        self.hidden = hidden
        self.negmean = sb("negmean", [TB, 2, B])
        self.sumsq = sb("sumsq", [TB, 2, B])
        self.rstd = sb("rstd", [TB, 2, B])
        self.minus_half = sb("minus_half", [TB, B])
        self.centred = sb("centred", [TB, 2, BC])
        self.squares = sb("squares", [TB, 2, BC])
        self.xn = sb("xn", [TB, 2, BC])
        self.total_ready, self.mean_ready = sem("total_ready"), sem("mean_ready")
        self.centred_ready, self.squares_ready = sem("centred_ready"), sem("squares_ready")
        self.sumsq_ready, self.var_ready = sem("sumsq_ready"), sem("var_ready")
        self.rstd_ready, self.xn_ready = sem("rstd_ready"), sem("xn_ready")
        self.half_set = sem("half_set")

    def vector_centre(self, dve, i, par):
        h = by_batch(block_cols(self.hidden, i))
        dve.tensor_reduce(self.negmean[:, par], h, X, ALU.add).then_inc(self.total_ready, 1)
        dve.wait_ge(self.total_ready, i + 1)
        dve.tensor_scalar(self.negmean[:, par], self.negmean[:, par], -1.0 / C, None, ALU.mult)\
           .then_inc(self.mean_ready, 1)
        dve.wait_ge(self.mean_ready, i + 1)
        wait_former(dve, self.xn_ready, i)
        dve.tensor_tensor(by_batch(self.centred[:, par]), h,
                          self.negmean[:, par].unsqueeze(2).broadcast_to([TB, B, C]), ALU.add)\
           .then_inc(self.centred_ready, 1)

    def scalar(self, act, i, par):
        act.wait_ge(self.centred_ready, i + 1)
        wait_former(act, self.sumsq_ready, i)
        act.activation(self.squares[:, par], self.centred[:, par], ACT.Square)\
           .then_inc(self.squares_ready, 1)

    def vector_sum(self, dve, i, par):
        dve.wait_ge(self.squares_ready, i + 1)
        wait_former(dve, self.xn_ready, i)
        dve.tensor_reduce(self.sumsq[:, par], by_batch(self.squares[:, par]), X, ALU.add)\
           .then_inc(self.sumsq_ready, 1)
        dve.wait_ge(self.sumsq_ready, i + 1)
        dve.tensor_scalar(self.rstd[:, par], self.sumsq[:, par], 1.0 / C, EPS, ALU.mult, ALU.add)\
           .then_inc(self.var_ready, 1)

    def bind_centre(self, dve):
        return lambda i, par: self.vector_centre(dve, i, par)

    def bind_sum(self, dve):
        return lambda i, par: self.vector_sum(dve, i, par)

    def bind_scalar(self, act):
        return lambda i, par: self.scalar(act, i, par)

    def bind_gpsimd(self, pool, turned):
        return lambda i, par: self.gpsimd(pool, i, par, turned)

    def gpsimd_setup(self, pool):
        pool.memset(self.minus_half[:], -0.5).then_inc(self.half_set, 1)
        pool.wait_ge(self.half_set, 1)

    def gpsimd(self, pool, i, par, turned):
        pool.wait_ge(self.var_ready, i + 1)
        pool.tensor_tensor(self.rstd[:, par], self.rstd[:, par], self.minus_half[:], ALU.pow)\
            .then_inc(self.rstd_ready, 1)
        pool.wait_ge(self.rstd_ready, i + 1)
        wait_former(pool, turned, i)
        pool.tensor_tensor(by_batch(self.xn[:, par]), by_batch(self.centred[:, par]),
                           self.rstd[:, par].unsqueeze(2).broadcast_to([TB, B, C]), ALU.mult)\
            .then_inc(self.xn_ready, 1)


def window_attention(nc, hidden, ident, bank, d):
    VHEADS = 5
    with ExitStack() as ctx:
        sb = lambda n, s: ctx.enter_context(nc.sbuf_tensor(f"wa_{n}", s, F32))
        sem = lambda n: ctx.enter_context(nc.semaphore(f"wa_{n}"))
        K1 = C + 1
        xs = [sb(f"xs{p}", [K1, WTOK, WINDOWS]) for p in range(2)]
        w_qkv, w_out = sb("w_qkv", [K1, 3 * C]), sb("w_out", [K1, C])
        qkv = [sb(f"qkv{p}", [WINDOWS, WTOK, 3, HEAD, NH]) for p in range(2)]
        bias, last_bias = sb("bias", [WINDOWS, WTOK, WTOK]), sb("last_bias", [WINDOWS, WTOK, WTOK])
        colmask, rowmask = sb("colmask", [WINDOWS, WTOK, WTOK]), sb("rowmask", [WINDOWS, WTOK, WTOK])
        out = [sb(f"att_out{p}", [WINDOWS, WTOK, HEAD, NH]) for p in range(2)]
        outT = [sb(f"outT{p}", [K1, B, WS, WD]) for p in range(2)]
        groups = []
        for g, (h0, h1) in enumerate(((0, VHEADS), (VHEADS, NH))):
            n = h1 - h0
            groups.append(dict(
                heads=slice(h0, h1), n=n,
                score=[sb(f"score{g}{p}", [WINDOWS, WTOK, WTOK, n]) for p in range(2)],
                prod=sb(f"prod{g}", [WINDOWS, WTOK, WTOK, n]),
                top=sb(f"top{g}", [WINDOWS, WTOK, n]), total=sb(f"total{g}", [WINDOWS, WTOK, n]),
                inverse=[sb(f"inverse{g}{p}", [WINDOWS, WTOK, n]) for p in range(2)],
                acc=sb(f"acc{g}", [WINDOWS, WTOK, HEAD, n]), part=sb(f"part{g}", [WINDOWS, WTOK, HEAD, n]),
                **{s: sem(f"{s}{g}") for s in ("qk_chain", "scored", "topped", "shifted", "exped",
                                               "summed", "inverted", "pv_chain", "done")}))
        p_qkv, p_outT, p_h = bank[0:4], bank[4:6], bank[6:8]
        loaded, ones_set, ready = sem("loaded"), sem("ones_set"), sem("ready")
        x_loaded = [sem(f"x_loaded{p}") for p in range(2)]
        qkv_mm, qkv_copied = sem("qkv_mm"), sem("qkv_copied")
        turned, turned_copied = sem("turned"), sem("turned_copied")
        projected, written = sem("projected"), sem("written")
        block = ctx.enter_context(nc.Block())

        @block.sync
        def _(sp):
            flat = lambda t: t[:].rearrange("p q k -> p (q k)")
            sp.dma_start(w_qkv[:], d["w_qkv"]).then_inc(loaded, 16)
            sp.dma_start(w_out[:], d["w_out"]).then_inc(loaded, 16)
            sp.dma_start(ident[:], d["ident"]).then_inc(loaded, 16)
            sp.dma_start(flat(bias), d["pos_bias"].partition_broadcast(WINDOWS)).then_inc(loaded, 16)
            sp.dma_start(flat(colmask), d["colmask"]).then_inc(loaded, 16)
            sp.dma_start(flat(rowmask), d["rowmask"].partition_broadcast(WINDOWS)).then_inc(loaded, 16)

            def load(i, par):
                wait_former(sp, qkv_mm, i, 8)
                sp.dma_start(xs[par][0:C].rearrange("c t w -> c (t w)"),
                             d["x"][bass.ds(i, 1)].rearrange("o c n -> (o c) n")).then_inc(x_loaded[par], 16)

            pipeline(sp, [(0, load)], STRIPS)

        @block.tensor
        def _(pe):
            pe.wait_ge(loaded, 96)
            pe.wait_ge(ones_set, 4)
            pe.wait_ge(ready, 3)

            def make_qkv(i, par):
                wait_load(pe, x_loaded, i, par)
                for t in range(WTOK):
                    if t % 2 == 0:
                        wait_count(pe, qkv_copied, i, 8, t // 2 - 3)
                    mm = pe.matmul(p_qkv[t // 2 % 4][0:WINDOWS, 192 * (t % 2):192 * (t % 2) + 192],
                                   xs[par][:, t], w_qkv[:], start=True, stop=True)
                    if t % 2:
                        mm.then_inc(qkv_mm, 1)

            def project(i, par):
                for g in groups:
                    pe.wait_ge(g["done"], i + 1)
                for r in range(WS):
                    wait_count(pe, turned_copied, i, 4, r - 1)
                    for c in range(WS):
                        tr = pe.matmul(p_outT[r % 2][0:C, c * WINDOWS:(c + 1) * WINDOWS],
                                       out[par][:, r * WS + c].rearrange("p e h -> p (e h)"),
                                       ident[0:WINDOWS, 0:WINDOWS], start=True, stop=True)
                    tr.then_inc(turned, 1)
                pe.wait_ge(turned_copied, i * 4 + 4)
                for half in range(2):
                    wait_count(pe, written, i, 2, half - 1)
                    for b in range(B):
                        mm = pe.matmul(p_h[half][0:TB, b * C:(b + 1) * C],
                                       outT[par][:, b, 2 * half:2 * half + 2, :].rearrange("c r w -> c (r w)"),
                                       w_out[:], start=True, stop=True)
                    mm.then_inc(projected, 1)

            pipeline(pe, [(0, make_qkv), (1, project)], STRIPS)

        @block.scalar
        def _(act):
            def copy_qkv(i, par):
                for g in groups:
                    wait_former(act, g["done"], i)
                for t in range(WTOK // 2):
                    act.wait_ge(qkv_mm, i * 8 + (t + 1))
                    act.activation(qkv[par][:, 2 * t:2 * t + 2].rearrange("p t s e h -> p (t s e h)"),
                                   p_qkv[t % 4][0:WINDOWS, 0:384], ACT.Copy).then_inc(qkv_copied, 1)

            def exps(i, par):
                for g in groups:
                    act.wait_ge(g["shifted"], i + 1)
                    act.activation(g["score"][par][:], g["score"][par][:], ACT.Exp).then_inc(g["exped"], 1)

            def copy_out(i, par):
                wait_former(act, projected, i, 2)
                for r in range(WS):
                    act.wait_ge(turned, i * 4 + (r + 1))
                    for c in range(WS):
                        cp = act.activation(
                            outT[par][0:C, :, r, c::WS],
                            p_outT[r % 2][0:C, c * WINDOWS:(c + 1) * WINDOWS].rearrange("p (b w) -> p b w", b=B),
                            ACT.Copy)
                    cp.then_inc(turned_copied, 1)
                for half in range(2):
                    act.wait_ge(projected, i * 2 + (half + 1))
                    act.activation(block_cols(hidden, i * 2 + half), p_h[half][0:TB, :], ACT.Copy)\
                       .then_inc(written, 1)

            pipeline(act, [(0, copy_qkv), (1, copy_out), (0, exps)], STRIPS)

        def scores(eng, g, i, par):
            score, shape = g["score"][par], [WINDOWS, WTOK, WTOK, g["n"]]
            q, k, _ = (qkv[par][:, :, s, :, g["heads"]] for s in range(3))
            made, steps = 0, 2 * HEAD - 1
            eng.wait_ge(qkv_copied, i * 8 + 8)
            wait_former(eng, g["done"], i)
            for e in range(HEAD):
                qe = q[:, :, e].unsqueeze(2).broadcast_to(shape)
                ke = k[:, :, e].unsqueeze(1).broadcast_to(shape)
                eng.tensor_tensor(g["prod"][:] if e else score[:], qe, ke, ALU.mult).then_inc(g["qk_chain"], 1)
                made += 1
                eng.wait_ge(g["qk_chain"], i * steps + made)
                if e:
                    eng.tensor_tensor(score[:], score[:], g["prod"][:], ALU.add).then_inc(g["qk_chain"], 1)
                    made += 1
                    eng.wait_ge(g["qk_chain"], i * steps + made)
            which = last_bias if isinstance(i, int) and i == STRIPS - 1 else bias
            eng.tensor_tensor(score[:], score[:], which[:].unsqueeze(3).broadcast_to(shape), ALU.add)\
               .then_inc(g["scored"], 1)

        def shift(dve, g, i, par):
            score = g["score"][par]
            dve.wait_ge(g["scored"], i + 1)
            dve.tensor_reduce(g["top"][:], score[:].rearrange("p q k h -> p q h k"), X, ALU.max)\
               .then_inc(g["topped"], 1)
            dve.wait_ge(g["topped"], i + 1)
            dve.tensor_tensor(score[:], score[:], g["top"][:].unsqueeze(2).broadcast_to([WINDOWS, WTOK, WTOK, g["n"]]),
                              ALU.subtract).then_inc(g["shifted"], 1)

        def invert(dve, g, i, par):
            dve.wait_ge(g["exped"], i + 1)
            wait_former(dve, g["done"], i)
            dve.tensor_reduce(g["total"][:], g["score"][par][:].rearrange("p q k h -> p q h k"), X, ALU.add)\
               .then_inc(g["summed"], 1)
            dve.wait_ge(g["summed"], i + 1)
            dve.reciprocal(g["inverse"][par][:], g["total"][:]).then_inc(g["inverted"], 1)

        def values(eng, g, i, par):
            oshape, v = [WINDOWS, WTOK, HEAD, g["n"]], qkv[par][:, :, 2, :, g["heads"]]
            made, steps = 0, 2 * WTOK - 1
            eng.wait_ge(g["exped"], i + 1)
            for t in range(WTOK):
                w = g["score"][par][:, :, t].unsqueeze(2).broadcast_to(oshape)
                vt = v[:, t].unsqueeze(1).broadcast_to(oshape)
                eng.tensor_tensor(g["part"][:] if t else g["acc"][:], w, vt, ALU.mult).then_inc(g["pv_chain"], 1)
                made += 1
                eng.wait_ge(g["pv_chain"], i * steps + made)
                if t:
                    eng.tensor_tensor(g["acc"][:], g["acc"][:], g["part"][:], ALU.add).then_inc(g["pv_chain"], 1)
                    made += 1
                    eng.wait_ge(g["pv_chain"], i * steps + made)
            eng.wait_ge(g["inverted"], i + 1)
            wait_former(eng, turned, i, 4)
            eng.tensor_tensor(out[par][:, :, :, g["heads"]], g["acc"][:],
                              g["inverse"][par][:].unsqueeze(2).broadcast_to(oshape), ALU.mult)\
               .then_inc(g["done"], 1)
            eng.wait_ge(g["done"], i + 1)

        @block.vector
        def _(dve):
            for t in (*xs, *outT):
                dve.memset(t[C:K1], 1.0).then_inc(ones_set, 1)
            dve.wait_ge(loaded, 96)
            dve.tensor_tensor(bias[:], bias[:], colmask[:], ALU.add).then_inc(ready, 1)
            dve.wait_ge(ready, 1)
            dve.tensor_tensor(last_bias[:], bias[:], rowmask[:], ALU.add).then_inc(ready, 1)
            dve.tensor_scalar(w_qkv[:, 0:C], w_qkv[:, 0:C], float(HEAD) ** -0.5, None, ALU.mult)\
               .then_inc(ready, 1)
            dve.wait_ge(ready, 3)
            own, other = groups

            def strip(i, par):
                scores(dve, own, i, par)
                shift(dve, own, i, par)
                invert(dve, own, i, par)
                values(dve, own, i, par)
                shift(dve, other, i, par)
                invert(dve, other, i, par)

            pipeline(dve, [(0, strip)], STRIPS, tail=2)

        @block.gpsimd
        def _(pool):
            pool.wait_ge(ready, 3)
            own = groups[1]
            pipeline(pool, [(0, lambda i, par: scores(pool, own, i, par)),
                            (1, lambda i, par: values(pool, own, i, par))], STRIPS, tail=2)


def time_mixing(nc, hidden, ident, bank, d):
    with ExitStack() as ctx:
        sb = lambda n, s: ctx.enter_context(nc.sbuf_tensor(f"tm_{n}", s, F32))
        sem = lambda n: ctx.enter_context(nc.semaphore(f"tm_{n}"))
        norm = Norm(nc, ctx, hidden, "n1")
        weights = {n: [sb(f"{n}_{which}", [PW, PW]) for which in ("now", "before")] for n in "kvr"}
        mix = sb("mix", [PW, 3])
        w_o = sb("w_o", [PW, PW])
        toeplitz = sb("toeplitz", [TB, BAND + 1, TB])
        triangle, ones = sb("triangle", [TB, TB]), sb("ones", [TB, TB])
        xT = [sb(f"xT{p}", [PW, PAIRS, 1 + TB]) for p in range(2)]
        clipped = sb("clipped", [TB, 2, BC])
        k = [sb(f"k{p}", [TB, BC]) for p in range(2)]
        neg_r_exp = sb("neg_r_exp", [TB, 2, BC])
        den, inverse = sb("den", [TB, BC]), sb("inverse", [TB, BC])
        y = [sb(f"y{p}", [TB, BC]) for p in range(2)]
        yT = [sb(f"yT{p}", [PW, PAIRS, TB]) for p in range(2)]
        kv = sb("kv", [TB, (BAND + NBLK) * BC])
        k_before = [sb(f"k_before{p}", [TB, BC]) for p in range(2)]
        kv_far = [sb(f"kv_far{p}", [TB, BC]) for p in range(2)]
        p_x, p_k, p_v, p_r, p_sum, p_wkv, p_y, p_o = bank
        (loaded, zeroed, mixed, turned, turned_copied, k_mm, v_mm, r_mm, clip_done, k_ready, r_ready, kv_ready,
         before_ready, far_ready, wkv_mm, den_ready, inverse_ready, y_ready, y_turned, y_copied, o_mm, added) = (
            sem(n) for n in (
                "loaded", "zeroed", "mixed", "turned", "turned_copied", "k_mm", "v_mm", "r_mm", "clip_done",
                "k_ready", "r_ready", "kv_ready", "before_ready", "far_ready", "wkv_mm", "den_ready",
                "inverse_ready", "y_ready", "y_turned", "y_copied", "o_mm", "added"))
        kv_block = lambda slot: block_cols(kv, slot)
        block = ctx.enter_context(nc.Block())

        @block.sync
        def _(sp):
            sp.wait_ge(zeroed, 8)
            for b in range(2):
                half = slice(b * C, b * C + C)
                for n in "kvr":
                    for t in weights[n]:
                        sp.dma_start(t[half, half], d[f"w_{n}"]).then_inc(loaded, 16)
                sp.dma_start(w_o[half, half], d["w_o"]).then_inc(loaded, 16)
                sp.dma_start(mix[half], d["mix"]).then_inc(loaded, 16)
            sp.dma_start(toeplitz[:], d["toeplitz"]).then_inc(loaded, 16)
            sp.dma_start(triangle[:], d["triangle"]).then_inc(loaded, 16)

        @block.tensor
        def _(pe):
            pe.wait_ge(loaded, 18 * 16)
            pe.wait_ge(mixed, 7)
            pe.wait_ge(zeroed, 17)

            def turn(i, par):
                pe.wait_ge(norm.xn_ready, i + 1)
                wait_former(pe, turned_copied, i, ago=1)
                for p in range(PAIRS):
                    tr = pe.transpose(p_x[:, p * TB:(p + 1) * TB], norm.xn[:, par, p * PW:(p + 1) * PW],
                                      ident[0:TB, 0:TB])
                tr.then_inc(turned, 1)

            def older(i, par):
                pe.wait_ge(far_ready, i + 1)
                wait_former(pe, y_ready, i, ago=1)
                pe.matmul(p_wkv[0:TB, :], toeplitz[:, BAND], kv_far[par][:], start=True, stop=False)
                wait_former(pe, kv_ready, i, ago=1)
                for j in range(BAND - 1, 0, -1):
                    pe.matmul(p_wkv[0:TB, :], toeplitz[:, j], kv_block(i + (BAND - j)), start=False, stop=False)

            def project(i, par):
                pe.wait_ge(turned_copied, i + 1)
                for n, into, read, made in (("k", p_k, clip_done, k_mm), ("v", p_v, kv_ready, v_mm),
                                            ("r", p_r, r_ready, r_mm)):
                    wait_former(pe, read, i, ago=1)
                    for p in range(PAIRS):
                        dst = into[0:TB, p * PW:(p + 1) * PW]
                        pe.matmul(dst, xT[par][:, p, 1:1 + TB], weights[n][0][:], start=True, stop=False)
                        mm = pe.matmul(dst, xT[par][:, p, 0:TB], weights[n][1][:], start=False, stop=True)
                    mm.then_inc(made, 1)

            def newest(i, par):
                pe.wait_ge(before_ready, i + 1)
                pe.matmul(p_sum[0:TB, :], ones[:], k_before[par][:], start=True, stop=False)
                pe.wait_ge(k_ready, i + 1)
                pe.matmul(p_sum[0:TB, :], triangle[:], k[par][:], start=False, stop=True)
                pe.wait_ge(kv_ready, i + 1)
                pe.matmul(p_wkv[0:TB, :], toeplitz[:, 0], kv_block(i + BAND), start=False, stop=True)\
                  .then_inc(wkv_mm, 1)

            def turn_y(i, par):
                pe.wait_ge(y_ready, i + 1)
                wait_former(pe, y_copied, i, ago=1)
                for p in range(PAIRS):
                    tr = pe.transpose(p_y[:, p * TB:(p + 1) * TB], y[par][:, p * PW:(p + 1) * PW], ident[0:TB, 0:TB])
                tr.then_inc(y_turned, 1)

            def output(i, par):
                pe.wait_ge(y_copied, i + 1)
                wait_former(pe, added, i, ago=1)
                for p in range(PAIRS):
                    mm = pe.matmul(p_o[0:TB, p * PW:(p + 1) * PW], yT[par][:, p], w_o[:], start=True, stop=True)
                mm.then_inc(o_mm, 1)

            pipeline(pe, [(1, turn), (1, older), (1, project), (2, turn_y), (1, newest), (2, output)], NBLK)

        @block.scalar
        def _(act):
            def copy_turned(i, par):
                act.wait_ge(turned, i + 1)
                wait_former(act, r_mm, i, ago=1)
                src = p_x[:, 0:HALF_TOK].rearrange("p (g t) -> p g t", g=PAIRS)
                act.activation(xT[par][:, :, 1:1 + TB], src, ACT.Copy)
                act.activation(xT[1 - par][:, :, 0:1], src[:, :, TB - 1:TB], ACT.Copy).then_inc(turned_copied, 1)

            def exp_k(i, par):
                act.wait_ge(clip_done, i + 1)
                wait_former(act, wkv_mm, i)
                wait_former(act, kv_ready, i)
                wait_count(act, before_ready, i, 1, 0)
                act.activation(k[par][:], clipped[:, par], ACT.Exp).then_inc(k_ready, 1)

            def exp_r(i, par):
                act.wait_ge(r_mm, i + 1)
                wait_former(act, y_ready, i)
                act.activation(neg_r_exp[:, par], p_r[0:TB, :], ACT.Exp, scale=-1.0).then_inc(r_ready, 1)

            def copy_y(i, par):
                act.wait_ge(y_turned, i + 1)
                wait_former(act, o_mm, i)
                act.activation(yT[par][:].rearrange("p g t -> p (g t)"), p_y[:, 0:HALF_TOK], ACT.Copy)\
                   .then_inc(y_copied, 1)

            act.wait_ge(zeroed, 17)
            pipeline(act, [(1, copy_turned), (0, norm.bind_scalar(act)), (1, exp_k), (1, exp_r), (2, copy_y)], NBLK)

        @block.vector
        def _(dve):
            for t in (*(t for n in "kvr" for t in weights[n]), w_o):
                dve.memset(t[:], 0.0).then_inc(zeroed, 1)
            dve.memset(ones[:], 1.0).then_inc(zeroed, 1)
            dve.memset(xT[0][:, :, 0:1], 0.0).then_inc(zeroed, 1)
            dve.memset(kv[:, 0:BAND * BC], 0.0).then_inc(zeroed, 1)
            for t in (*k_before, *kv_far):
                dve.memset(t[:], 0.0).then_inc(zeroed, 1)
            dve.memset(y[0][:], 0.0).then_inc(zeroed, 1)
            dve.memset(y[1][:], 0.0).then_inc(zeroed, 1)
            dve.memset(den[:], 0.0).then_inc(zeroed, 1)
            dve.wait_ge(loaded, 18 * 16)
            dve.wait_ge(zeroed, 17)
            for j, n in enumerate("kvr"):
                now, before = weights[n]
                dve.tensor_scalar(now[:], now[:], mix[:, j:j + 1], None, ALU.mult).then_inc(mixed, 1)
            dve.wait_ge(mixed, 3)
            dve.tensor_scalar(mix[:], mix[:], -1.0, 1.0, ALU.mult, ALU.add).then_inc(mixed, 1)
            dve.wait_ge(mixed, 4)
            for j, n in enumerate("kvr"):
                now, before = weights[n]
                dve.tensor_scalar(before[:], before[:], mix[:, j:j + 1], None, ALU.mult).then_inc(mixed, 1)

            def clip(i, par):
                dve.wait_ge(k_mm, i + 1)
                wait_former(dve, k_ready, i)
                dve.tensor_scalar(clipped[:, par], p_k[0:TB, :], 30.0, -60.0, ALU.min, ALU.max)\
                   .then_inc(clip_done, 1)

            def multiply_kv(i, par):
                dve.wait_ge(v_mm, i + 1)
                dve.wait_ge(k_ready, i + 1)
                dve.tensor_tensor(kv_block(i + BAND), p_v[0:TB, :], k[par][:], ALU.mult).then_inc(kv_ready, 1)

            def combine(i, par):
                dve.wait_ge(wkv_mm, i + 1)
                dve.wait_ge(r_ready, i + 1)
                dve.scalar_tensor_tensor(den[:], neg_r_exp[:, par], 1.0, p_sum[0:TB, :], ALU.add, ALU.mult)\
                   .then_inc(den_ready, 1)
                dve.wait_ge(den_ready, i + 1)
                wait_former(dve, y_ready, i, ago=1)
                dve.reciprocal(inverse[:], den[:]).then_inc(inverse_ready, 1)
                dve.wait_ge(inverse_ready, i + 1)
                wait_former(dve, y_turned, i)
                dve.tensor_tensor(y[par][:], p_wkv[0:TB, :], inverse[:], ALU.mult).then_inc(y_ready, 1)

            def add(i, par):
                dve.wait_ge(o_mm, i + 1)
                h = block_cols(hidden, i)
                dve.tensor_tensor(h, h, p_o[0:TB, :], ALU.add).then_inc(added, 1)

            pipeline(dve, [(0, norm.bind_centre(dve)), (0, norm.bind_sum(dve)), (1, clip), (1, multiply_kv),
                           (1, combine), (2, add)], NBLK)

        @block.gpsimd
        def _(pool):
            norm.gpsimd_setup(pool)
            pool.wait_ge(zeroed, 17)

            def far(i, par):
                wait_former(pool, k_mm, i)
                wait_former(pool, far_ready, i, ago=1)
                pool.tensor_tensor(kv_far[par][:], kv_far[1 - par][:], kv_block(i), ALU.add).then_inc(far_ready, 1)

            def before(i, par):
                if isinstance(i, int) and i == 0:
                    pool.sem_inc(before_ready, 1)
                pool.wait_ge(k_ready, i + 1)
                wait_former(pool, wkv_mm, i, ago=1)
                pool.wait_ge(before_ready, i + 1)
                pool.tensor_tensor(k_before[1 - par][:], k_before[par][:], k[par][:], ALU.add)\
                    .then_inc(before_ready, 1)

            pipeline(pool, [(0, norm.bind_gpsimd(pool, turned)), (0, far), (1, before)], NBLK)


def first_of_maxima(dve, like, order, key, last, hot, then):
    shape = [TB, B, EXPERTS]
    then(dve.scalar_tensor_tensor(by_batch(key), by_batch(like), 0.0, by_batch(order), ALU.is_equal, ALU.mult))
    then(dve.tensor_reduce(last, by_batch(key), X, ALU.max))
    then(dve.tensor_tensor(by_batch(hot), by_batch(key), last.unsqueeze(2).broadcast_to(shape), ALU.is_equal))


def expert_choice(nc, hidden, ident, bank, d):
    KH = HID // 128
    with ExitStack() as ctx:
        sb = lambda n, s: ctx.enter_context(nc.sbuf_tensor(f"ec_{n}", s, F32))
        sem = lambda n: ctx.enter_context(nc.semaphore(f"ec_{n}"))
        norm = Norm(nc, ctx, hidden, "n2")
        w1 = [sb(f"w1_{which}", [PW, HID]) for which in ("even", "odd")]
        b1 = sb("b1", [128, KH])
        w_gate = sb("w_gate", [128, KH, TB])
        gate_bias, order = sb("gate_bias", [TB, B * EXPERTS]), sb("order", [TB, B * EXPERTS])
        w_down = sb("w_down", [128, KH, EXPERTS * C])
        b_down = sb("b_down", [128, BC])
        xT = [sb(f"xT2{p}", [PW, HALF_TOK]) for p in range(2)]
        hT = [sb(f"hT{p}", [128, KH, 2, HALF_TOK]) for p in range(2)]
        logits, shifted = sb("logits", [TB, B * EXPERTS]), sb("shifted", [TB, B * EXPERTS])
        exps, key, hot = (sb(n, [TB, B * EXPERTS]) for n in ("exps", "key", "hot"))
        top, total, inverse, last = (sb(n, [TB, B]) for n in ("top2", "total2", "inverse2", "last"))
        gates = [sb(f"gates{p}", [TB, B * EXPERTS]) for p in range(2)]
        gatesT = [sb(f"gatesT{p}", [128, TB]) for p in range(2)]
        weighted = [sb(f"weighted{p}", [TB, EXPERTS, C]) for p in range(2)]
        chosen = sb("chosen", [TB, BC])
        p_x, p_gate, p_gT, p_bias = bank[0:4]
        p_h, p_e = bank[4:6], bank[6:8]
        (loaded, zeroed, turned, turned_copied, h_mm, h_ready, gate_mm, chain, shift_done, exp_done, gates_ready,
         gates_turned, gates_copied, expert_mm, weighted_ready, chosen_ready, bias_mm, added) = (sem(n) for n in (
            "loaded", "zeroed", "turned", "turned_copied", "h_mm", "h_ready", "gate_mm", "chain", "shift_done",
            "exp_done", "gates_ready", "gates_turned", "gates_copied", "expert_mm", "weighted_ready",
            "chosen_ready", "bias_mm", "added"))
        block = ctx.enter_context(nc.Block())

        def tokens_of(par, m, b):
            return hT[par][:, m, b % 2, b // 2 * TB:(b // 2 + 1) * TB]

        @block.sync
        def _(sp):
            for t, n in ((w1[0], "ffn_w1_even"), (w1[1], "ffn_w1_odd"), (b1, "ffn_b1"), (w_gate, "ffn_w_gate"),
                         (w_down, "ffn_w_down"), (b_down, "ffn_b_down")):
                sp.dma_start(t[:], d[n]).then_inc(loaded, 16)
            sp.dma_start(gate_bias[:], d["ffn_gate_bias"].partition_broadcast(TB)).then_inc(loaded, 16)
            sp.dma_start(order[:], d["order"].partition_broadcast(TB)).then_inc(loaded, 16)

        @block.tensor
        def _(pe):
            pe.wait_ge(loaded, 8 * 16)
            pe.wait_ge(zeroed, 2)

            def turn(i, par):
                pe.wait_ge(norm.xn_ready, i + 1)
                wait_former(pe, turned_copied, i, ago=1)
                for p in range(PAIRS):
                    tr = pe.transpose(p_x[:, p * TB:(p + 1) * TB], norm.xn[:, par, p * PW:(p + 1) * PW],
                                      ident[0:TB, 0:TB])
                tr.then_inc(turned, 1)

            def hid(i, par):
                pe.wait_ge(turned_copied, i + 1)
                for n in range(2 * KH):
                    m, side = n // 2, n % 2
                    wait_count(pe, h_ready, i, 2 * KH, n - 1)
                    pe.matmul(p_h[n % 2][:, 0:HALF_TOK], w1[side][:, m * 128:(m + 1) * 128], xT[par][:],
                              start=True, stop=True).then_inc(h_mm, 1)

            def turn_gates(i, par):
                pe.wait_ge(gates_ready, i + 1)
                wait_former(pe, gates_copied, i, ago=1)
                pe.matmul(p_gT[0:B * EXPERTS, 0:TB], gates[par][:], ident[0:TB, 0:TB], start=True, stop=True)\
                  .then_inc(gates_turned, 1)

            def experts(i, par):
                for b in range(B):
                    wait_count(pe, weighted_ready, i, B, b - 1)
                    for m in range(KH):
                        mm = pe.matmul(p_e[b % 2][0:TB, :], tokens_of(par, m, b), w_down[:, m],
                                       start=(m == 0), stop=(m == KH - 1))
                    mm.then_inc(expert_mm, 1)
                pe.wait_ge(gates_copied, i + 1)
                wait_former(pe, added, i, 2, ago=1)
                pe.matmul(p_bias[0:TB, :], gatesT[par][:], b_down[:], start=True, stop=True).then_inc(bias_mm, 1)

            def gate(i, par):
                pe.wait_ge(h_ready, i * 2 * KH + 2 * KH)
                wait_former(pe, shift_done, i, ago=1)
                for b in range(B):
                    for m in range(KH):
                        mm = pe.matmul(p_gate[0:TB, b * EXPERTS:b * EXPERTS + TB], tokens_of(par, m, b),
                                       w_gate[:, m], start=(m == 0), stop=(m == KH - 1))
                mm.then_inc(gate_mm, 1)

            pipeline(pe, [(1, turn), (1, hid), (2, turn_gates), (2, experts), (1, gate)], NBLK)

        @block.scalar
        def _(act):
            def copy_turned(i, par):
                act.wait_ge(turned, i + 1)
                wait_former(act, h_mm, i, 2 * KH)
                act.activation(xT[par][:], p_x[:, 0:HALF_TOK], ACT.Copy).then_inc(turned_copied, 1)

            def gelu(i, par):
                wait_former(act, expert_mm, i, B)
                for n in range(2 * KH):
                    act.wait_ge(h_mm, i * 2 * KH + (n + 1))
                    act.activation(hT[par][:, n // 2, n % 2], p_h[n % 2][:, 0:HALF_TOK], ACT.Gelu,
                                   bias=b1[:, n // 2:n // 2 + 1]).then_inc(h_ready, 1)

            def exp(i, par):
                act.wait_ge(shift_done, i + 1)
                wait_former(act, gates_ready, i, ago=1)
                act.activation(exps[:], shifted[:], ACT.Exp).then_inc(exp_done, 1)

            def copy_gates(i, par):
                act.wait_ge(gates_turned, i + 1)
                wait_former(act, bias_mm, i)
                act.activation(gatesT[par][0:B * EXPERTS], p_gT[0:B * EXPERTS, 0:TB], ACT.Copy)\
                   .then_inc(gates_copied, 1)

            act.wait_ge(loaded, 8 * 16)
            pipeline(act, [(2, exp), (1, copy_turned), (0, norm.bind_scalar(act)), (1, gelu), (2, copy_gates)], NBLK)

        @block.vector
        def _(dve):
            for t in gatesT:
                dve.memset(t[:], 0.0).then_inc(zeroed, 1)
            dve.wait_ge(loaded, 8 * 16)
            dve.wait_ge(zeroed, 2)

            def gating(i, par):
                shape, steps, made = [TB, B, EXPERTS], 7, [0]

                def then(ins):
                    made[0] += 1
                    ins.then_inc(chain, 1)
                    dve.wait_ge(chain, i * steps + made[0])

                dve.wait_ge(gate_mm, i + 1)
                then(dve.tensor_tensor(logits[:], p_gate[0:TB, 0:B * EXPERTS], gate_bias[:], ALU.add))
                then(dve.tensor_reduce(top[:], by_batch(logits[:]), X, ALU.max))
                dve.tensor_tensor(by_batch(shifted[:]), by_batch(logits[:]),
                                  top[:].unsqueeze(2).broadcast_to(shape), ALU.subtract).then_inc(shift_done, 1)
                dve.wait_ge(shift_done, i + 1)
                first_of_maxima(dve, shifted[:], order[:], key[:], last[:], hot[:], then)
                dve.wait_ge(exp_done, i + 1)
                then(dve.tensor_reduce(total[:], by_batch(exps[:]), X, ALU.add))
                then(dve.reciprocal(inverse[:], total[:]))
                wait_former(dve, gates_turned, i)
                dve.tensor_tensor(by_batch(gates[par][:]), by_batch(hot[:]),
                                  inverse[:].unsqueeze(2).broadcast_to(shape), ALU.mult).then_inc(gates_ready, 1)
                dve.wait_ge(gates_ready, i + 1)

            def weigh(i, par):
                def sum_experts(b):
                    dve.wait_ge(weighted_ready, i * B + (b + 1))
                    dve.tensor_reduce(chosen[:, b * C:(b + 1) * C], weighted[b % 2][:].rearrange("p e c -> p c e"),
                                      X, ALU.add).then_inc(chosen_ready, 1)

                wait_former(dve, added, i, 2, ago=1)
                for b in range(B):
                    dve.wait_ge(expert_mm, i * B + (b + 1))
                    wait_count(dve, chosen_ready, i, B, b - 1)
                    dve.tensor_tensor(weighted[b % 2][:], p_e[b % 2][0:TB, :].rearrange("p (e c) -> p e c", e=EXPERTS),
                                      gates[par][:, b * EXPERTS:(b + 1) * EXPERTS].unsqueeze(2)
                                      .broadcast_to([TB, EXPERTS, C]), ALU.mult).then_inc(weighted_ready, 1)
                    if b:
                        sum_experts(b - 1)
                sum_experts(B - 1)

            def add(i, par):
                h = block_cols(hidden, i)
                dve.wait_ge(bias_mm, i + 1)
                dve.tensor_tensor(h, h, p_bias[0:TB, :], ALU.add).then_inc(added, 1)
                dve.wait_ge(chosen_ready, i * B + B)
                dve.wait_ge(added, i * 2 + 1)
                dve.tensor_tensor(h, h, chosen[:], ALU.add).then_inc(added, 1)

            pipeline(dve, [(0, norm.bind_centre(dve)), (2, gating), (0, norm.bind_sum(dve)), (2, weigh), (2, add)],
                     NBLK)

        @block.gpsimd
        def _(pool):
            norm.gpsimd_setup(pool)
            pipeline(pool, [(0, norm.bind_gpsimd(pool, turned))], NBLK)


def rnn_inputs(nc, hidden, ident, bank, xt):
    with ExitStack() as ctx:
        sem = lambda n: ctx.enter_context(nc.semaphore(f"ri_{n}"))
        norm = Norm(nc, ctx, hidden, "n3")
        xT = [ctx.enter_context(nc.sbuf_tensor(f"xT3{p}", [C, TB, B], F32)) for p in range(2)]
        p_x = [bank[2 * p:2 * p + 2] for p in range(2)]
        turned, turned_copied = sem("turned"), sem("turned_copied")
        half_copied = sem("half_copied")
        stored = [sem(f"stored{p}") for p in range(2)]
        block = ctx.enter_context(nc.Block())

        @block.tensor
        def _(pe):
            def turn(i, par):
                pe.wait_ge(norm.xn_ready, i + 1)
                wait_former(pe, turned_copied, i)
                for b in range(B):
                    mm = pe.matmul(p_x[par][b // 4][0:C, b % 4 * TB:(b % 4 + 1) * TB],
                                   norm.xn[:, par, b * C:(b + 1) * C], ident[0:TB, 0:TB], start=True, stop=True)
                mm.then_inc(turned, 1)

            pipeline(pe, [(1, turn)], NBLK)

        @block.scalar
        def _(act):
            def copy_turned(i, par):
                act.wait_ge(turned, i + 1)
                wait_count(act, stored[par], i, 8, -8 * par)
                for half in range(2):
                    cp = act.activation(xT[par][:, :, 4 * half:4 * half + 4].rearrange("c t b -> c b t"),
                                        p_x[par][half][0:C, 0:HALF_TOK].rearrange("c (b t) -> c b t", b=4), ACT.Copy)
                    if half:
                        cp.then_inc(turned_copied, 1)
                    else:
                        cp.then_inc(half_copied, 1)

            pipeline(act, [(1, copy_turned), (0, norm.bind_scalar(act))], NBLK)

        @block.vector
        def _(dve):
            pipeline(dve, [(0, norm.bind_centre(dve)), (0, norm.bind_sum(dve))], NBLK)

        @block.gpsimd
        def _(pool):
            norm.gpsimd_setup(pool)
            pipeline(pool, [(0, norm.bind_gpsimd(pool, turned))], NBLK)

        @block.sync
        def _(sp):
            def store(i, par):
                sp.wait_ge(half_copied, i + 1)
                sp.wait_ge(turned_copied, i + 1)
                sp.dma_start(block_cols(xt, i, TB * B), xT[par][:].rearrange("c t b -> c (t b)"))\
                  .then_inc(stored[par], 16)

            pipeline(sp, [(0, store)], NBLK)
            for s in stored:
                sp.wait_ge(s, NBLK // 2 * 16)


def recurrence(nc, bank, d, xt, rnn_out):
    J, QUADS = HID // 128, 128 // QUAD
    QW = HID // QUADS
    CHUNKS = STEP_LOOP // XCHUNK
    LOOPS = TOKENS // STEP_LOOP
    KX = C + 2
    OUT_AT = {18: 0, 34: 1, 50: 2, STEP_LOOP - 1: 3}
    with ExitStack() as ctx:
        sb = lambda n, s: ctx.enter_context(nc.sbuf_tensor(f"rn_{n}", s, F32))
        sem = lambda n: ctx.enter_context(nc.semaphore(f"rn_{n}"))
        x = sb("rnn_x", [KX, STEP_LOOP, B])
        w_x = sb("w_x", [KX, QUADS, QW])
        w_hh = [sb(f"w_hh{l}", [128, J, QUADS, QW]) for l in range(2)]
        w_up = sb("w_up", [128, J, QUADS, QW])
        bias, bias2 = sb("rnn_bias", [128, J]), sb("rnn_bias2", [128, J])
        w_fc, fc_bias = sb("w_fc", [128, J, C]), sb("fc_bias", [128, C])
        h = [sb(f"h{l}", [128, J, STEP_LOOP, B]) for l in range(2)]
        pre = [sb(f"pre{l}", [128, 2, J * QUAD]) for l in range(2)]
        fc = sb("fc", [128, CHUNKS, C])
        p_h = [bank[0:2], bank[2:4]]
        p_fc = bank[4:6]
        loaded, zeroed, bias_ready = sem("loaded"), sem("zeroed"), sem("bias_ready")
        x_loaded = [sem(f"x_loaded{q}") for q in range(CHUNKS)]
        summed = [sem("summed0"), sem("summed1")]
        turned = [sem("turned0"), sem("turned1")]
        h_ready = [sem("h_ready0"), sem("h_ready1")]
        first_half = sem("first_half")
        fc_free, fc_mm = sem("fc_free"), sem("fc_mm")
        stored = [sem(f"stored{q}") for q in range(CHUNKS)]
        rows = rnn_out.rearrange("n t (b c) -> (n t b) c", b=B)
        block = ctx.enter_context(nc.Block())

        @block.sync
        def _(sp):
            for t, n in ((w_x, "rnn_w_x"), (w_hh[0], "rnn_w_hh0"), (w_hh[1], "rnn_w_hh1"), (w_up, "rnn_w_up"),
                         (w_fc, "rnn_w_fc")):
                flat = "p a b c -> p (a b c)" if len(t.shape) == 4 else "p a b -> p (a b)"
                sp.dma_start(t[:].rearrange(flat), d[n]).then_inc(loaded, 16)
            sp.dma_start(bias[:], d["rnn_b_ih1"]).then_inc(loaded, 16)
            sp.dma_start(bias2[:], d["rnn_b_hh1"]).then_inc(loaded, 16)
            sp.dma_start(fc_bias[:], d["rnn_fc_b"].partition_broadcast(128)).then_inc(loaded, 16)

            def load(chunk, q):
                sp.dma_start(x[0:C, q * XCHUNK:(q + 1) * XCHUNK, :].rearrange("c t b -> c (t b)"),
                             block_cols(xt, chunk, XCHUNK * B)).then_inc(x_loaded[q], 16)

            def store(loop, q):
                sp.wait_ge(fc_free, loop * CHUNKS + (q + 3))
                sp.dma_start(rows[bass.ds((loop * CHUNKS + q) * XCHUNK * B, XCHUNK * B)], fc[:, q])\
                  .then_inc(stored[q], 16)

            for q in range(CHUNKS):
                load(q, q)
            with sp.Fori(1, LOOPS) as m:
                loop = sp.snap(m)
                for q in range(CHUNKS):
                    sp.wait_ge(summed[0], loop * STEP_LOOP + (q + 1 - CHUNKS) * XCHUNK)
                    load(loop * CHUNKS + q, q)
                    store(loop - 1, q)
            sp.wait_ge(summed[0], TOKENS - (CHUNKS - 1) * XCHUNK)
            load(TOKENS // XCHUNK - 1, 0)
            for q in range(CHUNKS):
                store(LOOPS - 1, q)
            for q in range(CHUNKS):
                sp.wait_ge(stored[q], (LOOPS + 1) * 16)
                sp.wait_ge(x_loaded[q], (LOOPS + (q == 0)) * 16)

        @block.tensor
        def _(pe):
            pe.wait_ge(loaded, 8 * 16)
            pe.wait_ge(zeroed, 7)

            def tiles(dst, state, weights, start, stop):
                for j in range(J):
                    for q in range(QUADS):
                        mm = pe.matmul(dst[QUAD * q:QUAD * q + B, 0:QW], state(j), weights[:, j, q],
                                       start=start and j == 0, stop=stop and j == J - 1,
                                       skip_group_check=True, tile_position=(0, QUAD * q))
                return mm

            def layer0(n, s):
                dst = p_h[0][s % 2]
                for q in range(QUADS):
                    pe.matmul(dst[QUAD * q:QUAD * q + B, 0:QW], x[:, s], w_x[:, q], start=True, stop=False,
                              skip_group_check=True, tile_position=(0, QUAD * q))
                pe.wait_ge(h_ready[0], n + 1)
                tiles(dst, lambda j: h[0][:, j, (s - 1) % STEP_LOOP], w_hh[0], False, True).then_inc(summed[0], 1)

            def layer1(n, s):
                dst = p_h[1][s % 2]
                tiles(dst, lambda j: h[0][:, j, s], w_up, True, False)
                pe.wait_ge(h_ready[1], n + 1)
                tiles(dst, lambda j: h[1][:, j, (s - 1) % STEP_LOOP], w_hh[1], False, True).then_inc(summed[1], 1)

            def outputs(loop, q):
                pe.wait_ge(h_ready[1], loop * STEP_LOOP + (q + 1) * XCHUNK + 1)
                pe.wait_ge(fc_free, loop * CHUNKS + (q + 1))
                for j in range(J):
                    mm = pe.matmul(p_fc[q % 2][:, 0:C],
                                   h[1][:, j, q * XCHUNK:(q + 1) * XCHUNK].rearrange("p t b -> p (t b)"),
                                   w_fc[:, j], start=(j == 0), stop=(j == J - 1))
                mm.then_inc(fc_mm, 1)

            pe.wait_ge(x_loaded[0], 16)
            layer0(0, 0)
            with pe.Fori(0, LOOPS) as m:
                loop = pe.snap(m)
                for s in range(STEP_LOOP):
                    nxt = s + 1
                    if nxt % XCHUNK == 0:
                        q = nxt // XCHUNK % CHUNKS
                        pe.wait_ge(x_loaded[q], loop * 16 + (16 if nxt < STEP_LOOP else 32))
                    layer0(loop * STEP_LOOP + nxt, nxt % STEP_LOOP)
                    layer1(loop * STEP_LOOP + s, s)
                    if s in OUT_AT:
                        outputs(loop, OUT_AT[s])

        @block.vector
        def _(dve):
            dve.memset(x[C:KX], 1.0).then_inc(zeroed, 1)
            for layer in range(2):
                dve.memset(h[layer][:], 0.0).then_inc(h_ready[layer], 1)
            for t in bank[0:4]:
                dve.memset(t[:], 0.0).then_inc(zeroed, 1)
            for q in range(CHUNKS):
                dve.sem_inc(stored[q], 16)
            for t in p_fc:
                dve.memset(t[:], 0.0).then_inc(fc_free, 1)
            dve.wait_ge(loaded, 8 * 16)
            dve.tensor_tensor(bias[:], bias[:], bias2[:], ALU.add).then_inc(zeroed, 1)
            dve.memset(fc[:], 0.0).then_inc(zeroed, 1)
            dve.wait_ge(zeroed, 7)

            def turn(layer, n, s):
                dve.wait_ge(summed[layer], n + 1)
                dve.transpose(pre[layer][:, s % 2], p_h[layer][s % 2][:, 0:QW]).then_inc(turned[layer], 1)

            def add_bias(loop, q):
                dve.wait_ge(fc_mm, loop * CHUNKS + (q + 1))
                dve.wait_ge(stored[q], (loop + 1) * 16)
                dve.tensor_tensor(fc[:, q], p_fc[q % 2][:, 0:C], fc_bias[:], ALU.add).then_inc(fc_free, 1)

            turn(0, 0, 0)
            with dve.Fori(0, LOOPS) as m:
                loop = dve.snap(m)
                for s in range(STEP_LOOP):
                    turn(0, loop * STEP_LOOP + (s + 1), s + 1)
                    turn(1, loop * STEP_LOOP + s, s)
                    if s in OUT_AT:
                        add_bias(loop, OUT_AT[s])

        @block.scalar
        def _(act):
            act.wait_ge(zeroed, 7)
            for layer in range(2):
                act.wait_ge(h_ready[layer], 1)

            def units(layer, s):
                return pre[layer][:, s % 2].rearrange("p (j b) -> p j b", j=J)[:, :, 0:B]

            def layer0(n, s):
                act.wait_ge(turned[0], n + 1)
                act.activation(h[0][:, :, s % STEP_LOOP], units(0, s), ACT.Tanh).then_inc(h_ready[0], 1)

            def layer1(n, s):
                act.wait_ge(turned[1], n + 1)
                for j in range(J):
                    act.activation(h[1][:, j, s], units(1, s)[:, j], ACT.Tanh, bias=bias[:, j:j + 1])\
                       .then_inc(h_ready[1] if j == J - 1 else first_half, 1)

            layer0(0, 0)
            with act.Fori(0, LOOPS) as m:
                loop = act.snap(m)
                for s in range(STEP_LOOP):
                    layer0(loop * STEP_LOOP + (s + 1), s + 1)
                    layer1(loop * STEP_LOOP + s, s)


def expert_pairs(nc, hidden, ident, bank, d, rnn_out, out):
    with ExitStack() as ctx:
        sb = lambda n, s: ctx.enter_context(nc.sbuf_tensor(f"ep_{n}", s, F32))
        sem = lambda n: ctx.enter_context(nc.semaphore(f"ep_{n}"))
        norm = Norm(nc, ctx, hidden, "n4")
        w1 = [sb(f"m_w1_{which}", [PW, EXPERTS, MHID]) for which in ("even", "odd")]
        b1 = sb("m_b1", [MHID, EXPERTS])
        w2 = sb("m_w2", [MHID, (EXPERTS + 1) * C])
        w_gate = sb("m_w_gate", [PW, PW])
        gate_bias, order = sb("m_gate_bias", [TB, B * EXPERTS]), sb("m_order", [TB, B * EXPERTS])
        b2 = sb("m_b2", [128, BC])
        rnn = [sb(f"rnn{p}", [TB, BC]) for p in range(2)]
        xT = [sb(f"xT4{p}", [PW, HALF_TOK]) for p in range(2)]
        hT = [sb(f"m_hT{p}", [MHID, 2, HALF_TOK]) for p in range(2)]
        logits, shifted, second = (sb(f"m_{n}", [TB, B * EXPERTS]) for n in ("logits", "shifted", "second"))
        exps, key, hot, hot2 = (sb(f"m_{n}", [TB, B * EXPERTS]) for n in ("exps", "key", "hot", "hot2"))
        top, total, inverse, last = (sb(f"m_{n}", [TB, B]) for n in ("top", "total", "inverse", "last"))
        gates = [sb(f"m_gates{p}", [TB, B * EXPERTS]) for p in range(2)]
        gatesT = [sb(f"m_gatesT{p}", [128, TB]) for p in range(2)]
        weighted = [sb(f"m_weighted{p}", [TB, BC]) for p in range(2)]
        acc = [sb(f"acc{p}", [TB, BC]) for p in range(2)]
        result = [sb(f"result{p}", [TB, BC]) for p in range(2)]
        p_x, p_gate, p_gT, p_bias = bank[0:4]
        p_h, p_y = bank[4:6], bank[6:8]
        (loaded, zeroed, rnn_added, turned, turned_copied, h_mm, h_ready, y_mm, gate_mm, chain, shift_done,
         exp_done, gates_ready, gates_turned, gates_copied, weighted_ready, acc_ready, bias_mm, partial,
         result_ready) = (sem(n) for n in (
             "loaded", "zeroed", "rnn_added", "turned", "turned_copied", "h_mm", "h_ready", "y_mm", "gate_mm",
             "chain", "shift_done", "exp_done", "gates_ready", "gates_turned", "gates_copied",
             "weighted_ready", "acc_ready", "bias_mm", "partial", "result_ready"))
        rnn_loaded, stored = ([sem(f"{n}{p}") for p in range(2)] for n in ("rnn_loaded", "stored"))
        block = ctx.enter_context(nc.Block())

        @block.sync
        def _(sp):
            for t, n in ((w1[0], "moe_w1_even"), (w1[1], "moe_w1_odd"), (b1, "moe_b1"), (w2, "moe_w2"),
                         (w_gate, "moe_w_gate"), (b2, "moe_b2")):
                sp.dma_start(t[:].rearrange("p a b -> p (a b)") if len(t.shape) == 3 else t[:], d[n])\
                  .then_inc(loaded, 16)
            sp.dma_start(gate_bias[:], d["moe_gate_bias"].partition_broadcast(TB)).then_inc(loaded, 16)
            sp.dma_start(order[:], d["order"].partition_broadcast(TB)).then_inc(loaded, 16)

            def load(i, par):
                wait_former(sp, rnn_added, i)
                sp.dma_start(rnn[par][:], rnn_out[bass.ds(i, 1)].rearrange("o t f -> (o t) f"))\
                  .then_inc(rnn_loaded[par], 16)

            def store(i, par):
                sp.wait_ge(result_ready, i + 1)
                sp.dma_start(out[bass.ds(i, 1)].rearrange("o t f -> (o t) f"), result[par][:])\
                  .then_inc(stored[par], 16)

            pipeline(sp, [(0, load), (2, store)], NBLK)
            for s in stored:
                sp.wait_ge(s, NBLK // 2 * 16)

        @block.tensor
        def _(pe):
            pe.wait_ge(loaded, 8 * 16)
            pe.wait_ge(zeroed, 2)

            def turn(i, par):
                pe.wait_ge(norm.xn_ready, i + 1)
                wait_former(pe, turned_copied, i, ago=1)
                for p in range(PAIRS):
                    tr = pe.transpose(p_x[:, p * TB:(p + 1) * TB], norm.xn[:, par, p * PW:(p + 1) * PW],
                                      ident[0:TB, 0:TB])
                tr.then_inc(turned, 1)

            def gate(i, par):
                pe.wait_ge(turned_copied, i + 1)
                wait_former(pe, shift_done, i, ago=1)
                for p in range(PAIRS):
                    mm = pe.matmul(p_gate[0:TB, 2 * p * EXPERTS:2 * p * EXPERTS + PW], xT[par][:, p * TB:(p + 1) * TB],
                                   w_gate[:], start=True, stop=True)
                mm.then_inc(gate_mm, 1)

            def up(i, par, e):
                for side in range(2):
                    wait_count(pe, h_ready, i, 2 * EXPERTS, 2 * e + side - 1)
                    pe.matmul(p_h[side][:, 0:HALF_TOK], w1[side][:, e], xT[par][:], start=True, stop=True)\
                      .then_inc(h_mm, 1)

            def down(i, par, e):
                pe.wait_ge(h_ready, i * 2 * EXPERTS + (2 * e + 2))
                wait_count(pe, weighted_ready, i, EXPERTS, e - 1)
                for b in range(B):
                    width = PW if b < B - 1 else C
                    mm = pe.matmul(p_y[e % 2][0:TB, b * C:b * C + width],
                                   hT[e % 2][:, b % 2, b // 2 * TB:(b // 2 + 1) * TB], w2[:, e * C:e * C + width],
                                   start=True, stop=True)
                mm.then_inc(y_mm, 1)

            def experts(i, par):
                for e in range(EXPERTS):
                    up(i, par, e)
                    if e:
                        down(i, par, e - 1)
                down(i, par, EXPERTS - 1)

            def bias(i, par):
                pe.wait_ge(gates_ready, i + 1)
                wait_former(pe, gates_copied, i, ago=1)
                pe.matmul(p_gT[0:B * EXPERTS, 0:TB], gates[par][:], ident[0:TB, 0:TB], start=True, stop=True)\
                  .then_inc(gates_turned, 1)
                pe.wait_ge(gates_copied, i + 1)
                wait_former(pe, partial, i, ago=1)
                pe.matmul(p_bias[0:TB, :], gatesT[par][:], b2[:], start=True, stop=True).then_inc(bias_mm, 1)

            pipeline(pe, [(1, turn), (2, bias), (1, gate), (1, experts)], NBLK)

        @block.scalar
        def _(act):
            def copy_turned(i, par):
                act.wait_ge(turned, i + 1)
                wait_former(act, h_mm, i, 2 * EXPERTS)
                act.activation(xT[par][:], p_x[:, 0:HALF_TOK], ACT.Copy).then_inc(turned_copied, 1)

            def gelu(i, par):
                for e in range(EXPERTS):
                    wait_count(act, y_mm, i, EXPERTS, e - 1)
                    for side in range(2):
                        act.wait_ge(h_mm, i * 2 * EXPERTS + (2 * e + side + 1))
                        act.activation(hT[e % 2][:, side], p_h[side][:, 0:HALF_TOK], ACT.Gelu, bias=b1[:, e:e + 1])\
                           .then_inc(h_ready, 1)

            def exp(i, par):
                act.wait_ge(shift_done, i + 1)
                wait_former(act, gates_ready, i, ago=1)
                act.activation(exps[:], shifted[:], ACT.Exp).then_inc(exp_done, 1)

            def copy_gates(i, par):
                act.wait_ge(gates_turned, i + 1)
                wait_former(act, bias_mm, i)
                act.activation(gatesT[par][0:B * EXPERTS], p_gT[0:B * EXPERTS, 0:TB], ACT.Copy)\
                   .then_inc(gates_copied, 1)

            act.wait_ge(loaded, 8 * 16)
            pipeline(act, [(1, copy_turned), (2, copy_gates), (1, exp), (0, norm.bind_scalar(act)), (1, gelu)], NBLK)

        @block.vector
        def _(dve):
            for t in gatesT:
                dve.memset(t[:], 0.0).then_inc(zeroed, 1)
            dve.wait_ge(loaded, 8 * 16)
            dve.wait_ge(zeroed, 2)

            def add_rnn(i, par):
                h = block_cols(hidden, i)
                wait_load(dve, rnn_loaded, i, par)
                dve.tensor_tensor(h, h, rnn[par][:], ALU.add).then_inc(rnn_added, 1)
                wait_former(dve, norm.xn_ready, i)
                dve.wait_ge(rnn_added, i + 1)
                dve.memset(norm.rstd[:, par], 0.0)

            def gating(i, par):
                shape, steps, made = [TB, B, EXPERTS], 15, [0]

                def then(ins):
                    made[0] += 1
                    ins.then_inc(chain, 1)
                    dve.wait_ge(chain, i * steps + made[0])

                spread = lambda t: t.unsqueeze(2).broadcast_to(shape)
                dve.wait_ge(gate_mm, i + 1)
                then(dve.tensor_tensor(logits[:], p_gate[0:TB, 0:B * EXPERTS], gate_bias[:], ALU.add))
                then(dve.tensor_reduce(top[:], by_batch(logits[:]), X, ALU.max))
                dve.tensor_tensor(by_batch(shifted[:]), by_batch(logits[:]), spread(top[:]), ALU.subtract)\
                   .then_inc(shift_done, 1)
                dve.wait_ge(shift_done, i + 1)
                first_of_maxima(dve, shifted[:], order[:], key[:], last[:], hot[:], then)
                then(dve.scalar_tensor_tensor(second[:], hot[:], NEG, shifted[:], ALU.mult, ALU.add))
                then(dve.tensor_reduce(top[:], by_batch(second[:]), X, ALU.max))
                then(dve.tensor_tensor(by_batch(second[:]), by_batch(second[:]), spread(top[:]), ALU.subtract))
                first_of_maxima(dve, second[:], order[:], key[:], last[:], hot2[:], then)
                then(dve.tensor_tensor(hot[:], hot[:], hot2[:], ALU.add))
                dve.wait_ge(exp_done, i + 1)
                then(dve.tensor_reduce(total[:], by_batch(exps[:]), X, ALU.add))
                then(dve.reciprocal(inverse[:], total[:]))
                then(dve.tensor_tensor(by_batch(hot[:]), by_batch(hot[:]), spread(inverse[:]), ALU.mult))
                wait_former(dve, gates_turned, i)
                dve.tensor_tensor(gates[par][:], hot[:], exps[:], ALU.mult).then_inc(gates_ready, 1)
                dve.wait_ge(gates_ready, i + 1)

            def weigh(i, par):
                for e in range(EXPERTS):
                    dve.wait_ge(y_mm, i * EXPERTS + (e + 1))
                    wait_count(dve, acc_ready, i, EXPERTS - 1, max(e - 1, 0))
                    dve.tensor_tensor(by_batch(weighted[e % 2][:]), by_batch(p_y[e % 2][0:TB, :]),
                                      gates[par][:, e::EXPERTS].unsqueeze(2).broadcast_to([TB, B, C]), ALU.mult)\
                       .then_inc(weighted_ready, 1)

            def finish(i, par):
                dve.wait_ge(bias_mm, i + 1)
                wait_count(dve, stored[par], i, 8, -8 * par)
                dve.tensor_tensor(result[par][:], block_cols(hidden, i), p_bias[0:TB, :], ALU.add)\
                   .then_inc(partial, 1)
                dve.wait_ge(partial, i + 1)
                dve.wait_ge(acc_ready, (i + 1) * (EXPERTS - 1))
                dve.tensor_tensor(result[par][:], result[par][:], acc[par][:], ALU.add).then_inc(result_ready, 1)

            pipeline(dve, [(1, gating), (0, add_rnn), (0, norm.bind_centre(dve)), (0, norm.bind_sum(dve)),
                           (1, weigh), (2, finish)], NBLK)

        @block.gpsimd
        def _(pool):
            norm.gpsimd_setup(pool)

            def accumulate(i, par):
                wait_former(pool, result_ready, i)
                for e in range(1, EXPERTS):
                    pool.wait_ge(weighted_ready, i * EXPERTS + (e + 1))
                    if e > 1:
                        pool.wait_ge(acc_ready, i * (EXPERTS - 1) + (e - 1))
                    pool.tensor_tensor(acc[par][:], acc[par][:] if e > 1 else weighted[0][:], weighted[e % 2][:],
                                       ALU.add).then_inc(acc_ready, 1)

            pipeline(pool, [(0, norm.bind_gpsimd(pool, turned)), (1, accumulate)], NBLK)


def build(nc, d, out):
    with ExitStack() as ctx:
        hidden = ctx.enter_context(nc.sbuf_tensor("hidden", [TB, NBLK * BC], F32))
        ident = ctx.enter_context(nc.sbuf_tensor("identity", [128, 128], F32))
        bank = [ctx.enter_context(nc.psum_tensor(f"bank{k}", [128, 512], F32)) for k in range(8)]
        xt = nc.dram_tensor("normed_turned", (C, TOKENS * B), F32, kind="Internal").ap()
        rnn_out = nc.dram_tensor("rnn_out", (NBLK, TB, BC), F32, kind="Internal").ap()
        window_attention(nc, hidden, ident, bank, d)
        time_mixing(nc, hidden, ident, bank, d)
        expert_choice(nc, hidden, ident, bank, d)
        rnn_inputs(nc, hidden, ident, bank, xt)
        recurrence(nc, bank, d, xt, rnn_out)
        expert_pairs(nc, hidden, ident, bank, d, rnn_out, out)


def by_batch_diagonal(m):
    o = np.zeros((128, BC), np.float32)
    for b in range(B):
        o[b * EXPERTS:(b + 1) * EXPERTS, b * C:(b + 1) * C] = m
    return o


def lay_out(a):
    o = {"ident": np.eye(128, dtype=np.float32)}
    x = np.roll(a["x"], (-(WS // 2), -(WS // 2)), axis=(2, 3)).reshape(B, C, STRIPS, WS, WCOLS, WS)
    o["x"] = x.transpose(2, 1, 3, 5, 0, 4).reshape(STRIPS, C, WTOK * WINDOWS)
    o["w_qkv"] = np.concatenate([a["L0_tok_w1"], a["L0_tok_b1"][:, None]], 1)\
        .reshape(HEAD, NH, 3, C + 1).transpose(3, 2, 0, 1).reshape(C + 1, 3 * C)
    w2 = a["L0_tok_w2"].reshape(C, NH, HEAD).transpose(2, 1, 0).reshape(C, C)
    o["w_out"] = np.concatenate([w2, a["L0_tok_b2"][None]], 0)
    at = np.array([[i, j] for i in range(WS) for j in range(WS)])
    rel = at[None] - at[:, None] + WS - 1
    o["pos_bias"] = a["L0_tok_pos_emb"][rel[..., 0], rel[..., 1]].reshape(-1)
    low, right = at[:, 0] >= WS // 2, at[:, 1] >= WS // 2
    mask = lambda side: np.where(side[:, None] != side[None], np.float32(NEG), np.float32(0)).reshape(-1)
    o["rowmask"] = mask(low)
    o["colmask"] = np.zeros((B, WCOLS, WTOK * WTOK), np.float32)
    o["colmask"][:, -1] = mask(right)
    o["colmask"] = o["colmask"].reshape(WINDOWS, -1)
    for n in "kvr":
        o[f"w_{n}"] = a[f"L0_attn_W{n}"]
    o["w_o"] = a["L0_attn_Wo"]
    o["mix"] = np.stack([a[f"L0_attn_time_mix_{n}"].reshape(C) for n in "kvr"], 1)
    u, j, t = np.ogrid[0:TB, 0:BAND + 1, 0:TB]
    distance = j * TB + t - u
    distance[:, BAND] = MAXLEN
    o["toeplitz"] = np.where(distance < 0, np.float32(0), a["L0_attn_time_w"][np.clip(MAXLEN - 1 - distance, 0, MAXLEN - 1)])
    o["triangle"] = np.triu(np.ones((TB, TB), np.float32))
    zero = lambda *s: np.zeros(s, np.float32)
    w1 = a["L0_ffn_W1"]
    o["ffn_w1_even"] = np.concatenate([w1, zero(C, HID)])
    o["ffn_w1_odd"] = np.concatenate([zero(C, HID), w1])
    o["ffn_b1"] = a["L0_ffn_b1"].reshape(HID // 128, 128).T
    wg = a["L0_ffn_Wg"].reshape(HID // 128, 128, EXPERTS).transpose(1, 0, 2)
    o["ffn_w_gate"] = np.concatenate([wg, zero(128, HID // 128, TB - EXPERTS)], 2)
    o["ffn_gate_bias"] = np.tile(a["L0_ffn_bg"], B)
    o["order"] = np.tile(np.arange(EXPERTS, 0, -1, dtype=np.float32), B)
    o["ffn_w_down"] = a["L0_ffn_Wd"].reshape(EXPERTS, HID // 128, 128, C).transpose(2, 1, 0, 3)\
        .reshape(128, HID // 128, EXPERTS * C)
    o["ffn_b_down"] = by_batch_diagonal(a["L0_ffn_bd"])
    def unit_rows(m):
        return m.reshape(4, HID // 128, QUAD, -1).transpose(0, 2, 1, 3).reshape(128, -1)
    o["rnn_w_x"] = np.concatenate([a["L1_attn_W_ih_0"].T, a["L1_attn_b_ih_0"][None], a["L1_attn_b_hh_0"][None]])
    o["rnn_w_hh0"] = unit_rows(a["L1_attn_W_hh_0"].T)
    o["rnn_w_hh1"] = unit_rows(a["L1_attn_W_hh_1"].T)
    o["rnn_w_up"] = unit_rows(a["L1_attn_W_ih_1"].T)
    o["rnn_w_fc"] = unit_rows(a["L1_attn_fc_w"].T)
    o["rnn_b_ih1"], o["rnn_b_hh1"] = unit_rows(a["L1_attn_b_ih_1"][:, None]), unit_rows(a["L1_attn_b_hh_1"][:, None])
    o["rnn_fc_b"] = a["L1_attn_fc_b"]
    w1 = a["L1_ffn_W1"].transpose(1, 0, 2).reshape(C, EXPERTS * MHID)
    o["moe_w1_even"] = np.concatenate([w1, zero(C, EXPERTS * MHID)])
    o["moe_w1_odd"] = np.concatenate([zero(C, EXPERTS * MHID), w1])
    o["moe_b1"] = a["L1_ffn_b1"].T
    o["moe_w2"] = np.concatenate([a["L1_ffn_W2"].transpose(1, 0, 2).reshape(MHID, EXPERTS * C), zero(MHID, C)], 1)
    o["moe_w_gate"] = zero(PW, PW)
    for b in range(2):
        o["moe_w_gate"][b * C:(b + 1) * C, b * EXPERTS:(b + 1) * EXPERTS] = a["L1_ffn_gate_w"]
    o["moe_gate_bias"] = np.tile(a["L1_ffn_gate_b"], B)
    o["moe_b2"] = by_batch_diagonal(a["L1_ffn_b2"])
    return {k: np.ascontiguousarray(v) for k, v in o.items()}


def kernel(**inputs):
    import concourse.bacc as bacc
    from concourse.bass_utils import run_bass_kernel_spmd

    nc = bacc.Bacc("TRN2", target_bir_lowering=False, num_devices=1)
    arrays = {f"in_{n}": v for n, v in lay_out({n: np.asarray(v) for n, v in inputs.items()}).items()}
    d = {n[3:]: nc.dram_tensor(n, v.shape, mybir.dt.from_np(v.dtype), kind="ExternalInput").ap()
         for n, v in arrays.items()}
    out = nc.dram_tensor("out", (NBLK, TB, BC), F32, kind="ExternalOutput").ap()
    build(nc, d, out)
    got = run_bass_kernel_spmd(nc, [arrays], core_ids=[0]).results[0]["out"]
    return np.ascontiguousarray(got.reshape(NBLK, TB, B, C).transpose(2, 0, 1, 3).reshape(B, TOKENS, C))
```

```python
from contextlib import ExitStack

import numpy as np

import concourse.bass as bass
from concourse import mybir

F32 = mybir.dt.float32
ALU = mybir.AluOpType
ACT = mybir.ActivationFunctionType
X = mybir.AxisListType.X

B, C, HT, WD = 8, 64, 56, 56
TOKENS = HT * WD
WS, NH = 4, 8
HEAD = C // NH
STRIPS = HT // WS
WCOLS = WD // WS
WINDOWS = B * WCOLS
WTOK = WS * WS
TB = 2 * WD
NBLK = TOKENS // TB
BC = B * C
PAIRS = B // 2
PW = 2 * C
MAXLEN = 512
BAND = (MAXLEN - 2 + TB) // TB + 1
HID = 256
EXPERTS = 8
MHID = 128
HALF_TOK = PAIRS * TB
STEP_LOOP = 64
XCHUNK = 16
QUAD = 32
EPS = 1e-5
NEG = -1.0e30


def pipeline(eng, stages, n, tail=0):
    head, most = 4, max(lag for lag, _ in stages)

    def step(t, n_blocks):
        for lag, stage in stages:
            if 0 <= t - lag < n_blocks:
                stage(t - lag, (t - lag) % 2)

    for t in range(head):
        step(t, n)
    with eng.Fori(head // 2, (n - tail) // 2) as pair:
        first = eng.snap(pair * 2)
        for par in range(2):
            for lag, stage in stages:
                stage(first + (par - lag), (par - lag) % 2)
    for t in range(n - tail, n + most):
        step(t, n)


def wait_count(eng, sem, i, per, offset):
    if isinstance(i, int) and i * per + offset <= 0:
        return
    eng.wait_ge(sem, i * per + offset)


def wait_former(eng, sem, i, per=1, ago=2):
    wait_count(eng, sem, i, per, (1 - ago) * per)


def wait_load(eng, sems, i, par):
    eng.wait_ge(sems[par], i * 8 + (16 - 8 * par))


def block_cols(t, i, width=BC):
    return t[:, bass.ds(i * width, width)]


def by_batch(ap, n=B):
    return ap.rearrange("p (b c) -> p b c", b=n)


class Norm:

    def __init__(self, nc, ctx, hidden, name):
        sb = lambda n, s: ctx.enter_context(nc.sbuf_tensor(f"{name}_{n}", s, F32))
        sem = lambda n: ctx.enter_context(nc.semaphore(f"{name}_{n}"))
        self.hidden = hidden
        self.negmean = sb("negmean", [TB, 2, B])
        self.sumsq = sb("sumsq", [TB, 2, B])
        self.rstd = sb("rstd", [TB, 2, B])
        self.minus_half = sb("minus_half", [TB, B])
        self.centred = sb("centred", [TB, 2, BC])
        self.squares = sb("squares", [TB, 2, BC])
        self.xn = sb("xn", [TB, 2, BC])
        self.total_ready, self.mean_ready = sem("total_ready"), sem("mean_ready")
        self.centred_ready, self.squares_ready = sem("centred_ready"), sem("squares_ready")
        self.sumsq_ready, self.var_ready = sem("sumsq_ready"), sem("var_ready")
        self.rstd_ready, self.xn_ready = sem("rstd_ready"), sem("xn_ready")
        self.half_set = sem("half_set")

    def vector_centre(self, dve, i, par):
        h = by_batch(block_cols(self.hidden, i))
        dve.tensor_reduce(self.negmean[:, par], h, X, ALU.add).then_inc(self.total_ready, 1)
        dve.wait_ge(self.total_ready, i + 1)
        dve.tensor_scalar(self.negmean[:, par], self.negmean[:, par], -1.0 / C, None, ALU.mult)\
           .then_inc(self.mean_ready, 1)
        dve.wait_ge(self.mean_ready, i + 1)
        wait_former(dve, self.xn_ready, i)
        dve.tensor_tensor(by_batch(self.centred[:, par]), h,
                          self.negmean[:, par].unsqueeze(2).broadcast_to([TB, B, C]), ALU.add)\
           .then_inc(self.centred_ready, 1)

    def gpsimd_square(self, pool, i, par):
        pool.wait_ge(self.centred_ready, i + 1)
        wait_former(pool, self.sumsq_ready, i)
        pool.tensor_tensor(self.squares[:, par], self.centred[:, par], self.centred[:, par], ALU.mult)\
            .then_inc(self.squares_ready, 1)

    def vector_sum(self, dve, i, par):
        dve.wait_ge(self.squares_ready, i + 1)
        wait_former(dve, self.xn_ready, i)
        dve.tensor_reduce(self.sumsq[:, par], by_batch(self.squares[:, par]), X, ALU.add)\
           .then_inc(self.sumsq_ready, 1)
        dve.wait_ge(self.sumsq_ready, i + 1)
        dve.tensor_scalar(self.rstd[:, par], self.sumsq[:, par], 1.0 / C, EPS, ALU.mult, ALU.add)\
           .then_inc(self.var_ready, 1)

    def bind_centre(self, dve):
        return lambda i, par: self.vector_centre(dve, i, par)

    def bind_sum(self, dve):
        return lambda i, par: self.vector_sum(dve, i, par)

    def bind_square(self, pool):
        return lambda i, par: self.gpsimd_square(pool, i, par)

    def bind_scale(self, pool, turned, per=1):
        return lambda i, par: self.gpsimd_scale(pool, i, par, turned, per)

    def gpsimd_setup(self, pool):
        pool.memset(self.minus_half[:], -0.5).then_inc(self.half_set, 1)
        pool.wait_ge(self.half_set, 1)

    def gpsimd_scale(self, pool, i, par, turned, per):
        pool.wait_ge(self.var_ready, i + 1)
        pool.tensor_tensor(self.rstd[:, par], self.rstd[:, par], self.minus_half[:], ALU.pow)\
            .then_inc(self.rstd_ready, 1)
        pool.wait_ge(self.rstd_ready, i + 1)
        wait_former(pool, turned, i, per)
        pool.tensor_tensor(by_batch(self.xn[:, par]), by_batch(self.centred[:, par]),
                           self.rstd[:, par].unsqueeze(2).broadcast_to([TB, B, C]), ALU.mult)\
            .then_inc(self.xn_ready, 1)


def window_attention(nc, hidden, ident, bank, d):
    VHEADS = 5
    with ExitStack() as ctx:
        sb = lambda n, s: ctx.enter_context(nc.sbuf_tensor(f"wa_{n}", s, F32))
        sem = lambda n: ctx.enter_context(nc.semaphore(f"wa_{n}"))
        K1 = C + 1
        xs = [sb(f"xs{p}", [K1, WTOK, WINDOWS]) for p in range(2)]
        w_qkv, w_out = sb("w_qkv", [K1, 3 * C]), sb("w_out", [K1, C])
        qkv = [sb(f"qkv{p}", [WINDOWS, WTOK, 3, HEAD, NH]) for p in range(2)]
        bias, last_bias = sb("bias", [WINDOWS, WTOK, WTOK]), sb("last_bias", [WINDOWS, WTOK, WTOK])
        colmask, rowmask = sb("colmask", [WINDOWS, WTOK, WTOK]), sb("rowmask", [WINDOWS, WTOK, WTOK])
        out = [sb(f"att_out{p}", [WINDOWS, WTOK, HEAD, NH]) for p in range(2)]
        outT = [sb(f"outT{p}", [K1, B, WS, WD]) for p in range(2)]
        groups = []
        for g, (h0, h1) in enumerate(((0, VHEADS), (VHEADS, NH))):
            n = h1 - h0
            groups.append(dict(
                heads=slice(h0, h1), n=n,
                score=[sb(f"score{g}{p}", [WINDOWS, WTOK, WTOK, n]) for p in range(2)],
                prod=sb(f"prod{g}", [WINDOWS, WTOK, WTOK, n]),
                top=sb(f"top{g}", [WINDOWS, WTOK, n]), total=sb(f"total{g}", [WINDOWS, WTOK, n]),
                inverse=[sb(f"inverse{g}{p}", [WINDOWS, WTOK, n]) for p in range(2)],
                acc=sb(f"acc{g}", [WINDOWS, WTOK, HEAD, n]), part=sb(f"part{g}", [WINDOWS, WTOK, HEAD, n]),
                **{s: sem(f"{s}{g}") for s in ("qk_chain", "scored", "topped", "shifted", "exped",
                                               "summed", "inverted", "pv_chain", "done")}))
        p_qkv, p_outT, p_h = bank[0:4], bank[4:6], bank[6:8]
        loaded, ones_set, ready = sem("loaded"), sem("ones_set"), sem("ready")
        x_loaded = [sem(f"x_loaded{p}") for p in range(2)]
        qkv_mm, qkv_copied = sem("qkv_mm"), sem("qkv_copied")
        turned, turned_copied = sem("turned"), sem("turned_copied")
        projected, written = sem("projected"), sem("written")
        block = ctx.enter_context(nc.Block())

        @block.sync
        def _(sp):
            flat = lambda t: t[:].rearrange("p q k -> p (q k)")
            sp.dma_start(w_qkv[:], d["w_qkv"]).then_inc(loaded, 16)
            sp.dma_start(w_out[:], d["w_out"]).then_inc(loaded, 16)
            sp.dma_start(ident[:], d["ident"]).then_inc(loaded, 16)
            sp.dma_start(flat(bias), d["pos_bias"].partition_broadcast(WINDOWS)).then_inc(loaded, 16)
            sp.dma_start(flat(colmask), d["colmask"]).then_inc(loaded, 16)
            sp.dma_start(flat(rowmask), d["rowmask"].partition_broadcast(WINDOWS)).then_inc(loaded, 16)

            def load(i, par):
                wait_former(sp, qkv_mm, i, 8)
                sp.dma_start(xs[par][0:C].rearrange("c t w -> c (t w)"),
                             d["x"][bass.ds(i, 1)].rearrange("o c n -> (o c) n")).then_inc(x_loaded[par], 16)

            pipeline(sp, [(0, load)], STRIPS)

        @block.tensor
        def _(pe):
            pe.wait_ge(loaded, 96)
            pe.wait_ge(ones_set, 4)
            pe.wait_ge(ready, 3)

            def make_qkv(i, par):
                wait_load(pe, x_loaded, i, par)
                for t in range(WTOK):
                    if t % 2 == 0:
                        wait_count(pe, qkv_copied, i, 8, t // 2 - 3)
                    mm = pe.matmul(p_qkv[t // 2 % 4][0:WINDOWS, 192 * (t % 2):192 * (t % 2) + 192],
                                   xs[par][:, t], w_qkv[:], start=True, stop=True)
                    if t % 2:
                        mm.then_inc(qkv_mm, 1)

            def project(i, par):
                for g in groups:
                    pe.wait_ge(g["done"], i + 1)
                for r in range(WS):
                    wait_count(pe, turned_copied, i, 4, r - 1)
                    for c in range(WS):
                        tr = pe.matmul(p_outT[r % 2][0:C, c * WINDOWS:(c + 1) * WINDOWS],
                                       out[par][:, r * WS + c].rearrange("p e h -> p (e h)"),
                                       ident[0:WINDOWS, 0:WINDOWS], start=True, stop=True)
                    tr.then_inc(turned, 1)
                pe.wait_ge(turned_copied, i * 4 + 4)
                for half in range(2):
                    wait_count(pe, written, i, 2, half - 1)
                    for b in range(B):
                        mm = pe.matmul(p_h[half][0:TB, b * C:(b + 1) * C],
                                       outT[par][:, b, 2 * half:2 * half + 2, :].rearrange("c r w -> c (r w)"),
                                       w_out[:], start=True, stop=True)
                    mm.then_inc(projected, 1)

            pipeline(pe, [(2, project), (0, make_qkv)], STRIPS)

        @block.scalar
        def _(act):
            def copy_qkv(i, par):
                for g in groups:
                    wait_former(act, g["done"], i)
                for t in range(WTOK // 2):
                    act.wait_ge(qkv_mm, i * 8 + (t + 1))
                    act.activation(qkv[par][:, 2 * t:2 * t + 2].rearrange("p t s e h -> p (t s e h)"),
                                   p_qkv[t % 4][0:WINDOWS, 0:384], ACT.Copy).then_inc(qkv_copied, 1)

            def exps(i, par):
                for g in groups:
                    act.wait_ge(g["shifted"], i + 1)
                    act.activation(g["score"][par][:], g["score"][par][:], ACT.Exp).then_inc(g["exped"], 1)

            def copy_out(i, par):
                wait_former(act, projected, i, 2)
                for r in range(WS):
                    act.wait_ge(turned, i * 4 + (r + 1))
                    for c in range(WS):
                        cp = act.activation(
                            outT[par][0:C, :, r, c::WS],
                            p_outT[r % 2][0:C, c * WINDOWS:(c + 1) * WINDOWS].rearrange("p (b w) -> p b w", b=B),
                            ACT.Copy)
                    cp.then_inc(turned_copied, 1)
                for half in range(2):
                    act.wait_ge(projected, i * 2 + (half + 1))
                    act.activation(block_cols(hidden, i * 2 + half), p_h[half][0:TB, :], ACT.Copy)\
                       .then_inc(written, 1)

            pipeline(act, [(2, copy_out), (0, copy_qkv), (1, exps)], STRIPS)

        def scores(eng, g, i, par):
            score, shape = g["score"][par], [WINDOWS, WTOK, WTOK, g["n"]]
            q, k, _ = (qkv[par][:, :, s, :, g["heads"]] for s in range(3))
            made, steps = 0, 2 * HEAD - 1
            eng.wait_ge(qkv_copied, i * 8 + 8)
            wait_former(eng, g["done"], i)
            for e in range(HEAD):
                qe = q[:, :, e].unsqueeze(2).broadcast_to(shape)
                ke = k[:, :, e].unsqueeze(1).broadcast_to(shape)
                eng.tensor_tensor(g["prod"][:] if e else score[:], qe, ke, ALU.mult).then_inc(g["qk_chain"], 1)
                made += 1
                eng.wait_ge(g["qk_chain"], i * steps + made)
                if e:
                    eng.tensor_tensor(score[:], score[:], g["prod"][:], ALU.add).then_inc(g["qk_chain"], 1)
                    made += 1
                    eng.wait_ge(g["qk_chain"], i * steps + made)
            which = last_bias if isinstance(i, int) and i == STRIPS - 1 else bias
            eng.tensor_tensor(score[:], score[:], which[:].unsqueeze(3).broadcast_to(shape), ALU.add)\
               .then_inc(g["scored"], 1)

        def shift(dve, g, i, par):
            score = g["score"][par]
            dve.wait_ge(g["scored"], i + 1)
            dve.tensor_reduce(g["top"][:], score[:].rearrange("p q k h -> p q h k"), X, ALU.max)\
               .then_inc(g["topped"], 1)
            dve.wait_ge(g["topped"], i + 1)
            dve.tensor_tensor(score[:], score[:], g["top"][:].unsqueeze(2).broadcast_to([WINDOWS, WTOK, WTOK, g["n"]]),
                              ALU.subtract).then_inc(g["shifted"], 1)

        def invert(dve, g, i, par):
            dve.wait_ge(g["exped"], i + 1)
            wait_former(dve, g["done"], i)
            dve.tensor_reduce(g["total"][:], g["score"][par][:].rearrange("p q k h -> p q h k"), X, ALU.add)\
               .then_inc(g["summed"], 1)
            dve.wait_ge(g["summed"], i + 1)
            dve.reciprocal(g["inverse"][par][:], g["total"][:]).then_inc(g["inverted"], 1)

        def values(eng, g, i, par):
            oshape, v = [WINDOWS, WTOK, HEAD, g["n"]], qkv[par][:, :, 2, :, g["heads"]]
            made, steps = 0, 2 * WTOK - 1
            eng.wait_ge(g["exped"], i + 1)
            for t in range(WTOK):
                w = g["score"][par][:, :, t].unsqueeze(2).broadcast_to(oshape)
                vt = v[:, t].unsqueeze(1).broadcast_to(oshape)
                eng.tensor_tensor(g["part"][:] if t else g["acc"][:], w, vt, ALU.mult).then_inc(g["pv_chain"], 1)
                made += 1
                eng.wait_ge(g["pv_chain"], i * steps + made)
                if t:
                    eng.tensor_tensor(g["acc"][:], g["acc"][:], g["part"][:], ALU.add).then_inc(g["pv_chain"], 1)
                    made += 1
                    eng.wait_ge(g["pv_chain"], i * steps + made)
            eng.wait_ge(g["inverted"], i + 1)
            wait_former(eng, turned, i, 4)
            eng.tensor_tensor(out[par][:, :, :, g["heads"]], g["acc"][:],
                              g["inverse"][par][:].unsqueeze(2).broadcast_to(oshape), ALU.mult)\
               .then_inc(g["done"], 1)
            eng.wait_ge(g["done"], i + 1)

        @block.vector
        def _(dve):
            for t in (*xs, *outT):
                dve.memset(t[C:K1], 1.0).then_inc(ones_set, 1)
            dve.wait_ge(loaded, 96)
            dve.tensor_tensor(bias[:], bias[:], colmask[:], ALU.add).then_inc(ready, 1)
            dve.wait_ge(ready, 1)
            dve.tensor_tensor(last_bias[:], bias[:], rowmask[:], ALU.add).then_inc(ready, 1)
            dve.tensor_scalar(w_qkv[:, 0:C], w_qkv[:, 0:C], float(HEAD) ** -0.5, None, ALU.mult)\
               .then_inc(ready, 1)
            dve.wait_ge(ready, 3)
            own, other = groups

            def strip(i, par):
                scores(dve, own, i, par)
                shift(dve, own, i, par)
                shift(dve, other, i, par)
                invert(dve, own, i, par)
                invert(dve, other, i, par)
                values(dve, own, i, par)

            pipeline(dve, [(1, strip)], STRIPS, tail=2)

        @block.gpsimd
        def _(pool):
            pool.wait_ge(ready, 3)
            own = groups[1]
            pipeline(pool, [(1, lambda i, par: scores(pool, own, i, par)),
                            (1, lambda i, par: values(pool, own, i, par))], STRIPS, tail=2)


def time_mixing(nc, hidden, ident, bank, d):
    with ExitStack() as ctx:
        sb = lambda n, s: ctx.enter_context(nc.sbuf_tensor(f"tm_{n}", s, F32))
        sem = lambda n: ctx.enter_context(nc.semaphore(f"tm_{n}"))
        norm = Norm(nc, ctx, hidden, "n1")
        weights = {n: [sb(f"{n}_{which}", [PW, PW]) for which in ("now", "before")] for n in "kvr"}
        mix = sb("mix", [PW, 3])
        w_o = sb("w_o", [PW, PW])
        toeplitz = sb("toeplitz", [TB, BAND + 1, TB])
        triangle, ones = sb("triangle", [TB, TB]), sb("ones", [TB, TB])
        xT = [sb(f"xT{p}", [PW, PAIRS, 1 + TB]) for p in range(2)]
        clipped = sb("clipped", [TB, 2, BC])
        k = [sb(f"k{p}", [TB, BC]) for p in range(2)]
        neg_r_exp = sb("neg_r_exp", [TB, 2, BC])
        den, inverse = sb("den", [TB, BC]), sb("inverse", [TB, BC])
        y = [sb(f"y{p}", [TB, BC]) for p in range(2)]
        yT = [sb(f"yT{p}", [PW, PAIRS, TB]) for p in range(2)]
        kv = sb("kv", [TB, (BAND + NBLK) * BC])
        k_before = [sb(f"k_before{p}", [TB, BC]) for p in range(2)]
        kv_far = [sb(f"kv_far{p}", [TB, BC]) for p in range(2)]
        p_x, p_k, p_v, p_r, p_sum, p_wkv, p_y, p_o = bank
        (loaded, zeroed, mixed, turned, turned_copied, k_mm, v_mm, r_mm, clip_done, k_ready, r_ready, kv_ready,
         before_ready, far_ready, wkv_mm, den_ready, inverse_ready, y_ready, y_turned, y_copied, o_mm, added) = (
            sem(n) for n in (
                "loaded", "zeroed", "mixed", "turned", "turned_copied", "k_mm", "v_mm", "r_mm", "clip_done",
                "k_ready", "r_ready", "kv_ready", "before_ready", "far_ready", "wkv_mm", "den_ready",
                "inverse_ready", "y_ready", "y_turned", "y_copied", "o_mm", "added"))
        kv_block = lambda slot: block_cols(kv, slot)
        block = ctx.enter_context(nc.Block())

        @block.sync
        def _(sp):
            sp.wait_ge(zeroed, 8)
            for b in range(2):
                half = slice(b * C, b * C + C)
                for n in "kvr":
                    for t in weights[n]:
                        sp.dma_start(t[half, half], d[f"w_{n}"]).then_inc(loaded, 16)
                sp.dma_start(w_o[half, half], d["w_o"]).then_inc(loaded, 16)
                sp.dma_start(mix[half], d["mix"]).then_inc(loaded, 16)
            sp.dma_start(toeplitz[:], d["toeplitz"]).then_inc(loaded, 16)
            sp.dma_start(triangle[:], d["triangle"]).then_inc(loaded, 16)

        @block.tensor
        def _(pe):
            pe.wait_ge(loaded, 18 * 16)
            pe.wait_ge(mixed, 7)
            pe.wait_ge(zeroed, 17)

            def turn(i, par):
                pe.wait_ge(norm.xn_ready, i + 1)
                wait_former(pe, turned_copied, i, ago=1)
                for p in range(PAIRS):
                    tr = pe.transpose(p_x[:, p * TB:(p + 1) * TB], norm.xn[:, par, p * PW:(p + 1) * PW],
                                      ident[0:TB, 0:TB])
                tr.then_inc(turned, 1)

            def older(i, par):
                pe.wait_ge(far_ready, i + 1)
                wait_former(pe, y_ready, i, ago=1)
                pe.matmul(p_wkv[0:TB, :], toeplitz[:, BAND], kv_far[par][:], start=True, stop=False)
                wait_former(pe, kv_ready, i, ago=1)
                for j in range(BAND - 1, 0, -1):
                    pe.matmul(p_wkv[0:TB, :], toeplitz[:, j], kv_block(i + (BAND - j)), start=False, stop=False)

            def project(i, par):
                pe.wait_ge(turned_copied, i + 1)
                for n, into, read, made in (("k", p_k, clip_done, k_mm), ("v", p_v, kv_ready, v_mm),
                                            ("r", p_r, r_ready, r_mm)):
                    wait_former(pe, read, i, ago=1)
                    for p in range(PAIRS):
                        dst = into[0:TB, p * PW:(p + 1) * PW]
                        pe.matmul(dst, xT[par][:, p, 1:1 + TB], weights[n][0][:], start=True, stop=False)
                        mm = pe.matmul(dst, xT[par][:, p, 0:TB], weights[n][1][:], start=False, stop=True)
                    mm.then_inc(made, 1)

            def newest(i, par):
                pe.wait_ge(before_ready, i + 1)
                pe.matmul(p_sum[0:TB, :], ones[:], k_before[par][:], start=True, stop=False)
                pe.wait_ge(k_ready, i + 1)
                pe.matmul(p_sum[0:TB, :], triangle[:], k[par][:], start=False, stop=True)
                pe.wait_ge(kv_ready, i + 1)
                pe.matmul(p_wkv[0:TB, :], toeplitz[:, 0], kv_block(i + BAND), start=False, stop=True)\
                  .then_inc(wkv_mm, 1)

            def turn_y(i, par):
                pe.wait_ge(y_ready, i + 1)
                wait_former(pe, y_copied, i, ago=1)
                for p in range(PAIRS):
                    tr = pe.transpose(p_y[:, p * TB:(p + 1) * TB], y[par][:, p * PW:(p + 1) * PW], ident[0:TB, 0:TB])
                tr.then_inc(y_turned, 1)

            def output(i, par):
                pe.wait_ge(y_copied, i + 1)
                wait_former(pe, added, i, ago=1)
                for p in range(PAIRS):
                    mm = pe.matmul(p_o[0:TB, p * PW:(p + 1) * PW], yT[par][:, p], w_o[:], start=True, stop=True)
                mm.then_inc(o_mm, 1)

            pipeline(pe, [(1, turn), (1, older), (1, project), (2, turn_y), (1, newest), (2, output)], NBLK)

        @block.scalar
        def _(act):
            def copy_turned(i, par):
                act.wait_ge(turned, i + 1)
                wait_former(act, r_mm, i, ago=1)
                src = p_x[:, 0:HALF_TOK].rearrange("p (g t) -> p g t", g=PAIRS)
                act.activation(xT[par][:, :, 1:1 + TB], src, ACT.Copy)
                act.activation(xT[1 - par][:, :, 0:1], src[:, :, TB - 1:TB], ACT.Copy).then_inc(turned_copied, 1)

            def exp_k(i, par):
                act.wait_ge(clip_done, i + 1)
                wait_former(act, wkv_mm, i)
                wait_former(act, kv_ready, i)
                wait_count(act, before_ready, i, 1, 0)
                act.activation(k[par][:], clipped[:, par], ACT.Exp).then_inc(k_ready, 1)

            def exp_r(i, par):
                act.wait_ge(r_mm, i + 1)
                wait_former(act, y_ready, i)
                act.activation(neg_r_exp[:, par], p_r[0:TB, :], ACT.Exp, scale=-1.0).then_inc(r_ready, 1)

            def copy_y(i, par):
                act.wait_ge(y_turned, i + 1)
                wait_former(act, o_mm, i)
                act.activation(yT[par][:].rearrange("p g t -> p (g t)"), p_y[:, 0:HALF_TOK], ACT.Copy)\
                   .then_inc(y_copied, 1)

            act.wait_ge(zeroed, 17)
            pipeline(act, [(1, copy_turned), (1, exp_k), (1, exp_r), (2, copy_y)], NBLK)

        @block.vector
        def _(dve):
            for t in (*(t for n in "kvr" for t in weights[n]), w_o):
                dve.memset(t[:], 0.0).then_inc(zeroed, 1)
            dve.memset(ones[:], 1.0).then_inc(zeroed, 1)
            dve.memset(xT[0][:, :, 0:1], 0.0).then_inc(zeroed, 1)
            dve.memset(kv[:, 0:BAND * BC], 0.0).then_inc(zeroed, 1)
            for t in (*k_before, *kv_far):
                dve.memset(t[:], 0.0).then_inc(zeroed, 1)
            dve.memset(y[0][:], 0.0).then_inc(zeroed, 1)
            dve.memset(y[1][:], 0.0).then_inc(zeroed, 1)
            dve.memset(den[:], 0.0).then_inc(zeroed, 1)
            dve.wait_ge(loaded, 18 * 16)
            dve.wait_ge(zeroed, 17)
            for j, n in enumerate("kvr"):
                now, before = weights[n]
                dve.tensor_scalar(now[:], now[:], mix[:, j:j + 1], None, ALU.mult).then_inc(mixed, 1)
            dve.wait_ge(mixed, 3)
            dve.tensor_scalar(mix[:], mix[:], -1.0, 1.0, ALU.mult, ALU.add).then_inc(mixed, 1)
            dve.wait_ge(mixed, 4)
            for j, n in enumerate("kvr"):
                now, before = weights[n]
                dve.tensor_scalar(before[:], before[:], mix[:, j:j + 1], None, ALU.mult).then_inc(mixed, 1)

            def clip(i, par):
                dve.wait_ge(k_mm, i + 1)
                wait_former(dve, k_ready, i)
                dve.tensor_scalar(clipped[:, par], p_k[0:TB, :], 30.0, -60.0, ALU.min, ALU.max)\
                   .then_inc(clip_done, 1)

            def multiply_kv(i, par):
                dve.wait_ge(v_mm, i + 1)
                dve.wait_ge(k_ready, i + 1)
                dve.tensor_tensor(kv_block(i + BAND), p_v[0:TB, :], k[par][:], ALU.mult).then_inc(kv_ready, 1)

            def combine(i, par):
                dve.wait_ge(wkv_mm, i + 1)
                dve.wait_ge(r_ready, i + 1)
                dve.scalar_tensor_tensor(den[:], neg_r_exp[:, par], 1.0, p_sum[0:TB, :], ALU.add, ALU.mult)\
                   .then_inc(den_ready, 1)
                dve.wait_ge(den_ready, i + 1)
                wait_former(dve, y_ready, i, ago=1)
                dve.reciprocal(inverse[:], den[:]).then_inc(inverse_ready, 1)
                dve.wait_ge(inverse_ready, i + 1)
                wait_former(dve, y_turned, i)
                dve.tensor_tensor(y[par][:], p_wkv[0:TB, :], inverse[:], ALU.mult).then_inc(y_ready, 1)

            def add(i, par):
                dve.wait_ge(o_mm, i + 1)
                h = block_cols(hidden, i)
                dve.tensor_tensor(h, h, p_o[0:TB, :], ALU.add).then_inc(added, 1)

            pipeline(dve, [(0, norm.bind_centre(dve)), (0, norm.bind_sum(dve)), (1, clip), (1, multiply_kv),
                           (1, combine), (2, add)], NBLK)

        @block.gpsimd
        def _(pool):
            norm.gpsimd_setup(pool)
            pool.wait_ge(zeroed, 17)

            def far(i, par):
                wait_former(pool, k_mm, i)
                wait_former(pool, far_ready, i, ago=1)
                pool.tensor_tensor(kv_far[par][:], kv_far[1 - par][:], kv_block(i), ALU.add).then_inc(far_ready, 1)

            def before(i, par):
                if isinstance(i, int) and i == 0:
                    pool.sem_inc(before_ready, 1)
                pool.wait_ge(k_ready, i + 1)
                wait_former(pool, wkv_mm, i, ago=1)
                pool.wait_ge(before_ready, i + 1)
                pool.tensor_tensor(k_before[1 - par][:], k_before[par][:], k[par][:], ALU.add)\
                    .then_inc(before_ready, 1)

            pipeline(pool, [(0, norm.bind_square(pool)), (0, norm.bind_scale(pool, turned)), (0, far), (1, before)], NBLK)


def first_of_maxima(dve, like, order, key, last, hot, then):
    shape = [TB, B, EXPERTS]
    then(dve.scalar_tensor_tensor(by_batch(key), by_batch(like), 0.0, by_batch(order), ALU.is_equal, ALU.mult))
    then(dve.tensor_reduce(last, by_batch(key), X, ALU.max))
    then(dve.tensor_tensor(by_batch(hot), by_batch(key), last.unsqueeze(2).broadcast_to(shape), ALU.is_equal))


def expert_choice(nc, hidden, ident, bank, d, xt):
    KH = HID // 128
    with ExitStack() as ctx:
        sb = lambda n, s: ctx.enter_context(nc.sbuf_tensor(f"ec_{n}", s, F32))
        sem = lambda n: ctx.enter_context(nc.semaphore(f"ec_{n}"))
        norm, norm_rnn = Norm(nc, ctx, hidden, "n2"), Norm(nc, ctx, hidden, "n3")
        w1 = [sb(f"w1_{which}", [PW, HID]) for which in ("even", "odd")]
        b1 = sb("b1", [128, KH])
        w_gate = sb("w_gate", [128, KH, TB])
        gate_bias, order = sb("gate_bias", [TB, B * EXPERTS]), sb("order", [TB, B * EXPERTS])
        w_down = sb("w_down", [128, KH, EXPERTS * C])
        b_down = sb("b_down", [128, BC])
        xT = [sb(f"xT2{p}", [PW, HALF_TOK]) for p in range(2)]
        hT = [sb(f"hT{p}", [128, KH, 2, HALF_TOK]) for p in range(2)]
        logits, shifted = sb("logits", [TB, B * EXPERTS]), sb("shifted", [TB, B * EXPERTS])
        exps, key, hot = (sb(n, [TB, B * EXPERTS]) for n in ("exps", "key", "hot"))
        top, total, inverse, last = (sb(n, [TB, B]) for n in ("top2", "total2", "inverse2", "last"))
        gates = [sb(f"gates{p}", [TB, B * EXPERTS]) for p in range(2)]
        gatesT = [sb(f"gatesT{p}", [128, TB]) for p in range(2)]
        weighted = [sb(f"weighted{p}", [TB, EXPERTS, C]) for p in range(2)]
        chosen = sb("chosen", [TB, BC])
        xT_rnn = [sb(f"xT_rnn{p}", [C, TB, B]) for p in range(2)]
        p_x, p_gate, p_bias, p_rnn = bank[0:4]
        p_gT = p_gate
        p_h, p_e = bank[4:6], bank[6:8]
        rnn_turned, rnn_copied = sem("rnn_turned"), sem("rnn_copied")
        stored = [sem(f"stored{p}") for p in range(2)]
        (loaded, zeroed, turned, turned_copied, h_mm, h_ready, gate_mm, chain, shift_done, exp_done, gates_ready,
         gates_turned, gates_copied, expert_mm, weighted_ready, chosen_ready, bias_mm, added) = (sem(n) for n in (
            "loaded", "zeroed", "turned", "turned_copied", "h_mm", "h_ready", "gate_mm", "chain", "shift_done",
            "exp_done", "gates_ready", "gates_turned", "gates_copied", "expert_mm", "weighted_ready",
            "chosen_ready", "bias_mm", "added"))
        block = ctx.enter_context(nc.Block())

        def tokens_of(par, m, b):
            return hT[par][:, m, b % 2, b // 2 * TB:(b // 2 + 1) * TB]

        @block.sync
        def _(sp):
            for t, n in ((w1[0], "ffn_w1_even"), (w1[1], "ffn_w1_odd"), (b1, "ffn_b1"), (w_gate, "ffn_w_gate"),
                         (w_down, "ffn_w_down"), (b_down, "ffn_b_down")):
                sp.dma_start(t[:], d[n]).then_inc(loaded, 16)
            sp.dma_start(gate_bias[:], d["ffn_gate_bias"].partition_broadcast(TB)).then_inc(loaded, 16)
            sp.dma_start(order[:], d["order"].partition_broadcast(TB)).then_inc(loaded, 16)

            def store(i, par):
                sp.wait_ge(rnn_copied, i * 2 + 2)
                sp.dma_start(block_cols(xt, i, TB * B), xT_rnn[par][:].rearrange("c t b -> c (t b)"))\
                  .then_inc(stored[par], 16)

            pipeline(sp, [(0, store)], NBLK)
            for s in stored:
                sp.wait_ge(s, NBLK // 2 * 16)

        @block.tensor
        def _(pe):
            pe.wait_ge(loaded, 8 * 16)
            pe.wait_ge(zeroed, 2)

            def turn(i, par):
                pe.wait_ge(norm.xn_ready, i + 1)
                wait_former(pe, turned_copied, i, ago=1)
                for p in range(PAIRS):
                    tr = pe.transpose(p_x[:, p * TB:(p + 1) * TB], norm.xn[:, par, p * PW:(p + 1) * PW],
                                      ident[0:TB, 0:TB])
                tr.then_inc(turned, 1)

            def hid(i, par):
                pe.wait_ge(turned_copied, i + 1)
                for n in range(2 * KH):
                    m, side = n // 2, n % 2
                    wait_count(pe, h_ready, i, 2 * KH, n - 1)
                    pe.matmul(p_h[n % 2][:, 0:HALF_TOK], w1[side][:, m * 128:(m + 1) * 128], xT[par][:],
                              start=True, stop=True).then_inc(h_mm, 1)

            def turn_gates(i, par):
                pe.wait_ge(gates_ready, i + 1)
                wait_former(pe, gates_copied, i, ago=1)
                pe.matmul(p_gT[0:B * EXPERTS, 0:TB], gates[par][:], ident[0:TB, 0:TB], start=True, stop=True)\
                  .then_inc(gates_turned, 1)

            def experts(i, par):
                for b in range(B):
                    if b == B // 2:
                        turn_gates(i, par)
                    wait_count(pe, weighted_ready, i, B, b - 1)
                    for m in range(KH):
                        mm = pe.matmul(p_e[b % 2][0:TB, :], tokens_of(par, m, b), w_down[:, m],
                                       start=(m == 0), stop=(m == KH - 1))
                    mm.then_inc(expert_mm, 1)
                pe.wait_ge(gates_copied, i + 1)
                wait_former(pe, added, i, 2, ago=1)
                pe.matmul(p_bias[0:TB, :], gatesT[par][:], b_down[:], start=True, stop=True).then_inc(bias_mm, 1)

            def gate(i, par):
                pe.wait_ge(h_ready, i * 2 * KH + 2 * KH)
                wait_former(pe, shift_done, i, ago=1)
                for b in range(B):
                    for m in range(KH):
                        mm = pe.matmul(p_gate[0:TB, b * EXPERTS:b * EXPERTS + TB], tokens_of(par, m, b),
                                       w_gate[:, m], start=(m == 0), stop=(m == KH - 1))
                mm.then_inc(gate_mm, 1)

            def turn_rnn(i, par, half):
                pe.wait_ge(norm_rnn.xn_ready, i + 1)
                wait_count(pe, rnn_copied, i, 2, half)
                for b in range(B // 2):
                    at = (half * B // 2 + b) * C
                    mm = pe.matmul(p_rnn[0:C, b * TB:(b + 1) * TB], norm_rnn.xn[:, par, at:at + C], ident[0:TB, 0:TB],
                                   start=True, stop=True)
                mm.then_inc(rnn_turned, 1)

            pipeline(pe, [(1, hid), (2, experts), (3, lambda i, par: turn_rnn(i, par, 0)), (1, gate), (0, turn),
                          (3, lambda i, par: turn_rnn(i, par, 1))], NBLK)

        @block.scalar
        def _(act):
            def copy_turned(i, par):
                act.wait_ge(turned, i + 1)
                wait_former(act, h_mm, i, 2 * KH)
                act.activation(xT[par][:], p_x[:, 0:HALF_TOK], ACT.Copy).then_inc(turned_copied, 1)

            def gelu(i, par):
                wait_former(act, expert_mm, i, B)
                for n in range(2 * KH):
                    act.wait_ge(h_mm, i * 2 * KH + (n + 1))
                    act.activation(hT[par][:, n // 2, n % 2], p_h[n % 2][:, 0:HALF_TOK], ACT.Gelu,
                                   bias=b1[:, n // 2:n // 2 + 1]).then_inc(h_ready, 1)

            def exp(i, par):
                act.wait_ge(shift_done, i + 1)
                wait_former(act, gates_ready, i, ago=1)
                act.activation(exps[:], shifted[:], ACT.Exp).then_inc(exp_done, 1)

            def copy_gates(i, par):
                act.wait_ge(gates_turned, i + 1)
                wait_former(act, bias_mm, i)
                act.activation(gatesT[par][0:B * EXPERTS], p_gT[0:B * EXPERTS, 0:TB], ACT.Copy)\
                   .then_inc(gates_copied, 1)

            def copy_rnn(i, par, half):
                act.wait_ge(rnn_turned, i * 2 + (half + 1))
                if half == 0:
                    wait_count(act, stored[par], i, 8, -8 * par)
                b0 = half * B // 2
                act.activation(xT_rnn[par][:, :, b0:b0 + B // 2].rearrange("c t b -> c b t"),
                               p_rnn[0:C, 0:HALF_TOK].rearrange("c (b t) -> c b t", b=B // 2), ACT.Copy)\
                   .then_inc(rnn_copied, 1)

            act.wait_ge(loaded, 8 * 16)
            pipeline(act, [(1, gelu), (2, exp), (2, copy_gates), (3, lambda i, par: copy_rnn(i, par, 0)),
                           (0, copy_turned), (3, lambda i, par: copy_rnn(i, par, 1))], NBLK)

        @block.vector
        def _(dve):
            for t in gatesT:
                dve.memset(t[:], 0.0).then_inc(zeroed, 1)
            dve.wait_ge(loaded, 8 * 16)
            dve.wait_ge(zeroed, 2)

            shape = [TB, B, EXPERTS]

            def counter(i, made):
                made = [made]

                def then(ins):
                    made[0] += 1
                    ins.then_inc(chain, 1)
                    dve.wait_ge(chain, i * 7 + made[0])
                return then

            def choose(i, par):
                then = counter(i, 0)
                dve.wait_ge(gate_mm, i + 1)
                then(dve.tensor_tensor(logits[:], p_gate[0:TB, 0:B * EXPERTS], gate_bias[:], ALU.add))
                then(dve.tensor_reduce(top[:], by_batch(logits[:]), X, ALU.max))
                dve.tensor_tensor(by_batch(shifted[:]), by_batch(logits[:]),
                                  top[:].unsqueeze(2).broadcast_to(shape), ALU.subtract).then_inc(shift_done, 1)
                dve.wait_ge(shift_done, i + 1)
                first_of_maxima(dve, shifted[:], order[:], key[:], last[:], hot[:], then)

            def make_gates(i, par):
                then = counter(i, 5)
                dve.wait_ge(exp_done, i + 1)
                then(dve.tensor_reduce(total[:], by_batch(exps[:]), X, ALU.add))
                then(dve.reciprocal(inverse[:], total[:]))
                wait_former(dve, gates_turned, i)
                dve.tensor_tensor(by_batch(gates[par][:]), by_batch(hot[:]),
                                  inverse[:].unsqueeze(2).broadcast_to(shape), ALU.mult).then_inc(gates_ready, 1)
                dve.wait_ge(gates_ready, i + 1)

            def weigh(i, par):
                def sum_experts(b):
                    dve.wait_ge(weighted_ready, i * B + (b + 1))
                    dve.tensor_reduce(chosen[:, b * C:(b + 1) * C], weighted[b % 2][:].rearrange("p e c -> p c e"),
                                      X, ALU.add).then_inc(chosen_ready, 1)

                wait_former(dve, added, i, 2, ago=1)
                for b in range(B):
                    dve.wait_ge(expert_mm, i * B + (b + 1))
                    wait_count(dve, chosen_ready, i, B, b - 1)
                    dve.tensor_tensor(weighted[b % 2][:], p_e[b % 2][0:TB, :].rearrange("p (e c) -> p e c", e=EXPERTS),
                                      gates[par][:, b * EXPERTS:(b + 1) * EXPERTS].unsqueeze(2)
                                      .broadcast_to([TB, EXPERTS, C]), ALU.mult).then_inc(weighted_ready, 1)
                    if b:
                        sum_experts(b - 1)
                sum_experts(B - 1)

            def add(i, par):
                h = block_cols(hidden, i)
                dve.wait_ge(bias_mm, i + 1)
                dve.tensor_tensor(h, h, p_bias[0:TB, :], ALU.add).then_inc(added, 1)
                dve.wait_ge(chosen_ready, i * B + B)
                dve.wait_ge(added, i * 2 + 1)
                dve.tensor_tensor(h, h, chosen[:], ALU.add).then_inc(added, 1)

            def settle(i, par):
                wait_former(dve, norm_rnn.xn_ready, i)
                dve.wait_ge(added, i * 2 + 2)
                dve.memset(norm_rnn.rstd[:, par], 0.0)

            pipeline(dve, [(2, choose), (3, settle), (3, norm_rnn.bind_centre(dve)), (0, norm.bind_centre(dve)),
                           (3, norm_rnn.bind_sum(dve)), (0, norm.bind_sum(dve)), (2, make_gates), (2, weigh), (2, add)],
                     NBLK)

        @block.gpsimd
        def _(pool):
            norm.gpsimd_setup(pool)
            norm_rnn.gpsimd_setup(pool)
            pipeline(pool, [(3, norm_rnn.bind_square(pool)), (0, norm.bind_square(pool)),
                            (3, norm_rnn.bind_scale(pool, rnn_turned, 2)), (0, norm.bind_scale(pool, turned))], NBLK)


def recurrence(nc, ident, bank, d, xt, rnn_out):
    J, QUADS = HID // 128, 128 // QUAD
    QW = HID // QUADS
    CHUNKS = STEP_LOOP // XCHUNK
    LOOPS = TOKENS // STEP_LOOP
    LEAD = 24
    EXTRA = -(-LEAD // XCHUNK)
    OUT_AT = {18: 0, 34: 1, 50: 2, STEP_LOOP - 1: 3}
    with ExitStack() as ctx:
        sb = lambda n, s: ctx.enter_context(nc.sbuf_tensor(f"rn_{n}", s, F32))
        sem = lambda n: ctx.enter_context(nc.semaphore(f"rn_{n}"))
        x = sb("rnn_x", [128, STEP_LOOP, B])
        w_x = sb("w_x", [128, QUADS, QW])
        w_hh = [sb(f"w_hh{l}", [128, J, QUADS, QW]) for l in range(2)]
        w_up = sb("w_up", [128, J, QUADS, QW])
        bias, bias2 = sb("rnn_bias", [128, J]), sb("rnn_bias2", [128, J])
        w_fc, fc_bias = sb("w_fc", [128, J, C]), sb("fc_bias", [128, C])
        h = [sb(f"h{l}", [128, J, STEP_LOOP, B]) for l in range(2)]
        pre = [sb(f"pre{l}", [128, 2, J * QUAD]) for l in range(2)]
        up = sb("up", [128, 2, 2, XCHUNK, B])
        fc = sb("fc", [128, CHUNKS, C])
        p_h = [bank[0:2], bank[2:4]]
        p_fc, p_up = bank[4:6], bank[6:8]
        loaded, zeroed = sem("loaded"), sem("zeroed")
        x_loaded = [sem(f"x_loaded{q}") for q in range(CHUNKS)]
        summed = [sem("summed0"), sem("summed1")]
        turned = [sem("turned0"), sem("turned1")]
        h_ready = [sem("h_ready0"), sem("h_ready1")]
        up_mm, up_ready = sem("up_mm"), sem("up_ready")
        fc_free, fc_mm = sem("fc_free"), sem("fc_mm")
        stored = [sem(f"stored{q}") for q in range(CHUNKS)]
        rows = rnn_out.rearrange("n t (b c) -> (n t b) c", b=B)
        block = ctx.enter_context(nc.Block())

        @block.sync
        def _(sp):
            for t, n in ((w_x, "rnn_w_x"), (w_hh[0], "rnn_w_hh0"), (w_hh[1], "rnn_w_hh1"), (w_up, "rnn_w_up"),
                         (w_fc, "rnn_w_fc")):
                flat = "p a b c -> p (a b c)" if len(t.shape) == 4 else "p a b -> p (a b)"
                sp.dma_start(t[:].rearrange(flat), d[n]).then_inc(loaded, 16)
            sp.dma_start(bias[:], d["rnn_b_ih1"]).then_inc(loaded, 16)
            sp.dma_start(bias2[:], d["rnn_b_hh1"]).then_inc(loaded, 16)
            sp.dma_start(fc_bias[:], d["rnn_fc_b"].partition_broadcast(128)).then_inc(loaded, 16)

            def load(chunk, q):
                sp.dma_start(x[0:C, q * XCHUNK:(q + 1) * XCHUNK, :].rearrange("c t b -> c (t b)"),
                             block_cols(xt, chunk, XCHUNK * B)).then_inc(x_loaded[q], 16)

            def store(loop, q):
                sp.wait_ge(fc_free, loop * CHUNKS + (q + 3))
                sp.dma_start(rows[bass.ds((loop * CHUNKS + q) * XCHUNK * B, XCHUNK * B)], fc[:, q])\
                  .then_inc(stored[q], 16)

            for q in range(CHUNKS):
                load(q, q)
            with sp.Fori(1, LOOPS) as m:
                loop = sp.snap(m)
                for q in range(CHUNKS):
                    sp.wait_ge(summed[0], loop * STEP_LOOP + (q + 1 - CHUNKS) * XCHUNK)
                    load(loop * CHUNKS + q, q)
                    store(loop - 1, q)
            for q in range(EXTRA):
                sp.wait_ge(summed[0], TOKENS + (q + 1 - CHUNKS) * XCHUNK)
                load(TOKENS // XCHUNK - 1, q)
            for q in range(CHUNKS):
                store(LOOPS - 1, q)
            for q in range(CHUNKS):
                sp.wait_ge(stored[q], (LOOPS + 1) * 16)
                sp.wait_ge(x_loaded[q], (LOOPS + (q < EXTRA)) * 16)

        @block.tensor
        def _(pe):
            pe.wait_ge(loaded, 8 * 16)
            pe.wait_ge(zeroed, 7)

            def tile(dst, q, state, weights, start, stop):
                return pe.matmul(dst[QUAD * q:QUAD * q + B, 0:QW], state, weights, start=start, stop=stop,
                                 skip_group_check=True, tile_position=(0, QUAD * q))

            def recur(layer, dst, s):
                for j in range(J):
                    for q in range(QUADS):
                        mm = tile(dst, q, h[layer][:, j, (s - 1) % STEP_LOOP], w_hh[layer][:, j, q], False, j == J - 1)
                mm.then_inc(summed[layer], 1)

            def layer0(n, s):
                for q in range(QUADS):
                    tile(p_h[0][s % 2], q, x[:, s], w_x[:, q], True, False)
                pe.wait_ge(h_ready[0], n + 1)
                recur(0, p_h[0][s % 2], s)

            def layer1(n, s):
                for q in range(QUADS):
                    tile(p_h[1][s % 2], q, up[:, s // XCHUNK % 2, q // 2, s % XCHUNK],
                         ident[:, q % 2 * QW:(q % 2 + 1) * QW], True, False)
                pe.wait_ge(h_ready[1], n + 1)
                recur(1, p_h[1][s % 2], s)

            def up_products(s):
                half, j = divmod(s % XCHUNK, 2)
                first = (s // XCHUNK - 1) % CHUNKS * XCHUNK
                mm = pe.matmul(p_up[half][:, 0:XCHUNK * B],
                               w_up[:, j, 2 * half:2 * half + 2].rearrange("p q u -> p (q u)"),
                               h[0][:, j, first:first + XCHUNK].rearrange("p t b -> p (t b)"),
                               start=(j == 0), stop=(j == J - 1))
                if j == J - 1:
                    mm.then_inc(up_mm, 1)

            def outputs(loop, q):
                pe.wait_ge(h_ready[1], loop * STEP_LOOP + (q + 1) * XCHUNK + 1)
                pe.wait_ge(fc_free, loop * CHUNKS + (q + 1))
                for j in range(J):
                    mm = pe.matmul(p_fc[q % 2][:, 0:C],
                                   h[1][:, j, q * XCHUNK:(q + 1) * XCHUNK].rearrange("p t b -> p (t b)"),
                                   w_fc[:, j], start=(j == 0), stop=(j == J - 1))
                mm.then_inc(fc_mm, 1)

            for n in range(LEAD):
                if n % XCHUNK == 0:
                    pe.wait_ge(x_loaded[n // XCHUNK], 16)
                layer0(n, n)
                if n >= XCHUNK and n % XCHUNK < 4:
                    up_products(n)
            with pe.Fori(0, LOOPS) as m:
                loop = pe.snap(m)
                for s in range(STEP_LOOP):
                    ahead = s + LEAD
                    if ahead % XCHUNK == 0:
                        pe.wait_ge(x_loaded[ahead // XCHUNK % CHUNKS], loop * 16 + (16 if ahead < STEP_LOOP else 32))
                    layer0(loop * STEP_LOOP + ahead, ahead % STEP_LOOP)
                    if s % XCHUNK == 0:
                        pe.wait_ge(up_ready, loop * 2 * CHUNKS + (2 * (s // XCHUNK) + 2))
                    layer1(loop * STEP_LOOP + s, s)
                    if ahead % XCHUNK < 4:
                        up_products(ahead)
                    if s in OUT_AT:
                        outputs(loop, OUT_AT[s])

        @block.vector
        def _(dve):
            dve.memset(x[C:128], 0.0).then_inc(zeroed, 1)
            dve.wait_ge(zeroed, 1)
            dve.memset(x[C:C + 2], 1.0).then_inc(zeroed, 1)
            for layer in range(2):
                dve.memset(h[layer][:], 0.0).then_inc(h_ready[layer], 1)
            for t in bank[0:4]:
                dve.memset(t[:], 0.0).then_inc(zeroed, 1)
            for q in range(CHUNKS):
                dve.sem_inc(stored[q], 16)
            for t in p_fc:
                dve.memset(t[:], 0.0).then_inc(fc_free, 1)
            dve.memset(fc[:], 0.0).then_inc(zeroed, 1)
            dve.wait_ge(loaded, 8 * 16)
            dve.wait_ge(zeroed, 7)

            def turn(layer, n, s):
                dve.wait_ge(summed[layer], n + 1)
                dve.transpose(pre[layer][:, s % 2], p_h[layer][s % 2][:, 0:QW]).then_inc(turned[layer], 1)

            def copy_up(s, count):
                half, par = (s % XCHUNK - 2) // 2, (s // XCHUNK - 1) % 2
                dve.wait_ge(up_mm, count + 1)
                dve.tensor_scalar(up[:, par, half].rearrange("p t b -> p (t b)"), p_up[half][:, 0:XCHUNK * B],
                                  bias[:, half:half + 1], bias2[:, half:half + 1], ALU.add, ALU.add)\
                   .then_inc(up_ready, 1)

            def add_bias(loop, q):
                dve.wait_ge(fc_mm, loop * CHUNKS + (q + 1))
                dve.wait_ge(stored[q], (loop + 1) * 16)
                dve.tensor_tensor(fc[:, q], p_fc[q % 2][:, 0:C], fc_bias[:], ALU.add).then_inc(fc_free, 1)

            for n in range(LEAD):
                turn(0, n, n)
                if n >= XCHUNK and n % XCHUNK in (2, 4):
                    copy_up(n, (n % XCHUNK - 2) // 2)
            with dve.Fori(0, LOOPS) as m:
                loop = dve.snap(m)
                for s in range(STEP_LOOP):
                    ahead = s + LEAD
                    turn(0, loop * STEP_LOOP + ahead, ahead)
                    turn(1, loop * STEP_LOOP + s, s)
                    if ahead % XCHUNK in (2, 4):
                        copy_up(ahead, loop * 2 * CHUNKS + (2 * (ahead // XCHUNK - 1) + (ahead % XCHUNK - 2) // 2))
                    if s in OUT_AT:
                        add_bias(loop, OUT_AT[s])

        @block.scalar
        def _(act):
            act.wait_ge(zeroed, 7)
            for layer in range(2):
                act.wait_ge(h_ready[layer], 1)

            def tanh(layer, n, s):
                act.wait_ge(turned[layer], n + 1)
                act.activation(h[layer][:, :, s % STEP_LOOP],
                               pre[layer][:, s % 2].rearrange("p (j b) -> p j b", j=J)[:, :, 0:B], ACT.Tanh)\
                   .then_inc(h_ready[layer], 1)

            for n in range(LEAD):
                tanh(0, n, n)
            with act.Fori(0, LOOPS) as m:
                loop = act.snap(m)
                for s in range(STEP_LOOP):
                    tanh(0, loop * STEP_LOOP + (s + LEAD), s + LEAD)
                    tanh(1, loop * STEP_LOOP + s, s)


def expert_pairs(nc, hidden, ident, bank, d, rnn_out, out):
    with ExitStack() as ctx:
        sb = lambda n, s: ctx.enter_context(nc.sbuf_tensor(f"ep_{n}", s, F32))
        sem = lambda n: ctx.enter_context(nc.semaphore(f"ep_{n}"))
        norm = Norm(nc, ctx, hidden, "n4")
        w1 = [sb(f"m_w1_{which}", [PW, EXPERTS, MHID]) for which in ("even", "odd")]
        b1 = sb("m_b1", [MHID, EXPERTS])
        w2 = sb("m_w2", [MHID, (EXPERTS + 1) * C])
        w_gate = sb("m_w_gate", [PW, PW])
        gate_bias, order = sb("m_gate_bias", [TB, B * EXPERTS]), sb("m_order", [TB, B * EXPERTS])
        b2 = sb("m_b2", [128, BC])
        rnn = [sb(f"rnn{p}", [TB, BC]) for p in range(2)]
        xT = [sb(f"xT4{p}", [PW, HALF_TOK]) for p in range(2)]
        hT = [sb(f"m_hT{p}", [MHID, 2, HALF_TOK]) for p in range(2)]
        logits, shifted, second = (sb(f"m_{n}", [TB, B * EXPERTS]) for n in ("logits", "shifted", "second"))
        exps, key, hot, hot2 = (sb(f"m_{n}", [TB, B * EXPERTS]) for n in ("exps", "key", "hot", "hot2"))
        top, total, inverse, last = (sb(f"m_{n}", [TB, B]) for n in ("top", "total", "inverse", "last"))
        gates = [sb(f"m_gates{p}", [TB, B * EXPERTS]) for p in range(2)]
        gatesT = [sb(f"m_gatesT{p}", [128, TB]) for p in range(2)]
        weighted = [sb(f"m_weighted{p}", [TB, BC]) for p in range(2)]
        acc = [sb(f"acc{p}", [TB, BC]) for p in range(2)]
        result = [sb(f"result{p}", [TB, BC]) for p in range(2)]
        p_x, p_gate, p_gT, p_bias = bank[0:4]
        p_h, p_y = bank[4:6], bank[6:8]
        (loaded, zeroed, rnn_added, turned, turned_copied, h_mm, h_ready, y_mm, gate_mm, chain, shift_done,
         exp_done, gates_ready, gates_turned, gates_copied, weighted_ready, acc_ready, bias_mm, partial,
         result_ready) = (sem(n) for n in (
             "loaded", "zeroed", "rnn_added", "turned", "turned_copied", "h_mm", "h_ready", "y_mm", "gate_mm",
             "chain", "shift_done", "exp_done", "gates_ready", "gates_turned", "gates_copied",
             "weighted_ready", "acc_ready", "bias_mm", "partial", "result_ready"))
        rnn_loaded, stored = ([sem(f"{n}{p}") for p in range(2)] for n in ("rnn_loaded", "stored"))
        block = ctx.enter_context(nc.Block())

        @block.sync
        def _(sp):
            for t, n in ((w1[0], "moe_w1_even"), (w1[1], "moe_w1_odd"), (b1, "moe_b1"), (w2, "moe_w2"),
                         (w_gate, "moe_w_gate"), (b2, "moe_b2")):
                sp.dma_start(t[:].rearrange("p a b -> p (a b)") if len(t.shape) == 3 else t[:], d[n])\
                  .then_inc(loaded, 16)
            sp.dma_start(gate_bias[:], d["moe_gate_bias"].partition_broadcast(TB)).then_inc(loaded, 16)
            sp.dma_start(order[:], d["order"].partition_broadcast(TB)).then_inc(loaded, 16)

            def load(i, par):
                wait_former(sp, rnn_added, i)
                sp.dma_start(rnn[par][:], rnn_out[bass.ds(i, 1)].rearrange("o t f -> (o t) f"))\
                  .then_inc(rnn_loaded[par], 16)

            def store(i, par):
                sp.wait_ge(result_ready, i + 1)
                sp.dma_start(out[bass.ds(i, 1)].rearrange("o t f -> (o t) f"), result[par][:])\
                  .then_inc(stored[par], 16)

            pipeline(sp, [(0, load), (3, store)], NBLK)
            for s in stored:
                sp.wait_ge(s, NBLK // 2 * 16)

        @block.tensor
        def _(pe):
            pe.wait_ge(loaded, 8 * 16)
            pe.wait_ge(zeroed, 2)

            def turn(i, par):
                pe.wait_ge(norm.xn_ready, i + 1)
                wait_former(pe, turned_copied, i, ago=1)
                for p in range(PAIRS):
                    tr = pe.transpose(p_x[:, p * TB:(p + 1) * TB], norm.xn[:, par, p * PW:(p + 1) * PW],
                                      ident[0:TB, 0:TB])
                tr.then_inc(turned, 1)

            def gate(i, par):
                pe.wait_ge(turned_copied, i + 1)
                wait_former(pe, shift_done, i, ago=1)
                for p in range(PAIRS):
                    mm = pe.matmul(p_gate[0:TB, 2 * p * EXPERTS:2 * p * EXPERTS + PW], xT[par][:, p * TB:(p + 1) * TB],
                                   w_gate[:], start=True, stop=True)
                mm.then_inc(gate_mm, 1)

            def up(i, par, e):
                for side in range(2):
                    wait_count(pe, h_ready, i, 2 * EXPERTS, 2 * e + side - 1)
                    pe.matmul(p_h[side][:, 0:HALF_TOK], w1[side][:, e], xT[par][:], start=True, stop=True)\
                      .then_inc(h_mm, 1)

            def down(i, par, e):
                pe.wait_ge(h_ready, i * 2 * EXPERTS + (2 * e + 2))
                wait_count(pe, weighted_ready, i, EXPERTS, e - 1)
                for b in range(B):
                    width = PW if b < B - 1 else C
                    mm = pe.matmul(p_y[e % 2][0:TB, b * C:b * C + width],
                                   hT[e % 2][:, b % 2, b // 2 * TB:(b // 2 + 1) * TB], w2[:, e * C:e * C + width],
                                   start=True, stop=True)
                mm.then_inc(y_mm, 1)

            def first_experts(i, par):
                for e in range(2):
                    up(i, par, e)
                down(i, par, 0)

            def other_experts(i, par):
                for e in range(2, EXPERTS):
                    up(i, par, e)
                    down(i, par, e - 1)
                down(i, par, EXPERTS - 1)

            def turn_gates(i, par):
                pe.wait_ge(gates_ready, i + 1)
                wait_former(pe, gates_copied, i, ago=1)
                pe.matmul(p_gT[0:B * EXPERTS, 0:TB], gates[par][:], ident[0:TB, 0:TB], start=True, stop=True)\
                  .then_inc(gates_turned, 1)

            def bias(i, par):
                pe.wait_ge(gates_copied, i + 1)
                wait_former(pe, partial, i, ago=1)
                pe.matmul(p_bias[0:TB, :], gatesT[par][:], b2[:], start=True, stop=True).then_inc(bias_mm, 1)

            pipeline(pe, [(2, turn_gates), (2, first_experts), (1, gate), (2, other_experts), (2, bias), (0, turn)], NBLK)

        @block.scalar
        def _(act):
            def copy_turned(i, par):
                act.wait_ge(turned, i + 1)
                wait_former(act, h_mm, i, 2 * EXPERTS)
                act.activation(xT[par][:], p_x[:, 0:HALF_TOK], ACT.Copy).then_inc(turned_copied, 1)

            def gelu(i, par, first, last):
                for e in range(first, last):
                    wait_count(act, y_mm, i, EXPERTS, e - 1)
                    for side in range(2):
                        act.wait_ge(h_mm, i * 2 * EXPERTS + (2 * e + side + 1))
                        act.activation(hT[e % 2][:, side], p_h[side][:, 0:HALF_TOK], ACT.Gelu, bias=b1[:, e:e + 1])\
                           .then_inc(h_ready, 1)

            def exp(i, par):
                act.wait_ge(shift_done, i + 1)
                wait_former(act, gates_ready, i, ago=1)
                act.activation(exps[:], shifted[:], ACT.Exp).then_inc(exp_done, 1)

            def copy_gates(i, par):
                act.wait_ge(gates_turned, i + 1)
                wait_former(act, bias_mm, i)
                act.activation(gatesT[par][0:B * EXPERTS], p_gT[0:B * EXPERTS, 0:TB], ACT.Copy)\
                   .then_inc(gates_copied, 1)

            act.wait_ge(loaded, 8 * 16)
            pipeline(act, [(2, copy_gates), (2, lambda i, par: gelu(i, par, 0, 3)), (1, exp),
                           (2, lambda i, par: gelu(i, par, 3, EXPERTS)), (0, copy_turned)], NBLK)

        @block.vector
        def _(dve):
            for t in gatesT:
                dve.memset(t[:], 0.0).then_inc(zeroed, 1)
            dve.wait_ge(loaded, 8 * 16)
            dve.wait_ge(zeroed, 2)

            def add_rnn(i, par):
                h = block_cols(hidden, i)
                wait_load(dve, rnn_loaded, i, par)
                dve.tensor_tensor(h, h, rnn[par][:], ALU.add).then_inc(rnn_added, 1)
                wait_former(dve, norm.xn_ready, i)
                dve.wait_ge(rnn_added, i + 1)
                dve.memset(norm.rstd[:, par], 0.0)

            spread = lambda t: t.unsqueeze(2).broadcast_to([TB, B, EXPERTS])

            def counter(i, made):
                made = [made]

                def then(ins):
                    made[0] += 1
                    ins.then_inc(chain, 1)
                    dve.wait_ge(chain, i * 15 + made[0])
                return then

            def choose(i, par):
                then = counter(i, 0)
                dve.wait_ge(gate_mm, i + 1)
                then(dve.tensor_tensor(logits[:], p_gate[0:TB, 0:B * EXPERTS], gate_bias[:], ALU.add))
                then(dve.tensor_reduce(top[:], by_batch(logits[:]), X, ALU.max))
                dve.tensor_tensor(by_batch(shifted[:]), by_batch(logits[:]), spread(top[:]), ALU.subtract)\
                   .then_inc(shift_done, 1)
                dve.wait_ge(shift_done, i + 1)
                first_of_maxima(dve, shifted[:], order[:], key[:], last[:], hot[:], then)
                then(dve.scalar_tensor_tensor(second[:], hot[:], NEG, shifted[:], ALU.mult, ALU.add))
                then(dve.tensor_reduce(top[:], by_batch(second[:]), X, ALU.max))
                then(dve.tensor_tensor(by_batch(second[:]), by_batch(second[:]), spread(top[:]), ALU.subtract))
                first_of_maxima(dve, second[:], order[:], key[:], last[:], hot2[:], then)
                then(dve.tensor_tensor(hot[:], hot[:], hot2[:], ALU.add))

            def make_gates(i, par):
                then = counter(i, 12)
                dve.wait_ge(exp_done, i + 1)
                then(dve.tensor_reduce(total[:], by_batch(exps[:]), X, ALU.add))
                then(dve.reciprocal(inverse[:], total[:]))
                then(dve.tensor_tensor(by_batch(hot[:]), by_batch(hot[:]), spread(inverse[:]), ALU.mult))
                wait_former(dve, gates_turned, i)
                dve.tensor_tensor(gates[par][:], hot[:], exps[:], ALU.mult).then_inc(gates_ready, 1)
                dve.wait_ge(gates_ready, i + 1)

            def weigh(i, par, first, last):
                for e in range(first, last):
                    dve.wait_ge(y_mm, i * EXPERTS + (e + 1))
                    wait_count(dve, acc_ready, i, EXPERTS - 1, max(e - 1, 0))
                    dve.tensor_tensor(by_batch(weighted[e % 2][:]), by_batch(p_y[e % 2][0:TB, :]),
                                      gates[par][:, e::EXPERTS].unsqueeze(2).broadcast_to([TB, B, C]), ALU.mult)\
                       .then_inc(weighted_ready, 1)

            def finish(i, par):
                dve.wait_ge(bias_mm, i + 1)
                wait_count(dve, stored[par], i, 8, -8 * par)
                dve.tensor_tensor(result[par][:], block_cols(hidden, i), p_bias[0:TB, :], ALU.add)\
                   .then_inc(partial, 1)
                dve.wait_ge(partial, i + 1)
                dve.wait_ge(acc_ready, (i + 1) * (EXPERTS - 1))
                dve.tensor_tensor(result[par][:], result[par][:], acc[par][:], ALU.add).then_inc(result_ready, 1)

            weigh_some = lambda first, last: lambda i, par: weigh(i, par, first, last)
            pipeline(dve, [(3, finish), (2, weigh_some(0, 1)), (1, choose), (2, weigh_some(1, 3)), (0, add_rnn),
                           (0, norm.bind_centre(dve)), (2, weigh_some(3, 4)), (0, norm.bind_sum(dve)),
                           (1, make_gates), (2, weigh_some(4, EXPERTS))], NBLK)

        @block.gpsimd
        def _(pool):
            norm.gpsimd_setup(pool)

            def accumulate(i, par, first, last):
                for e in range(first, last):
                    if e == 1:
                        wait_former(pool, result_ready, i)
                    pool.wait_ge(weighted_ready, i * EXPERTS + (e + 1))
                    if e > 1:
                        pool.wait_ge(acc_ready, i * (EXPERTS - 1) + (e - 1))
                    pool.tensor_tensor(acc[par][:], acc[par][:] if e > 1 else weighted[0][:], weighted[e % 2][:],
                                       ALU.add).then_inc(acc_ready, 1)

            add_some = lambda first, last: lambda i, par: accumulate(i, par, first, last)
            pipeline(pool, [(2, add_some(1, 3)), (0, norm.bind_square(pool)), (2, add_some(3, 4)),
                            (0, norm.bind_scale(pool, turned)), (2, add_some(4, EXPERTS))], NBLK)


def build(nc, d, out):
    with ExitStack() as ctx:
        hidden = ctx.enter_context(nc.sbuf_tensor("hidden", [TB, NBLK * BC], F32))
        ident = ctx.enter_context(nc.sbuf_tensor("identity", [128, 128], F32))
        bank = [ctx.enter_context(nc.psum_tensor(f"bank{k}", [128, 512], F32)) for k in range(8)]
        xt = nc.dram_tensor("normed_turned", (C, TOKENS * B), F32, kind="Internal").ap()
        rnn_out = nc.dram_tensor("rnn_out", (NBLK, TB, BC), F32, kind="Internal").ap()
        window_attention(nc, hidden, ident, bank, d)
        time_mixing(nc, hidden, ident, bank, d)
        expert_choice(nc, hidden, ident, bank, d, xt)
        recurrence(nc, ident, bank, d, xt, rnn_out)
        expert_pairs(nc, hidden, ident, bank, d, rnn_out, out)


def by_batch_diagonal(m):
    o = np.zeros((128, BC), np.float32)
    for b in range(B):
        o[b * EXPERTS:(b + 1) * EXPERTS, b * C:(b + 1) * C] = m
    return o


def lay_out(a):
    o = {"ident": np.eye(128, dtype=np.float32)}
    x = np.roll(a["x"], (-(WS // 2), -(WS // 2)), axis=(2, 3)).reshape(B, C, STRIPS, WS, WCOLS, WS)
    o["x"] = x.transpose(2, 1, 3, 5, 0, 4).reshape(STRIPS, C, WTOK * WINDOWS)
    o["w_qkv"] = np.concatenate([a["L0_tok_w1"], a["L0_tok_b1"][:, None]], 1)\
        .reshape(HEAD, NH, 3, C + 1).transpose(3, 2, 0, 1).reshape(C + 1, 3 * C)
    w2 = a["L0_tok_w2"].reshape(C, NH, HEAD).transpose(2, 1, 0).reshape(C, C)
    o["w_out"] = np.concatenate([w2, a["L0_tok_b2"][None]], 0)
    at = np.array([[i, j] for i in range(WS) for j in range(WS)])
    rel = at[None] - at[:, None] + WS - 1
    o["pos_bias"] = a["L0_tok_pos_emb"][rel[..., 0], rel[..., 1]].reshape(-1)
    low, right = at[:, 0] >= WS // 2, at[:, 1] >= WS // 2
    mask = lambda side: np.where(side[:, None] != side[None], np.float32(NEG), np.float32(0)).reshape(-1)
    o["rowmask"] = mask(low)
    o["colmask"] = np.zeros((B, WCOLS, WTOK * WTOK), np.float32)
    o["colmask"][:, -1] = mask(right)
    o["colmask"] = o["colmask"].reshape(WINDOWS, -1)
    for n in "kvr":
        o[f"w_{n}"] = a[f"L0_attn_W{n}"]
    o["w_o"] = a["L0_attn_Wo"]
    o["mix"] = np.stack([a[f"L0_attn_time_mix_{n}"].reshape(C) for n in "kvr"], 1)
    u, j, t = np.ogrid[0:TB, 0:BAND + 1, 0:TB]
    distance = j * TB + t - u
    distance[:, BAND] = MAXLEN
    o["toeplitz"] = np.where(distance < 0, np.float32(0), a["L0_attn_time_w"][np.clip(MAXLEN - 1 - distance, 0, MAXLEN - 1)])
    o["triangle"] = np.triu(np.ones((TB, TB), np.float32))
    zero = lambda *s: np.zeros(s, np.float32)
    w1 = a["L0_ffn_W1"]
    o["ffn_w1_even"] = np.concatenate([w1, zero(C, HID)])
    o["ffn_w1_odd"] = np.concatenate([zero(C, HID), w1])
    o["ffn_b1"] = a["L0_ffn_b1"].reshape(HID // 128, 128).T
    wg = a["L0_ffn_Wg"].reshape(HID // 128, 128, EXPERTS).transpose(1, 0, 2)
    o["ffn_w_gate"] = np.concatenate([wg, zero(128, HID // 128, TB - EXPERTS)], 2)
    o["ffn_gate_bias"] = np.tile(a["L0_ffn_bg"], B)
    o["order"] = np.tile(np.arange(EXPERTS, 0, -1, dtype=np.float32), B)
    o["ffn_w_down"] = a["L0_ffn_Wd"].reshape(EXPERTS, HID // 128, 128, C).transpose(2, 1, 0, 3)\
        .reshape(128, HID // 128, EXPERTS * C)
    o["ffn_b_down"] = by_batch_diagonal(a["L0_ffn_bd"])
    def unit_rows(m):
        return m.reshape(4, HID // 128, QUAD, -1).transpose(0, 2, 1, 3).reshape(128, -1)
    o["rnn_w_x"] = np.concatenate([a["L1_attn_W_ih_0"].T, a["L1_attn_b_ih_0"][None], a["L1_attn_b_hh_0"][None],
                                   zero(128 - C - 2, HID)])
    o["rnn_w_hh0"] = unit_rows(a["L1_attn_W_hh_0"].T)
    o["rnn_w_hh1"] = unit_rows(a["L1_attn_W_hh_1"].T)
    o["rnn_w_up"] = unit_rows(a["L1_attn_W_ih_1"].T)
    o["rnn_w_fc"] = unit_rows(a["L1_attn_fc_w"].T)
    o["rnn_b_ih1"], o["rnn_b_hh1"] = a["L1_attn_b_ih_1"].reshape(2, 128).T, a["L1_attn_b_hh_1"].reshape(2, 128).T
    o["rnn_fc_b"] = a["L1_attn_fc_b"]
    w1 = a["L1_ffn_W1"].transpose(1, 0, 2).reshape(C, EXPERTS * MHID)
    o["moe_w1_even"] = np.concatenate([w1, zero(C, EXPERTS * MHID)])
    o["moe_w1_odd"] = np.concatenate([zero(C, EXPERTS * MHID), w1])
    o["moe_b1"] = a["L1_ffn_b1"].T
    o["moe_w2"] = np.concatenate([a["L1_ffn_W2"].transpose(1, 0, 2).reshape(MHID, EXPERTS * C), zero(MHID, C)], 1)
    o["moe_w_gate"] = zero(PW, PW)
    for b in range(2):
        o["moe_w_gate"][b * C:(b + 1) * C, b * EXPERTS:(b + 1) * EXPERTS] = a["L1_ffn_gate_w"]
    o["moe_gate_bias"] = np.tile(a["L1_ffn_gate_b"], B)
    o["moe_b2"] = by_batch_diagonal(a["L1_ffn_b2"])
    return {k: np.ascontiguousarray(v) for k, v in o.items()}


def kernel(**inputs):
    import concourse.bacc as bacc
    from concourse.bass_utils import run_bass_kernel_spmd

    nc = bacc.Bacc("TRN2", target_bir_lowering=False, num_devices=1)
    arrays = {f"in_{n}": v for n, v in lay_out({n: np.asarray(v) for n, v in inputs.items()}).items()}
    d = {n[3:]: nc.dram_tensor(n, v.shape, mybir.dt.from_np(v.dtype), kind="ExternalInput").ap()
         for n, v in arrays.items()}
    out = nc.dram_tensor("out", (NBLK, TB, BC), F32, kind="ExternalOutput").ap()
    build(nc, d, out)
    got = run_bass_kernel_spmd(nc, [arrays], core_ids=[0]).results[0]["out"]
    return np.ascontiguousarray(got.reshape(NBLK, TB, B, C).transpose(2, 0, 1, 3).reshape(B, TOKENS, C))
```

```python
from contextlib import ExitStack

import numpy as np

import concourse.bass as bass
from concourse import mybir

F32 = mybir.dt.float32
ALU = mybir.AluOpType
ACT = mybir.ActivationFunctionType
X = mybir.AxisListType.X

B, C, HT, WD = 8, 64, 56, 56
TOKENS = HT * WD
WS, NH = 4, 8
HEAD = C // NH
STRIPS = HT // WS
WCOLS = WD // WS
WINDOWS = B * WCOLS
WTOK = WS * WS
TB = 2 * WD
NBLK = TOKENS // TB
BC = B * C
PAIRS = B // 2
PW = 2 * C
MAXLEN = 512
BAND = (MAXLEN - 2 + TB) // TB + 1
HID = 256
EXPERTS = 8
MHID = 128
HALF_TOK = PAIRS * TB
STEP_LOOP = 64
XCHUNK = 16
QUAD = 32
EPS = 1e-5
NEG = -1.0e30


def pipeline(eng, stages, n, tail=0):
    head, most = 4, max(lag for lag, _ in stages)

    def step(t, n_blocks):
        for lag, stage in stages:
            if 0 <= t - lag < n_blocks:
                stage(t - lag, (t - lag) % 2)

    for t in range(head):
        step(t, n)
    with eng.Fori(head // 2, (n - tail) // 2) as pair:
        first = eng.snap(pair * 2)
        for par in range(2):
            for lag, stage in stages:
                stage(first + (par - lag), (par - lag) % 2)
    for t in range(n - tail, n + most):
        step(t, n)


def wait_count(eng, sem, i, per, offset):
    if isinstance(i, int) and i * per + offset <= 0:
        return
    eng.wait_ge(sem, i * per + offset)


def is_first(i):
    return isinstance(i, int) and i == 0


def wait_former(eng, sem, i, per=1, ago=2):
    wait_count(eng, sem, i, per, (1 - ago) * per)


def wait_load(eng, sems, i, par):
    eng.wait_ge(sems[par], i * 8 + (16 - 8 * par))


def block_cols(t, i, width=BC):
    return t[:, bass.ds(i * width, width)]


def by_batch(ap, n=B):
    return ap.rearrange("p (b c) -> p b c", b=n)


class Norm:

    def __init__(self, nc, ctx, hidden, name):
        sb = lambda n, s: ctx.enter_context(nc.sbuf_tensor(f"{name}_{n}", s, F32))
        sem = lambda n: ctx.enter_context(nc.semaphore(f"{name}_{n}"))
        self.hidden = hidden
        self.negmean = sb("negmean", [TB, 2, B])
        self.sumsq = sb("sumsq", [TB, 2, B])
        self.rstd = sb("rstd", [TB, 2, B])
        self.minus_half = sb("minus_half", [TB, B])
        self.centred = sb("centred", [TB, 2, BC])
        self.squares = sb("squares", [TB, 2, BC])
        self.xn = sb("xn", [TB, 2, BC])
        self.total_ready, self.mean_ready = sem("total_ready"), sem("mean_ready")
        self.centred_ready, self.squares_ready = sem("centred_ready"), sem("squares_ready")
        self.sumsq_ready, self.var_ready = sem("sumsq_ready"), sem("var_ready")
        self.rstd_ready, self.xn_ready = sem("rstd_ready"), sem("xn_ready")
        self.half_set = sem("half_set")

    def vector_centre(self, dve, i, par):
        h = by_batch(block_cols(self.hidden, i))
        dve.tensor_reduce(self.negmean[:, par], h, X, ALU.add).then_inc(self.total_ready, 1)
        dve.wait_ge(self.total_ready, i + 1)
        dve.tensor_scalar(self.negmean[:, par], self.negmean[:, par], -1.0 / C, None, ALU.mult)\
           .then_inc(self.mean_ready, 1)
        dve.wait_ge(self.mean_ready, i + 1)
        wait_former(dve, self.xn_ready, i)
        dve.tensor_tensor(by_batch(self.centred[:, par]), h,
                          self.negmean[:, par].unsqueeze(2).broadcast_to([TB, B, C]), ALU.add)\
           .then_inc(self.centred_ready, 1)

    def gpsimd_square(self, pool, i, par):
        pool.wait_ge(self.centred_ready, i + 1)
        wait_former(pool, self.sumsq_ready, i)
        pool.tensor_tensor(self.squares[:, par], self.centred[:, par], self.centred[:, par], ALU.mult)\
            .then_inc(self.squares_ready, 1)

    def vector_sum(self, dve, i, par):
        dve.wait_ge(self.squares_ready, i + 1)
        wait_former(dve, self.xn_ready, i)
        dve.tensor_reduce(self.sumsq[:, par], by_batch(self.squares[:, par]), X, ALU.add)\
           .then_inc(self.sumsq_ready, 1)
        dve.wait_ge(self.sumsq_ready, i + 1)
        dve.tensor_scalar(self.rstd[:, par], self.sumsq[:, par], 1.0 / C, EPS, ALU.mult, ALU.add)\
           .then_inc(self.var_ready, 1)

    def bind_centre(self, dve):
        return lambda i, par: self.vector_centre(dve, i, par)

    def bind_sum(self, dve):
        return lambda i, par: self.vector_sum(dve, i, par)

    def bind_square(self, pool):
        return lambda i, par: self.gpsimd_square(pool, i, par)

    def bind_scale(self, pool, turned, per=1):
        return lambda i, par: self.gpsimd_scale(pool, i, par, turned, per)

    def gpsimd_setup(self, pool):
        pool.memset(self.minus_half[:], -0.5).then_inc(self.half_set, 1)
        pool.wait_ge(self.half_set, 1)

    def gpsimd_scale(self, pool, i, par, turned, per):
        pool.wait_ge(self.var_ready, i + 1)
        pool.tensor_tensor(self.rstd[:, par], self.rstd[:, par], self.minus_half[:], ALU.pow)\
            .then_inc(self.rstd_ready, 1)
        pool.wait_ge(self.rstd_ready, i + 1)
        wait_former(pool, turned, i, per)
        pool.tensor_tensor(by_batch(self.xn[:, par]), by_batch(self.centred[:, par]),
                           self.rstd[:, par].unsqueeze(2).broadcast_to([TB, B, C]), ALU.mult)\
            .then_inc(self.xn_ready, 1)


def window_attention(nc, hidden, ident, bank, d):
    VHEADS = 5
    RING = (8, 4)
    SENT = (WTOK // 2, WTOK)
    with ExitStack() as ctx:
        sb = lambda n, s: ctx.enter_context(nc.sbuf_tensor(f"wa_{n}", s, F32))
        sem = lambda n: ctx.enter_context(nc.semaphore(f"wa_{n}"))
        K1 = C + 1
        xs = [sb(f"xs{p}", [K1, WTOK, WINDOWS]) for p in range(2)]
        w_qkv, w_out = sb("w_qkv", [K1, 3 * C]), sb("w_out", [K1, C])
        qkv = [sb(f"qkv{p}", [WINDOWS, WTOK, 3, HEAD, NH]) for p in range(2)]
        bias, last_bias = sb("bias", [WINDOWS, WTOK, WTOK]), sb("last_bias", [WINDOWS, WTOK, WTOK])
        colmask, rowmask = sb("colmask", [WINDOWS, WTOK, WTOK]), sb("rowmask", [WINDOWS, WTOK, WTOK])
        out = [sb(f"att_out{p}", [WINDOWS, WTOK, HEAD, NH]) for p in range(2)]
        outT = [sb(f"outT{p}", [K1, B, WS, WD]) for p in range(2)]
        groups = []
        for g, (h0, h1) in enumerate(((0, VHEADS), (VHEADS, NH))):
            n = h1 - h0
            groups.append(dict(
                heads=slice(h0, h1), n=n,
                score=[sb(f"score{g}{p}", [WINDOWS, WTOK, WTOK, n]) for p in range(2)],
                prod=[sb(f"prod{g}{k}", [WINDOWS, WTOK, WTOK, n]) for k in range(3)],
                top=sb(f"top{g}", [WINDOWS, WTOK, n]), total=sb(f"total{g}", [WINDOWS, WTOK, n]),
                inverse=[sb(f"inverse{g}{p}", [WINDOWS, WTOK, n]) for p in range(2)],
                part=sb(f"part{g}", [WINDOWS, RING[g], WTOK, HEAD, n]),
                banks=(bank[5:7], bank[7:8])[g],
                **{s: sem(f"{s}{g}") for s in ("qk_chain", "scored", "topped", "shifted", "exped",
                                               "summed", "inverted", "product", "weighted", "added", "done")}))
        p_qkv, p_outT, p_h = bank[0:2], bank[2], bank[3:5]
        loaded, ones_set, ready = sem("loaded"), sem("ones_set"), sem("ready")
        x_loaded = [sem(f"x_loaded{p}") for p in range(2)]
        qkv_mm, qkv_copied = sem("qkv_mm"), sem("qkv_copied")
        turned, turned_copied = sem("turned"), sem("turned_copied")
        projected, written = sem("projected"), sem("written")
        block = ctx.enter_context(nc.Block())

        @block.sync
        def _(sp):
            flat = lambda t: t[:].rearrange("p q k -> p (q k)")
            sp.dma_start(w_qkv[:], d["w_qkv"]).then_inc(loaded, 16)
            sp.dma_start(w_out[:], d["w_out"]).then_inc(loaded, 16)
            sp.dma_start(ident[:], d["ident"]).then_inc(loaded, 16)
            sp.dma_start(flat(bias), d["pos_bias"].partition_broadcast(WINDOWS)).then_inc(loaded, 16)
            sp.dma_start(flat(colmask), d["colmask"]).then_inc(loaded, 16)
            sp.dma_start(flat(rowmask), d["rowmask"].partition_broadcast(WINDOWS)).then_inc(loaded, 16)

            def load(i, par):
                wait_former(sp, qkv_mm, i, 8)
                sp.dma_start(xs[par][0:C].rearrange("c t w -> c (t w)"),
                             d["x"][bass.ds(i, 1)].rearrange("o c n -> (o c) n")).then_inc(x_loaded[par], 16)

            pipeline(sp, [(0, load)], STRIPS)

        @block.tensor
        def _(pe):
            pe.wait_ge(loaded, 96)
            pe.wait_ge(ones_set, 4)
            pe.wait_ge(ready, 3)

            def make_qkv(i, par):
                wait_load(pe, x_loaded, i, par)
                for t in range(WTOK):
                    if t % 2 == 0:
                        wait_count(pe, qkv_copied, i, 8, t // 2 - 1)
                    mm = pe.matmul(p_qkv[t // 2 % 2][0:WINDOWS, 192 * (t % 2):192 * (t % 2) + 192],
                                   xs[par][:, t], w_qkv[:], start=True, stop=True)
                    if t % 2:
                        mm.then_inc(qkv_mm, 1)

            def project(i, par):
                for g in groups:
                    pe.wait_ge(g["done"], i + 1)
                for r in range(WS):
                    wait_count(pe, turned_copied, i, 4, r)
                    for c in range(WS):
                        tr = pe.matmul(p_outT[0:C, c * WINDOWS:(c + 1) * WINDOWS],
                                       out[par][:, r * WS + c].rearrange("p e h -> p (e h)"),
                                       ident[0:WINDOWS, 0:WINDOWS], start=True, stop=True)
                    tr.then_inc(turned, 1)
                pe.wait_ge(turned_copied, i * 4 + 4)
                for half in range(2):
                    wait_count(pe, written, i, 2, half - 1)
                    for b in range(B):
                        mm = pe.matmul(p_h[half][0:TB, b * C:(b + 1) * C],
                                       outT[par][:, b, 2 * half:2 * half + 2, :].rearrange("c r w -> c (r w)"),
                                       w_out[:], start=True, stop=True)
                    mm.then_inc(projected, 1)

            def add_values(g, i, k, last, slot):
                if k == 0:
                    wait_former(pe, g["done"], i, ago=1)
                pe.wait_ge(g["weighted"], i * (last + 1) + (k + 1))
                n = len(g["banks"])
                for half, acc in enumerate(g["banks"]):
                    tokens = slice(half * WTOK // n, (half + 1) * WTOK // n)
                    mm = pe.matmul(acc[0:WINDOWS, 0:WTOK * HEAD * g["n"] // n], ident[0:WINDOWS, 0:WINDOWS],
                                   g["part"][:, slot, tokens].rearrange("p q e h -> p (q e h)"),
                                   start=(k == 0), stop=(k == last))
                mm.then_inc(g["added"], 1)

            def sum_values(i, par):
                for t in range(WTOK + 2):
                    if t < WTOK:
                        add_values(groups[1], i, t, WTOK - 1, t % RING[1])
                    quad, k = divmod(t - 4, 4)
                    if quad >= 0 and k < 2:
                        add_values(groups[0], i, 2 * quad + k, SENT[0] - 1, quad % 2 * 4 + 2 * k)

            pipeline(pe, [(3, project), (0, make_qkv), (1, sum_values)], STRIPS)

        @block.scalar
        def _(act):
            def copy_qkv(i, par):
                for g, sent in zip(groups, SENT):
                    wait_former(act, g["weighted"], i, sent)
                for t in range(WTOK // 2):
                    act.wait_ge(qkv_mm, i * 8 + (t + 1))
                    act.activation(qkv[par][:, 2 * t:2 * t + 2].rearrange("p t s e h -> p (t s e h)"),
                                   p_qkv[t % 2][0:WINDOWS, 0:384], ACT.Copy).then_inc(qkv_copied, 1)

            def exps(i, par):
                for g in groups:
                    act.wait_ge(g["shifted"], i + 1)
                    act.activation(g["score"][par][:], g["score"][par][:], ACT.Exp).then_inc(g["exped"], 1)

            def copy_out(i, par):
                wait_former(act, projected, i, 2)
                for r in range(WS):
                    act.wait_ge(turned, i * 4 + (r + 1))
                    for c in range(WS):
                        cp = act.activation(
                            outT[par][0:C, :, r, c::WS],
                            p_outT[0:C, c * WINDOWS:(c + 1) * WINDOWS].rearrange("p (b w) -> p b w", b=B),
                            ACT.Copy)
                    cp.then_inc(turned_copied, 1)
                for half in range(2):
                    act.wait_ge(projected, i * 2 + (half + 1))
                    act.activation(block_cols(hidden, i * 2 + half), p_h[half][0:TB, :], ACT.Copy)\
                       .then_inc(written, 1)

            pipeline(act, [(3, copy_out), (0, copy_qkv), (1, exps)], STRIPS)

        def scores(eng, g, i, par):
            score, shape = g["score"][par], [WINDOWS, WTOK, WTOK, g["n"]]
            q, k, _ = (qkv[par][:, :, s, :, g["heads"]] for s in range(3))
            steps = 2 * HEAD - 1
            eng.wait_ge(qkv_copied, i * 8 + 8)
            wait_former(eng, g["done"], i)

            def multiply(e):
                qe = q[:, :, e].unsqueeze(2).broadcast_to(shape)
                ke = k[:, :, e].unsqueeze(1).broadcast_to(shape)
                eng.tensor_tensor(g["prod"][e % 3][:] if e else score[:], qe, ke, ALU.mult)\
                   .then_inc(g["qk_chain"], 1)

            multiply(0)
            multiply(1)
            for e in range(1, HEAD):
                if e + 1 < HEAD:
                    multiply(e + 1)
                eng.wait_ge(g["qk_chain"], i * steps + 2 * e)
                eng.tensor_tensor(score[:], score[:], g["prod"][e % 3][:], ALU.add).then_inc(g["qk_chain"], 1)
            eng.wait_ge(g["qk_chain"], i * steps + steps)
            which = last_bias if isinstance(i, int) and i == STRIPS - 1 else bias
            eng.tensor_tensor(score[:], score[:], which[:].unsqueeze(3).broadcast_to(shape), ALU.add)\
               .then_inc(g["scored"], 1)

        def maximum(dve, g, i, par):
            dve.wait_ge(g["scored"], i + 1)
            wait_former(dve, g["shifted"], i, ago=1)
            dve.tensor_reduce(g["top"][:], g["score"][par][:].rearrange("p q k h -> p q h k"), X, ALU.max)\
               .then_inc(g["topped"], 1)

        def shift(eng, g, i, par):
            score = g["score"][par]
            eng.wait_ge(g["topped"], i + 1)
            eng.tensor_tensor(score[:], score[:], g["top"][:].unsqueeze(2).broadcast_to([WINDOWS, WTOK, WTOK, g["n"]]),
                              ALU.subtract).then_inc(g["shifted"], 1)

        def invert(dve, g, i, par):
            dve.wait_ge(g["exped"], i + 1)
            wait_former(dve, g["done"], i)
            dve.tensor_reduce(g["total"][:], g["score"][par][:].rearrange("p q k h -> p q h k"), X, ALU.add)\
               .then_inc(g["summed"], 1)
            dve.wait_ge(g["summed"], i + 1)
            dve.reciprocal(g["inverse"][par][:], g["total"][:]).then_inc(g["inverted"], 1)

        def weigh(eng, g, i, par, t, slot):
            oshape = [WINDOWS, WTOK, HEAD, g["n"]]
            return eng.tensor_tensor(g["part"][:, slot], g["score"][par][:, :, t].unsqueeze(2).broadcast_to(oshape),
                                     qkv[par][:, t, 2, :, g["heads"]].unsqueeze(1).broadcast_to(oshape), ALU.mult)

        def values(pool, g, i, par):
            pool.wait_ge(g["exped"], i + 1)
            for t in range(WTOK):
                wait_count(pool, g["added"], i, WTOK, t + 1 - RING[1])
                weigh(pool, g, i, par, t, t % RING[1]).then_inc(g["weighted"], 1)

        def paired_values(dve, g, i, par):
            dve.wait_ge(g["exped"], i + 1)
            for quad in range(WTOK // 4):
                at = quad % 2 * 4
                wait_count(dve, g["added"], i, SENT[0], 2 * quad - 2)
                for t in range(4):
                    weigh(dve, g, i, par, 4 * quad + t, at + t).then_inc(g["product"], 1)
                for t in (0, 2):
                    dve.wait_ge(g["product"], i * WTOK + (4 * quad + t + 2))
                    two = g["part"][:, at + t]
                    dve.tensor_tensor(two, two, g["part"][:, at + t + 1], ALU.add).then_inc(g["weighted"], 1)

        def normalise(dve, i, par):
            wait_former(dve, turned, i, 4)
            for g, sent in zip(groups, SENT):
                n, per = len(g["banks"]), WTOK // len(g["banks"])
                dve.wait_ge(g["added"], i * sent + sent)
                dve.wait_ge(g["inverted"], i + 1)
                for k, acc in enumerate(g["banks"]):
                    tokens = slice(k * per, (k + 1) * per)
                    mul = dve.tensor_tensor(
                        out[par][:, tokens, :, g["heads"]],
                        acc[0:WINDOWS, 0:per * HEAD * g["n"]].rearrange("p (q e h) -> p q e h", q=per, e=HEAD),
                        g["inverse"][par][:, tokens].unsqueeze(2).broadcast_to([WINDOWS, per, HEAD, g["n"]]), ALU.mult)
                mul.then_inc(g["done"], 1)

        @block.vector
        def _(dve):
            for t in (*xs, *outT):
                dve.memset(t[C:K1], 1.0).then_inc(ones_set, 1)
            dve.wait_ge(loaded, 96)
            dve.tensor_tensor(bias[:], bias[:], colmask[:], ALU.add).then_inc(ready, 1)
            dve.wait_ge(ready, 1)
            dve.tensor_tensor(last_bias[:], bias[:], rowmask[:], ALU.add).then_inc(ready, 1)
            dve.tensor_scalar(w_qkv[:, 0:C], w_qkv[:, 0:C], float(HEAD) ** -0.5, None, ALU.mult)\
               .then_inc(ready, 1)
            dve.wait_ge(ready, 3)
            own, other = groups

            def strip(i, par):
                maximum(dve, own, i, par)
                shift(dve, own, i, par)
                maximum(dve, other, i, par)
                invert(dve, own, i, par)
                invert(dve, other, i, par)
                paired_values(dve, own, i, par)

            pipeline(dve, [(1, lambda i, par: scores(dve, own, i, par)), (2, lambda i, par: normalise(dve, i, par)),
                           (1, strip)], STRIPS, tail=2)

        @block.gpsimd
        def _(pool):
            pool.wait_ge(ready, 3)
            own = groups[1]
            pipeline(pool, [(1, lambda i, par: scores(pool, own, i, par)),
                            (1, lambda i, par: shift(pool, own, i, par)),
                            (1, lambda i, par: values(pool, own, i, par))], STRIPS, tail=2)


def time_mixing(nc, hidden, ident, bank, d):
    with ExitStack() as ctx:
        sb = lambda n, s: ctx.enter_context(nc.sbuf_tensor(f"tm_{n}", s, F32))
        sem = lambda n: ctx.enter_context(nc.semaphore(f"tm_{n}"))
        norm = Norm(nc, ctx, hidden, "n1")
        weights = {n: [sb(f"{n}_{which}", [PW, PW]) for which in ("now", "before")] for n in "kvr"}
        mix = sb("mix", [PW, 3])
        w_o = sb("w_o", [PW, PW])
        toeplitz = sb("toeplitz", [TB, BAND + 1, TB])
        triangle, ones = sb("triangle", [TB, TB]), sb("ones", [TB, TB])
        xT = [sb(f"xT{p}", [PW, PAIRS, 1 + TB]) for p in range(2)]
        clipped = sb("clipped", [TB, 2, BC])
        k = [sb(f"k{p}", [TB, BC]) for p in range(2)]
        neg_r_exp = sb("neg_r_exp", [TB, 2, BC])
        den, inverse = sb("den", [TB, BC]), sb("inverse", [TB, BC])
        y = [sb(f"y{p}", [TB, BC]) for p in range(2)]
        yT = [sb(f"yT{p}", [PW, PAIRS, TB]) for p in range(2)]
        kv = sb("kv", [TB, (BAND + NBLK) * BC])
        k_before = [sb(f"k_before{p}", [TB, BC]) for p in range(2)]
        kv_far = [sb(f"kv_far{p}", [TB, BC]) for p in range(2)]
        p_x, p_k, p_v, p_r, p_sum, p_wkv, p_y, p_o = bank
        (loaded, zeroed, mixed, turned, turned_copied, k_mm, v_mm, r_mm, clip_done, k_ready, r_ready, kv_ready,
         before_ready, far_ready, wkv_mm, den_ready, inverse_ready, y_ready, y_turned, y_copied, o_mm, added) = (
            sem(n) for n in (
                "loaded", "zeroed", "mixed", "turned", "turned_copied", "k_mm", "v_mm", "r_mm", "clip_done",
                "k_ready", "r_ready", "kv_ready", "before_ready", "far_ready", "wkv_mm", "den_ready",
                "inverse_ready", "y_ready", "y_turned", "y_copied", "o_mm", "added"))
        kv_block = lambda slot: block_cols(kv, slot)
        block = ctx.enter_context(nc.Block())

        def load_half(eng, b):
            half = slice(b * C, b * C + C)
            eng.dma_start(mix[half], d["mix"]).then_inc(loaded, 16)
            for n in "kvr":
                for t in weights[n]:
                    eng.dma_start(t[half, half], d[f"w_{n}"]).then_inc(loaded, 16)
            eng.dma_start(w_o[half, half], d["w_o"]).then_inc(loaded, 16)

        @block.sync
        def _(sp):
            sp.wait_ge(zeroed, 8)
            load_half(sp, 0)
            sp.dma_start(toeplitz[:], d["toeplitz"]).then_inc(loaded, 16)

        @block.tensor
        def _(pe):
            pe.wait_ge(zeroed, 17)

            def turn(i, par):
                pe.wait_ge(norm.xn_ready, i + 1)
                wait_former(pe, turned_copied, i, ago=1)
                for p in range(PAIRS):
                    tr = pe.transpose(p_x[:, p * TB:(p + 1) * TB], norm.xn[:, par, p * PW:(p + 1) * PW],
                                      ident[0:TB, 0:TB])
                tr.then_inc(turned, 1)

            def older(i, par):
                pe.wait_ge(far_ready, i + 1)
                wait_former(pe, y_ready, i, ago=1)
                pe.matmul(p_wkv[0:TB, :], toeplitz[:, BAND], kv_far[par][:], start=True, stop=False)
                wait_former(pe, kv_ready, i, ago=1)
                for j in range(BAND - 1, 0, -1):
                    pe.matmul(p_wkv[0:TB, :], toeplitz[:, j], kv_block(i + (BAND - j)), start=False, stop=False)

            def project(i, par):
                if is_first(i):
                    pe.wait_ge(loaded, 18 * 16)
                    pe.wait_ge(mixed, 7)
                pe.wait_ge(turned_copied, i + 1)
                for n, into, read, made in (("k", p_k, clip_done, k_mm), ("v", p_v, kv_ready, v_mm),
                                            ("r", p_r, r_ready, r_mm)):
                    wait_former(pe, read, i, ago=1)
                    for p in range(PAIRS):
                        dst = into[0:TB, p * PW:(p + 1) * PW]
                        pe.matmul(dst, xT[par][:, p, 1:1 + TB], weights[n][0][:], start=True, stop=False)
                        mm = pe.matmul(dst, xT[par][:, p, 0:TB], weights[n][1][:], start=False, stop=True)
                    mm.then_inc(made, 1)

            def newest(i, par):
                pe.wait_ge(before_ready, i + 1)
                pe.matmul(p_sum[0:TB, :], ones[:], k_before[par][:], start=True, stop=False)
                pe.wait_ge(k_ready, i + 1)
                pe.matmul(p_sum[0:TB, :], triangle[:], k[par][:], start=False, stop=True)
                pe.wait_ge(kv_ready, i + 1)
                pe.matmul(p_wkv[0:TB, :], toeplitz[:, 0], kv_block(i + BAND), start=False, stop=True)\
                  .then_inc(wkv_mm, 1)

            def turn_y(i, par):
                pe.wait_ge(y_ready, i + 1)
                wait_former(pe, y_copied, i, ago=1)
                for p in range(PAIRS):
                    tr = pe.transpose(p_y[:, p * TB:(p + 1) * TB], y[par][:, p * PW:(p + 1) * PW], ident[0:TB, 0:TB])
                tr.then_inc(y_turned, 1)

            def output(i, par):
                pe.wait_ge(y_copied, i + 1)
                wait_former(pe, added, i, ago=1)
                for p in range(PAIRS):
                    mm = pe.matmul(p_o[0:TB, p * PW:(p + 1) * PW], yT[par][:, p], w_o[:], start=True, stop=True)
                mm.then_inc(o_mm, 1)

            pipeline(pe, [(1, project), (2, turn_y), (1, older), (2, output), (1, newest), (0, turn)], NBLK)

        @block.scalar
        def _(act):
            def copy_turned(i, par):
                act.wait_ge(turned, i + 1)
                wait_former(act, r_mm, i, ago=1)
                src = p_x[:, 0:HALF_TOK].rearrange("p (g t) -> p g t", g=PAIRS)
                act.activation(xT[par][:, :, 1:1 + TB], src, ACT.Copy)
                act.activation(xT[1 - par][:, :, 0:1], src[:, :, TB - 1:TB], ACT.Copy).then_inc(turned_copied, 1)

            def exp_k(i, par):
                act.wait_ge(clip_done, i + 1)
                wait_former(act, wkv_mm, i)
                wait_former(act, kv_ready, i)
                wait_count(act, before_ready, i, 1, 0)
                act.activation(k[par][:], clipped[:, par], ACT.Exp).then_inc(k_ready, 1)

            def exp_r(i, par):
                act.wait_ge(r_mm, i + 1)
                wait_former(act, y_ready, i)
                act.activation(neg_r_exp[:, par], p_r[0:TB, :], ACT.Exp, scale=-1.0).then_inc(r_ready, 1)

            def copy_y(i, par):
                act.wait_ge(y_turned, i + 1)
                wait_former(act, o_mm, i)
                act.activation(yT[par][:].rearrange("p g t -> p (g t)"), p_y[:, 0:HALF_TOK], ACT.Copy)\
                   .then_inc(y_copied, 1)

            act.wait_ge(zeroed, 8)
            load_half(act, 1)
            act.dma_start(triangle[:], d["triangle"]).then_inc(loaded, 16)
            act.wait_ge(zeroed, 17)
            pipeline(act, [(1, exp_k), (1, exp_r), (2, copy_y), (0, copy_turned)], NBLK)

        @block.vector
        def _(dve):
            for t in (*(t for n in "kvr" for t in weights[n]), w_o):
                dve.memset(t[:], 0.0).then_inc(zeroed, 1)
            dve.memset(ones[:], 1.0).then_inc(zeroed, 1)
            dve.memset(xT[0][:, :, 0:1], 0.0).then_inc(zeroed, 1)
            dve.memset(kv[:, 0:BAND * BC], 0.0).then_inc(zeroed, 1)
            for t in (*k_before, *kv_far):
                dve.memset(t[:], 0.0).then_inc(zeroed, 1)
            dve.memset(y[0][:], 0.0).then_inc(zeroed, 1)
            dve.memset(y[1][:], 0.0).then_inc(zeroed, 1)
            dve.memset(den[:], 0.0).then_inc(zeroed, 1)
            dve.wait_ge(zeroed, 17)

            def prepare():
                dve.wait_ge(loaded, 18 * 16)
                for j, n in enumerate("kvr"):
                    now, before = weights[n]
                    dve.tensor_scalar(now[:], now[:], mix[:, j:j + 1], None, ALU.mult).then_inc(mixed, 1)
                dve.wait_ge(mixed, 3)
                dve.tensor_scalar(mix[:], mix[:], -1.0, 1.0, ALU.mult, ALU.add).then_inc(mixed, 1)
                dve.wait_ge(mixed, 4)
                for j, n in enumerate("kvr"):
                    now, before = weights[n]
                    dve.tensor_scalar(before[:], before[:], mix[:, j:j + 1], None, ALU.mult).then_inc(mixed, 1)

            def clip(i, par):
                if is_first(i):
                    prepare()
                dve.wait_ge(k_mm, i + 1)
                wait_former(dve, k_ready, i)
                dve.tensor_scalar(clipped[:, par], p_k[0:TB, :], 30.0, -60.0, ALU.min, ALU.max)\
                   .then_inc(clip_done, 1)

            def multiply_kv(i, par):
                dve.wait_ge(v_mm, i + 1)
                dve.wait_ge(k_ready, i + 1)
                dve.tensor_tensor(kv_block(i + BAND), p_v[0:TB, :], k[par][:], ALU.mult).then_inc(kv_ready, 1)

            def combine(i, par):
                dve.wait_ge(wkv_mm, i + 1)
                dve.wait_ge(r_ready, i + 1)
                dve.scalar_tensor_tensor(den[:], neg_r_exp[:, par], 1.0, p_sum[0:TB, :], ALU.add, ALU.mult)\
                   .then_inc(den_ready, 1)
                dve.wait_ge(den_ready, i + 1)
                wait_former(dve, y_ready, i, ago=1)
                dve.reciprocal(inverse[:], den[:]).then_inc(inverse_ready, 1)
                dve.wait_ge(inverse_ready, i + 1)
                wait_former(dve, y_turned, i)
                dve.tensor_tensor(y[par][:], p_wkv[0:TB, :], inverse[:], ALU.mult).then_inc(y_ready, 1)

            def add(i, par):
                dve.wait_ge(o_mm, i + 1)
                h = block_cols(hidden, i)
                dve.tensor_tensor(h, h, p_o[0:TB, :], ALU.add).then_inc(added, 1)

            pipeline(dve, [(1, clip), (0, norm.bind_centre(dve)), (1, multiply_kv), (0, norm.bind_sum(dve)),
                           (2, add), (1, combine)], NBLK)

        @block.gpsimd
        def _(pool):
            norm.gpsimd_setup(pool)
            pool.wait_ge(zeroed, 17)

            def far(i, par):
                wait_former(pool, k_mm, i)
                wait_former(pool, far_ready, i, ago=1)
                pool.tensor_tensor(kv_far[par][:], kv_far[1 - par][:], kv_block(i), ALU.add).then_inc(far_ready, 1)

            def before(i, par):
                if isinstance(i, int) and i == 0:
                    pool.sem_inc(before_ready, 1)
                pool.wait_ge(k_ready, i + 1)
                wait_former(pool, wkv_mm, i, ago=1)
                pool.wait_ge(before_ready, i + 1)
                pool.tensor_tensor(k_before[1 - par][:], k_before[par][:], k[par][:], ALU.add)\
                    .then_inc(before_ready, 1)

            pipeline(pool, [(0, norm.bind_square(pool)), (1, before), (0, norm.bind_scale(pool, turned)), (0, far)], NBLK)


def first_of_maxima(dve, like, order, key, last, hot, then):
    shape = [TB, B, EXPERTS]
    then(dve.scalar_tensor_tensor(by_batch(key), by_batch(like), 0.0, by_batch(order), ALU.is_equal, ALU.mult))
    then(dve.tensor_reduce(last, by_batch(key), X, ALU.max))
    then(dve.tensor_tensor(by_batch(hot), by_batch(key), last.unsqueeze(2).broadcast_to(shape), ALU.is_equal))


def expert_choice(nc, hidden, ident, bank, d, xt):
    KH = HID // 128
    with ExitStack() as ctx:
        sb = lambda n, s: ctx.enter_context(nc.sbuf_tensor(f"ec_{n}", s, F32))
        sem = lambda n: ctx.enter_context(nc.semaphore(f"ec_{n}"))
        norm, norm_rnn = Norm(nc, ctx, hidden, "n2"), Norm(nc, ctx, hidden, "n3")
        w1 = [sb(f"w1_{which}", [PW, HID]) for which in ("even", "odd")]
        b1 = sb("b1", [128, KH])
        w_gate = sb("w_gate", [128, KH, B * EXPERTS])
        gate_bias, order = sb("gate_bias", [TB, B * EXPERTS]), sb("order", [TB, B * EXPERTS])
        w_down = sb("w_down", [128, KH, EXPERTS * C])
        b_down = sb("b_down", [128, BC])
        xT = [sb(f"xT2{p}", [PW, HALF_TOK]) for p in range(2)]
        hT = [sb(f"hT{p}", [128, KH, 2, HALF_TOK]) for p in range(2)]
        logits, shifted = sb("logits", [TB, B * EXPERTS]), sb("shifted", [TB, B * EXPERTS])
        exps, key, hot = (sb(n, [TB, B * EXPERTS]) for n in ("exps", "key", "hot"))
        top, total, inverse, last = (sb(n, [TB, B]) for n in ("top2", "total2", "inverse2", "last"))
        gates = [sb(f"gates{p}", [TB, B * EXPERTS]) for p in range(2)]
        gatesT = [sb(f"gatesT{p}", [128, TB]) for p in range(2)]
        weighted = [sb(f"weighted{p}", [TB, EXPERTS, C]) for p in range(2)]
        chosen = sb("chosen", [TB, BC])
        xT_rnn = [sb(f"xT_rnn{p}", [C, TB, B]) for p in range(2)]
        p_x, p_gate, p_bias, p_rnn = bank[0:4]
        p_gT = p_gate
        p_h, p_e = bank[4:6], bank[6:8]
        rnn_turned, rnn_copied = sem("rnn_turned"), sem("rnn_copied")
        stored = [sem(f"stored{p}") for p in range(2)]
        (loaded, zeroed, turned, turned_copied, h_mm, h_ready, gate_mm, chain, shift_done, exp_done, gates_ready,
         gates_turned, gates_copied, expert_mm, weighted_ready, chosen_ready, bias_mm, added) = (sem(n) for n in (
            "loaded", "zeroed", "turned", "turned_copied", "h_mm", "h_ready", "gate_mm", "chain", "shift_done",
            "exp_done", "gates_ready", "gates_turned", "gates_copied", "expert_mm", "weighted_ready",
            "chosen_ready", "bias_mm", "added"))
        block = ctx.enter_context(nc.Block())

        def tokens_of(par, m, b):
            return hT[par][:, m, b % 2, b // 2 * TB:(b // 2 + 1) * TB]

        @block.sync
        def _(sp):
            for t, n in ((w1[0], "ffn_w1_even"), (w1[1], "ffn_w1_odd"), (b1, "ffn_b1"), (w_gate, "ffn_w_gate"),
                         (w_down, "ffn_w_down"), (b_down, "ffn_b_down")):
                sp.dma_start(t[:], d[n]).then_inc(loaded, 16)
            sp.dma_start(gate_bias[:], d["ffn_gate_bias"].partition_broadcast(TB)).then_inc(loaded, 16)
            sp.dma_start(order[:], d["order"].partition_broadcast(TB)).then_inc(loaded, 16)

            def store(i, par):
                sp.wait_ge(rnn_copied, i * 2 + 2)
                sp.dma_start(block_cols(xt, i, TB * B), xT_rnn[par][:].rearrange("c t b -> c (t b)"))\
                  .then_inc(stored[par], 16)

            pipeline(sp, [(0, store)], NBLK)
            for s in stored:
                sp.wait_ge(s, NBLK // 2 * 16)

        @block.tensor
        def _(pe):
            pe.wait_ge(zeroed, 2)

            def turn(i, par):
                pe.wait_ge(norm.xn_ready, i + 1)
                wait_former(pe, turned_copied, i, ago=1)
                for p in range(PAIRS):
                    tr = pe.transpose(p_x[:, p * TB:(p + 1) * TB], norm.xn[:, par, p * PW:(p + 1) * PW],
                                      ident[0:TB, 0:TB])
                tr.then_inc(turned, 1)

            def hid(i, par):
                if is_first(i):
                    pe.wait_ge(loaded, 8 * 16)
                pe.wait_ge(turned_copied, i + 1)
                for n in range(2 * KH):
                    m, side = n // 2, n % 2
                    wait_count(pe, h_ready, i, 2 * KH, n - 1)
                    pe.matmul(p_h[n % 2][:, 0:HALF_TOK], w1[side][:, m * 128:(m + 1) * 128], xT[par][:],
                              start=True, stop=True).then_inc(h_mm, 1)

            def turn_gates(i, par):
                pe.wait_ge(gates_ready, i + 1)
                wait_former(pe, gates_copied, i, ago=1)
                pe.matmul(p_gT[0:B * EXPERTS, 0:TB], gates[par][:], ident[0:TB, 0:TB], start=True, stop=True)\
                  .then_inc(gates_turned, 1)

            def experts(i, par):
                for b in range(B):
                    if b == B // 2:
                        turn_gates(i, par)
                    wait_count(pe, weighted_ready, i, B, b - 1)
                    for m in range(KH):
                        mm = pe.matmul(p_e[b % 2][0:TB, :], tokens_of(par, m, b), w_down[:, m],
                                       start=(m == 0), stop=(m == KH - 1))
                    mm.then_inc(expert_mm, 1)
                pe.wait_ge(gates_copied, i + 1)
                wait_former(pe, added, i, 2, ago=1)
                pe.matmul(p_bias[0:TB, :], gatesT[par][:], b_down[:], start=True, stop=True).then_inc(bias_mm, 1)

            def gate(i, par):
                pe.wait_ge(h_ready, i * 2 * KH + 2 * KH)
                wait_former(pe, shift_done, i, ago=1)
                for b in range(B):
                    for m in range(KH):
                        mm = pe.matmul(p_gate[0:TB, b * EXPERTS:(b + B) * EXPERTS], tokens_of(par, m, b),
                                       w_gate[:, m], start=(m == 0), stop=(m == KH - 1))
                mm.then_inc(gate_mm, 1)

            def turn_rnn(i, par, half):
                pe.wait_ge(norm_rnn.xn_ready, i + 1)
                wait_count(pe, rnn_copied, i, 2, half)
                for b in range(B // 2):
                    at = (half * B // 2 + b) * C
                    mm = pe.matmul(p_rnn[0:C, b * TB:(b + 1) * TB], norm_rnn.xn[:, par, at:at + C], ident[0:TB, 0:TB],
                                   start=True, stop=True)
                mm.then_inc(rnn_turned, 1)

            pipeline(pe, [(1, hid), (2, experts), (3, lambda i, par: turn_rnn(i, par, 0)), (1, gate), (0, turn),
                          (3, lambda i, par: turn_rnn(i, par, 1))], NBLK)

        @block.scalar
        def _(act):
            def copy_turned(i, par):
                act.wait_ge(turned, i + 1)
                wait_former(act, h_mm, i, 2 * KH)
                act.activation(xT[par][:], p_x[:, 0:HALF_TOK], ACT.Copy).then_inc(turned_copied, 1)

            def gelu(i, par):
                if is_first(i):
                    act.wait_ge(loaded, 8 * 16)
                wait_former(act, expert_mm, i, B)
                for n in range(2 * KH):
                    act.wait_ge(h_mm, i * 2 * KH + (n + 1))
                    act.activation(hT[par][:, n // 2, n % 2], p_h[n % 2][:, 0:HALF_TOK], ACT.Gelu,
                                   bias=b1[:, n // 2:n // 2 + 1]).then_inc(h_ready, 1)

            def exp(i, par):
                act.wait_ge(shift_done, i + 1)
                wait_former(act, gates_ready, i, ago=1)
                act.activation(exps[:], shifted[:], ACT.Exp).then_inc(exp_done, 1)

            def copy_gates(i, par):
                act.wait_ge(gates_turned, i + 1)
                wait_former(act, bias_mm, i)
                act.activation(gatesT[par][0:B * EXPERTS], p_gT[0:B * EXPERTS, 0:TB], ACT.Copy)\
                   .then_inc(gates_copied, 1)

            def copy_rnn(i, par, half):
                act.wait_ge(rnn_turned, i * 2 + (half + 1))
                if half == 0:
                    wait_count(act, stored[par], i, 8, -8 * par)
                b0 = half * B // 2
                act.activation(xT_rnn[par][:, :, b0:b0 + B // 2].rearrange("c t b -> c b t"),
                               p_rnn[0:C, 0:HALF_TOK].rearrange("c (b t) -> c b t", b=B // 2), ACT.Copy)\
                   .then_inc(rnn_copied, 1)

            pipeline(act, [(1, gelu), (2, exp), (2, copy_gates), (3, lambda i, par: copy_rnn(i, par, 0)),
                           (0, copy_turned), (3, lambda i, par: copy_rnn(i, par, 1))], NBLK)

        @block.vector
        def _(dve):
            for t in gatesT:
                dve.memset(t[:], 0.0).then_inc(zeroed, 1)
            dve.wait_ge(zeroed, 2)

            shape = [TB, B, EXPERTS]

            def counter(i, made):
                made = [made]

                def then(ins):
                    made[0] += 1
                    ins.then_inc(chain, 1)
                    dve.wait_ge(chain, i * 7 + made[0])
                return then

            def choose(i, par):
                if is_first(i):
                    dve.wait_ge(loaded, 8 * 16)
                then = counter(i, 0)
                dve.wait_ge(gate_mm, i + 1)
                then(dve.tensor_tensor(logits[:], p_gate[0:TB, 0:B * EXPERTS], gate_bias[:], ALU.add))
                then(dve.tensor_reduce(top[:], by_batch(logits[:]), X, ALU.max))
                dve.tensor_tensor(by_batch(shifted[:]), by_batch(logits[:]),
                                  top[:].unsqueeze(2).broadcast_to(shape), ALU.subtract).then_inc(shift_done, 1)
                dve.wait_ge(shift_done, i + 1)
                first_of_maxima(dve, shifted[:], order[:], key[:], last[:], hot[:], then)

            def make_gates(i, par):
                then = counter(i, 5)
                dve.wait_ge(exp_done, i + 1)
                then(dve.tensor_reduce(total[:], by_batch(exps[:]), X, ALU.add))
                then(dve.reciprocal(inverse[:], total[:]))
                wait_former(dve, gates_turned, i)
                dve.tensor_tensor(by_batch(gates[par][:]), by_batch(hot[:]),
                                  inverse[:].unsqueeze(2).broadcast_to(shape), ALU.mult).then_inc(gates_ready, 1)
                dve.wait_ge(gates_ready, i + 1)

            def weigh(i, par):
                def sum_experts(b):
                    dve.wait_ge(weighted_ready, i * B + (b + 1))
                    dve.tensor_reduce(chosen[:, b * C:(b + 1) * C], weighted[b % 2][:].rearrange("p e c -> p c e"),
                                      X, ALU.add).then_inc(chosen_ready, 1)

                wait_former(dve, added, i, 2, ago=1)
                for b in range(B):
                    dve.wait_ge(expert_mm, i * B + (b + 1))
                    wait_count(dve, chosen_ready, i, B, b - 1)
                    dve.tensor_tensor(weighted[b % 2][:], p_e[b % 2][0:TB, :].rearrange("p (e c) -> p e c", e=EXPERTS),
                                      gates[par][:, b * EXPERTS:(b + 1) * EXPERTS].unsqueeze(2)
                                      .broadcast_to([TB, EXPERTS, C]), ALU.mult).then_inc(weighted_ready, 1)
                    if b:
                        sum_experts(b - 1)
                sum_experts(B - 1)

            def add(i, par):
                h = block_cols(hidden, i)
                dve.wait_ge(bias_mm, i + 1)
                dve.tensor_tensor(h, h, p_bias[0:TB, :], ALU.add).then_inc(added, 1)
                dve.wait_ge(chosen_ready, i * B + B)
                dve.wait_ge(added, i * 2 + 1)
                dve.tensor_tensor(h, h, chosen[:], ALU.add).then_inc(added, 1)

            def settle(i, par):
                wait_former(dve, norm_rnn.xn_ready, i)
                dve.wait_ge(added, i * 2 + 2)
                dve.memset(norm_rnn.rstd[:, par], 0.0)

            pipeline(dve, [(2, choose), (3, settle), (3, norm_rnn.bind_centre(dve)), (0, norm.bind_centre(dve)),
                           (3, norm_rnn.bind_sum(dve)), (0, norm.bind_sum(dve)), (2, make_gates), (2, weigh), (2, add)],
                     NBLK)

        @block.gpsimd
        def _(pool):
            norm.gpsimd_setup(pool)
            norm_rnn.gpsimd_setup(pool)
            pipeline(pool, [(3, norm_rnn.bind_square(pool)), (0, norm.bind_square(pool)),
                            (3, norm_rnn.bind_scale(pool, rnn_turned, 2)), (0, norm.bind_scale(pool, turned))], NBLK)


def recurrence(nc, ident, bank, d, xt, rnn_out):
    J, QUADS = HID // 128, 128 // QUAD
    QW = HID // QUADS
    CHUNKS = STEP_LOOP // XCHUNK
    LOOPS = TOKENS // STEP_LOOP
    LEAD = 24
    FIRST1 = 2
    FIRST0 = FIRST1 + LEAD
    EXTRA = -(-FIRST0 // XCHUNK)
    OUT_AT = {min((q + 1) * XCHUNK, STEP_LOOP - 1): q for q in range(CHUNKS)}
    with ExitStack() as ctx:
        sb = lambda n, s: ctx.enter_context(nc.sbuf_tensor(f"rn_{n}", s, F32))
        sem = lambda n: ctx.enter_context(nc.semaphore(f"rn_{n}"))
        x = sb("rnn_x", [128, STEP_LOOP, B])
        w_x = sb("w_x", [128, QUADS, QW])
        w_hh = [sb(f"w_hh{l}", [128, J, QUADS, QW]) for l in range(2)]
        w_up = sb("w_up", [128, J, QUADS, QW])
        bias, bias2 = sb("rnn_bias", [128, J]), sb("rnn_bias2", [128, J])
        w_fc, fc_bias = sb("w_fc", [128, J, C]), sb("fc_bias", [128, C])
        h = [sb(f"h{l}", [128, J, STEP_LOOP, B]) for l in range(2)]
        up = sb("up", [128, 2, 2, XCHUNK, B])
        fc = sb("fc", [128, CHUNKS, C])
        p_h = [bank[0:2], bank[2:4]]
        pre, p_fc, p_up = bank[4:6], bank[6], bank[7]
        at_pre = lambda s: slice(s % 2 * QW, (s % 2 + 1) * QW)
        at_up = lambda half: slice(half * XCHUNK * B, (half + 1) * XCHUNK * B)
        loaded, zeroed = sem("loaded"), sem("zeroed")
        x_loaded = [sem(f"x_loaded{q}") for q in range(CHUNKS)]
        summed = [sem("summed0"), sem("summed1")]
        turned = [sem("turned0"), sem("turned1")]
        h_ready = [sem("h_ready0"), sem("h_ready1")]
        up_mm, up_ready = sem("up_mm"), sem("up_ready")
        fc_free, fc_mm = sem("fc_free"), sem("fc_mm")
        stored = [sem(f"stored{q}") for q in range(CHUNKS)]
        rows = rnn_out.rearrange("n t (b c) -> (n t b) c", b=B)
        block = ctx.enter_context(nc.Block())

        @block.sync
        def _(sp):
            for t, n in ((w_x, "rnn_w_x"), (w_hh[0], "rnn_w_hh0"), (w_hh[1], "rnn_w_hh1"), (w_up, "rnn_w_up"),
                         (w_fc, "rnn_w_fc")):
                flat = "p a b c -> p (a b c)" if len(t.shape) == 4 else "p a b -> p (a b)"
                sp.dma_start(t[:].rearrange(flat), d[n]).then_inc(loaded, 16)
            sp.dma_start(bias[:], d["rnn_b_ih1"]).then_inc(loaded, 16)
            sp.dma_start(bias2[:], d["rnn_b_hh1"]).then_inc(loaded, 16)
            sp.dma_start(fc_bias[:], d["rnn_fc_b"].partition_broadcast(128)).then_inc(loaded, 16)

            def load(chunk, q):
                sp.dma_start(x[0:C, q * XCHUNK:(q + 1) * XCHUNK, :].rearrange("c t b -> c (t b)"),
                             block_cols(xt, chunk, XCHUNK * B)).then_inc(x_loaded[q], 16)

            def store(loop, q):
                sp.wait_ge(fc_free, loop * CHUNKS + (q + 2))
                sp.dma_start(rows[bass.ds((loop * CHUNKS + q) * XCHUNK * B, XCHUNK * B)], fc[:, q])\
                  .then_inc(stored[q], 16)

            for q in range(CHUNKS):
                load(q, q)
            with sp.Fori(1, LOOPS) as m:
                loop = sp.snap(m)
                for q in range(CHUNKS):
                    sp.wait_ge(summed[0], loop * STEP_LOOP + (q + 1 - CHUNKS) * XCHUNK)
                    load(loop * CHUNKS + q, q)
                    store(loop - 1, q)
            for q in range(EXTRA):
                sp.wait_ge(summed[0], TOKENS + (q + 1 - CHUNKS) * XCHUNK)
                load(TOKENS // XCHUNK - 1, q)
            for q in range(CHUNKS):
                store(LOOPS - 1, q)
            for q in range(CHUNKS):
                sp.wait_ge(stored[q], (LOOPS + 1) * 16)
                sp.wait_ge(x_loaded[q], (LOOPS + (q < EXTRA)) * 16)

        @block.tensor
        def _(pe):
            pe.wait_ge(loaded, 8 * 16)
            pe.wait_ge(zeroed, 7)

            def tile(dst, q, state, weights, start, stop):
                return pe.matmul(dst[QUAD * q:QUAD * q + B, 0:QW], state, weights, start=start, stop=stop,
                                 skip_group_check=True, tile_position=(0, QUAD * q))

            def recur(layer, dst, s):
                for j in range(J):
                    for q in range(QUADS):
                        mm = tile(dst, q, h[layer][:, j, (s - 1) % STEP_LOOP], w_hh[layer][:, j, q], False, j == J - 1)
                mm.then_inc(summed[layer], 1)

            def layer0(n, s):
                for q in range(QUADS):
                    tile(p_h[0][s % 2], q, x[:, s], w_x[:, q], True, False)
                pe.wait_ge(h_ready[0], n + 1)
                recur(0, p_h[0][s % 2], s)

            def layer1(n, s):
                for q in range(QUADS):
                    tile(p_h[1][s % 2], q, up[:, s // XCHUNK % 2, q // 2, s % XCHUNK],
                         ident[:, q % 2 * QW:(q % 2 + 1) * QW], True, False)
                pe.wait_ge(h_ready[1], n + 1)
                recur(1, p_h[1][s % 2], s)

            def up_products(s):
                half, j = divmod(s % XCHUNK, 2)
                first = (s // XCHUNK - 1) % CHUNKS * XCHUNK
                mm = pe.matmul(p_up[:, at_up(half)],
                               w_up[:, j, 2 * half:2 * half + 2].rearrange("p q u -> p (q u)"),
                               h[0][:, j, first:first + XCHUNK].rearrange("p t b -> p (t b)"),
                               start=(j == 0), stop=(j == J - 1))
                if s % XCHUNK == 3:
                    mm.then_inc(up_mm, 1)

            def outputs(loop, q):
                pe.wait_ge(h_ready[1], loop * STEP_LOOP + (q + 1) * XCHUNK + 1)
                pe.wait_ge(fc_free, loop * CHUNKS + (q + 1))
                for j in range(J):
                    mm = pe.matmul(p_fc[:, 0:C],
                                   h[1][:, j, q * XCHUNK:(q + 1) * XCHUNK].rearrange("p t b -> p (t b)"),
                                   w_fc[:, j], start=(j == 0), stop=(j == J - 1))
                mm.then_inc(fc_mm, 1)

            for n in range(FIRST0):
                if n % XCHUNK == 0:
                    pe.wait_ge(x_loaded[n // XCHUNK], 16)
                layer0(n, n)
                if n == LEAD:
                    pe.wait_ge(up_ready, 2)
                if n >= LEAD:
                    layer1(n - LEAD, n - LEAD)
                if n >= XCHUNK and n % XCHUNK < 4:
                    up_products(n)
            with pe.Fori(0, LOOPS) as m:
                loop = pe.snap(m)
                for s in range(STEP_LOOP):
                    s1, ahead = s + FIRST1, s + FIRST0
                    if ahead % XCHUNK == 0:
                        pe.wait_ge(x_loaded[ahead // XCHUNK % CHUNKS], loop * 16 + (16 if ahead < STEP_LOOP else 32))
                    layer0(loop * STEP_LOOP + ahead, ahead % STEP_LOOP)
                    if s1 % XCHUNK == 0:
                        pe.wait_ge(up_ready, loop * 2 * CHUNKS + (2 * (s1 // XCHUNK) + 2))
                    layer1(loop * STEP_LOOP + s1, s1 % STEP_LOOP)
                    if ahead % XCHUNK < 4:
                        up_products(ahead)
                    if s in OUT_AT:
                        outputs(loop, OUT_AT[s])

        @block.vector
        def _(dve):
            dve.memset(x[C:128], 0.0).then_inc(zeroed, 1)
            dve.wait_ge(zeroed, 1)
            dve.memset(x[C:C + 2], 1.0).then_inc(zeroed, 1)
            for layer in range(2):
                dve.memset(h[layer][:], 0.0).then_inc(h_ready[layer], 1)
            for t in bank[0:4]:
                dve.memset(t[:], 0.0).then_inc(zeroed, 1)
            for q in range(CHUNKS):
                dve.sem_inc(stored[q], 16)
            dve.memset(p_fc[:], 0.0).then_inc(fc_free, 1)
            dve.memset(fc[:], 0.0).then_inc(zeroed, 1)
            dve.wait_ge(loaded, 8 * 16)
            dve.wait_ge(zeroed, 7)

            def turn(layer, n, s):
                dve.wait_ge(summed[layer], n + 1)
                dve.transpose(pre[layer][:, at_pre(s)], p_h[layer][s % 2][:, 0:QW]).then_inc(turned[layer], 1)

            def copy_up(s, chunk):
                dve.wait_ge(up_mm, chunk + 1)
                for half in range(2):
                    dve.tensor_scalar(up[:, (s // XCHUNK - 1) % 2, half].rearrange("p t b -> p (t b)"),
                                      p_up[:, at_up(half)], bias[:, half:half + 1], bias2[:, half:half + 1],
                                      ALU.add, ALU.add).then_inc(up_ready, 1)

            def add_bias(loop, q):
                dve.wait_ge(fc_mm, loop * CHUNKS + (q + 1))
                dve.wait_ge(stored[q], (loop + 1) * 16)
                dve.tensor_tensor(fc[:, q], p_fc[:, 0:C], fc_bias[:], ALU.add).then_inc(fc_free, 1)

            for n in range(FIRST0):
                turn(0, n, n)
                if n >= LEAD:
                    turn(1, n - LEAD, n - LEAD)
                if n >= XCHUNK and n % XCHUNK == 4:
                    copy_up(n, 0)
            with dve.Fori(0, LOOPS) as m:
                loop = dve.snap(m)
                for s in range(STEP_LOOP):
                    ahead = s + FIRST0
                    turn(0, loop * STEP_LOOP + ahead, ahead)
                    turn(1, loop * STEP_LOOP + (s + FIRST1), s + FIRST1)
                    if ahead % XCHUNK == 4:
                        copy_up(ahead, loop * CHUNKS + (ahead // XCHUNK - 1))
                    if s in OUT_AT:
                        add_bias(loop, OUT_AT[s])

        @block.scalar
        def _(act):
            act.wait_ge(zeroed, 7)
            for layer in range(2):
                act.wait_ge(h_ready[layer], 1)

            def tanh(layer, n, s):
                act.wait_ge(turned[layer], n + 1)
                act.activation(h[layer][:, :, s % STEP_LOOP],
                               pre[layer][:, at_pre(s)].rearrange("p (j b) -> p j b", j=J)[:, :, 0:B], ACT.Tanh)\
                   .then_inc(h_ready[layer], 1)

            for n in range(FIRST0):
                tanh(0, n, n)
                if n >= LEAD:
                    tanh(1, n - LEAD, n - LEAD)
            with act.Fori(0, LOOPS) as m:
                loop = act.snap(m)
                for s in range(STEP_LOOP):
                    tanh(0, loop * STEP_LOOP + (s + FIRST0), s + FIRST0)
                    tanh(1, loop * STEP_LOOP + (s + FIRST1), s + FIRST1)


def expert_pairs(nc, hidden, ident, bank, d, rnn_out, out):
    with ExitStack() as ctx:
        sb = lambda n, s: ctx.enter_context(nc.sbuf_tensor(f"ep_{n}", s, F32))
        sem = lambda n: ctx.enter_context(nc.semaphore(f"ep_{n}"))
        norm = Norm(nc, ctx, hidden, "n4")
        w1 = [sb(f"m_w1_{which}", [PW, EXPERTS, MHID]) for which in ("even", "odd")]
        b1 = sb("m_b1", [MHID, EXPERTS])
        w2 = sb("m_w2", [MHID, EXPERTS * C])
        w_gate = sb("m_w_gate", [PW, PW])
        gate_bias, order = sb("m_gate_bias", [TB, B * EXPERTS]), sb("m_order", [TB, B * EXPERTS])
        b2 = sb("m_b2", [128, BC])
        rnn = [sb(f"rnn{p}", [TB, BC]) for p in range(2)]
        xT = [sb(f"xT4{p}", [PW, HALF_TOK]) for p in range(2)]
        hT = [sb(f"m_hT{p}", [MHID, 2, HALF_TOK]) for p in range(2)]
        logits, shifted, second = (sb(f"m_{n}", [TB, B * EXPERTS]) for n in ("logits", "shifted", "second"))
        exps, key, hot, hot2 = (sb(f"m_{n}", [TB, B * EXPERTS]) for n in ("exps", "key", "hot", "hot2"))
        top, total, inverse, last = (sb(f"m_{n}", [TB, B]) for n in ("top", "total", "inverse", "last"))
        gates = [sb(f"m_gates{p}", [TB, B * EXPERTS]) for p in range(2)]
        gatesT = [sb(f"m_gatesT{p}", [128, TB]) for p in range(2)]
        weighted = [sb(f"m_weighted{p}", [TB, BC]) for p in range(2)]
        acc = [sb(f"acc{p}", [TB, BC]) for p in range(2)]
        result = [sb(f"result{p}", [TB, BC]) for p in range(2)]
        p_x, p_gate, p_gT, p_bias = bank[0:4]
        p_h, p_y = bank[4:6], bank[6:8]
        (loaded, zeroed, rnn_added, turned, turned_copied, h_mm, h_ready, y_mm, gate_mm, chain, shift_done,
         exp_done, gates_ready, gates_turned, gates_copied, weighted_ready, acc_ready, bias_mm, partial,
         result_ready) = (sem(n) for n in (
             "loaded", "zeroed", "rnn_added", "turned", "turned_copied", "h_mm", "h_ready", "y_mm", "gate_mm",
             "chain", "shift_done", "exp_done", "gates_ready", "gates_turned", "gates_copied",
             "weighted_ready", "acc_ready", "bias_mm", "partial", "result_ready"))
        rnn_loaded, stored = ([sem(f"{n}{p}") for p in range(2)] for n in ("rnn_loaded", "stored"))
        block = ctx.enter_context(nc.Block())

        @block.sync
        def _(sp):
            def load(i, par):
                wait_former(sp, rnn_added, i)
                sp.dma_start(rnn[par][:], rnn_out[bass.ds(i, 1)].rearrange("o t f -> (o t) f"))\
                  .then_inc(rnn_loaded[par], 16)

            def store(i, par):
                sp.wait_ge(result_ready, i + 1)
                sp.dma_start(out[bass.ds(i, 1)].rearrange("o t f -> (o t) f"), result[par][:])\
                  .then_inc(stored[par], 16)

            pipeline(sp, [(0, load), (3, store)], NBLK)
            for s in stored:
                sp.wait_ge(s, NBLK // 2 * 16)

        @block.tensor
        def _(pe):
            pe.wait_ge(zeroed, 2)

            def turn(i, par):
                pe.wait_ge(norm.xn_ready, i + 1)
                wait_former(pe, turned_copied, i, ago=1)
                for p in range(PAIRS):
                    tr = pe.transpose(p_x[:, p * TB:(p + 1) * TB], norm.xn[:, par, p * PW:(p + 1) * PW],
                                      ident[0:TB, 0:TB])
                tr.then_inc(turned, 1)

            def gate(i, par):
                if is_first(i):
                    pe.wait_ge(loaded, 8 * 16)
                pe.wait_ge(turned_copied, i + 1)
                wait_former(pe, shift_done, i, ago=1)
                for p in range(PAIRS):
                    mm = pe.matmul(p_gate[0:TB, 2 * p * EXPERTS:2 * p * EXPERTS + PW], xT[par][:, p * TB:(p + 1) * TB],
                                   w_gate[:], start=True, stop=True)
                mm.then_inc(gate_mm, 1)

            def up(i, par, e):
                for side in range(2):
                    wait_count(pe, h_ready, i, 2 * EXPERTS, 2 * e + side - 1)
                    pe.matmul(p_h[side][:, 0:HALF_TOK], w1[side][:, e], xT[par][:], start=True, stop=True)\
                      .then_inc(h_mm, 1)

            def down(i, par, e):
                pe.wait_ge(h_ready, i * 2 * EXPERTS + (2 * e + 2))
                wait_count(pe, weighted_ready, i, EXPERTS, e - 1)
                for b in range(B):
                    mm = pe.matmul(p_y[e % 2][0:TB, b * C:(b + 1) * C],
                                   hT[e % 2][:, b % 2, b // 2 * TB:(b // 2 + 1) * TB], w2[:, e * C:(e + 1) * C],
                                   start=True, stop=True)
                mm.then_inc(y_mm, 1)

            def first_experts(i, par):
                for e in range(2):
                    up(i, par, e)
                down(i, par, 0)

            def other_experts(i, par):
                for e in range(2, EXPERTS):
                    up(i, par, e)
                    down(i, par, e - 1)
                down(i, par, EXPERTS - 1)

            def turn_gates(i, par):
                pe.wait_ge(gates_ready, i + 1)
                wait_former(pe, gates_copied, i, ago=1)
                pe.matmul(p_gT[0:B * EXPERTS, 0:TB], gates[par][:], ident[0:TB, 0:TB], start=True, stop=True)\
                  .then_inc(gates_turned, 1)

            def bias(i, par):
                pe.wait_ge(gates_copied, i + 1)
                wait_former(pe, partial, i, ago=1)
                pe.matmul(p_bias[0:TB, :], gatesT[par][:], b2[:], start=True, stop=True).then_inc(bias_mm, 1)

            pipeline(pe, [(2, turn_gates), (2, first_experts), (1, gate), (2, other_experts), (2, bias), (0, turn)], NBLK)

        @block.scalar
        def _(act):
            for t, n in ((w1[0], "moe_w1_even"), (w1[1], "moe_w1_odd"), (b1, "moe_b1"), (w2, "moe_w2"),
                         (w_gate, "moe_w_gate"), (b2, "moe_b2")):
                act.dma_start(t[:].rearrange("p a b -> p (a b)") if len(t.shape) == 3 else t[:], d[n])\
                  .then_inc(loaded, 16)
            act.dma_start(gate_bias[:], d["moe_gate_bias"].partition_broadcast(TB)).then_inc(loaded, 16)
            act.dma_start(order[:], d["order"].partition_broadcast(TB)).then_inc(loaded, 16)

            def copy_turned(i, par):
                act.wait_ge(turned, i + 1)
                wait_former(act, h_mm, i, 2 * EXPERTS)
                act.activation(xT[par][:], p_x[:, 0:HALF_TOK], ACT.Copy).then_inc(turned_copied, 1)

            def gelu(i, par, first, last):
                if is_first(i):
                    act.wait_ge(loaded, 8 * 16)
                for e in range(first, last):
                    wait_count(act, y_mm, i, EXPERTS, e - 1)
                    for side in range(2):
                        act.wait_ge(h_mm, i * 2 * EXPERTS + (2 * e + side + 1))
                        act.activation(hT[e % 2][:, side], p_h[side][:, 0:HALF_TOK], ACT.Gelu, bias=b1[:, e:e + 1])\
                           .then_inc(h_ready, 1)

            def exp(i, par):
                act.wait_ge(shift_done, i + 1)
                wait_former(act, gates_ready, i, ago=1)
                act.activation(exps[:], shifted[:], ACT.Exp).then_inc(exp_done, 1)

            def copy_gates(i, par):
                act.wait_ge(gates_turned, i + 1)
                wait_former(act, bias_mm, i)
                act.activation(gatesT[par][0:B * EXPERTS], p_gT[0:B * EXPERTS, 0:TB], ACT.Copy)\
                   .then_inc(gates_copied, 1)

            pipeline(act, [(2, copy_gates), (2, lambda i, par: gelu(i, par, 0, 3)), (1, exp),
                           (2, lambda i, par: gelu(i, par, 3, EXPERTS)), (0, copy_turned)], NBLK)

        @block.vector
        def _(dve):
            for t in gatesT:
                dve.memset(t[:], 0.0).then_inc(zeroed, 1)
            dve.wait_ge(zeroed, 2)

            def add_rnn(i, par):
                h = block_cols(hidden, i)
                wait_load(dve, rnn_loaded, i, par)
                dve.tensor_tensor(h, h, rnn[par][:], ALU.add).then_inc(rnn_added, 1)
                wait_former(dve, norm.xn_ready, i)
                dve.wait_ge(rnn_added, i + 1)
                dve.memset(norm.rstd[:, par], 0.0)

            spread = lambda t: t.unsqueeze(2).broadcast_to([TB, B, EXPERTS])

            def counter(i, made):
                made = [made]

                def then(ins):
                    made[0] += 1
                    ins.then_inc(chain, 1)
                    dve.wait_ge(chain, i * 15 + made[0])
                return then

            def choose(i, par):
                if is_first(i):
                    dve.wait_ge(loaded, 8 * 16)
                then = counter(i, 0)
                dve.wait_ge(gate_mm, i + 1)
                then(dve.tensor_tensor(logits[:], p_gate[0:TB, 0:B * EXPERTS], gate_bias[:], ALU.add))
                then(dve.tensor_reduce(top[:], by_batch(logits[:]), X, ALU.max))
                dve.tensor_tensor(by_batch(shifted[:]), by_batch(logits[:]), spread(top[:]), ALU.subtract)\
                   .then_inc(shift_done, 1)
                dve.wait_ge(shift_done, i + 1)
                first_of_maxima(dve, shifted[:], order[:], key[:], last[:], hot[:], then)
                then(dve.scalar_tensor_tensor(second[:], hot[:], NEG, shifted[:], ALU.mult, ALU.add))
                then(dve.tensor_reduce(top[:], by_batch(second[:]), X, ALU.max))
                then(dve.tensor_tensor(by_batch(second[:]), by_batch(second[:]), spread(top[:]), ALU.subtract))
                first_of_maxima(dve, second[:], order[:], key[:], last[:], hot2[:], then)
                then(dve.tensor_tensor(hot[:], hot[:], hot2[:], ALU.add))

            def make_gates(i, par):
                then = counter(i, 12)
                dve.wait_ge(exp_done, i + 1)
                then(dve.tensor_reduce(total[:], by_batch(exps[:]), X, ALU.add))
                then(dve.reciprocal(inverse[:], total[:]))
                then(dve.tensor_tensor(by_batch(hot[:]), by_batch(hot[:]), spread(inverse[:]), ALU.mult))
                wait_former(dve, gates_turned, i)
                dve.tensor_tensor(gates[par][:], hot[:], exps[:], ALU.mult).then_inc(gates_ready, 1)
                dve.wait_ge(gates_ready, i + 1)

            def weigh(i, par, first, last):
                for e in range(first, last):
                    dve.wait_ge(y_mm, i * EXPERTS + (e + 1))
                    wait_count(dve, acc_ready, i, EXPERTS - 1, max(e - 1, 0))
                    dve.tensor_tensor(by_batch(weighted[e % 2][:]), by_batch(p_y[e % 2][0:TB, :]),
                                      gates[par][:, e::EXPERTS].unsqueeze(2).broadcast_to([TB, B, C]), ALU.mult)\
                       .then_inc(weighted_ready, 1)

            def finish(i, par):
                dve.wait_ge(bias_mm, i + 1)
                wait_count(dve, stored[par], i, 8, -8 * par)
                dve.tensor_tensor(result[par][:], block_cols(hidden, i), p_bias[0:TB, :], ALU.add)\
                   .then_inc(partial, 1)
                dve.wait_ge(partial, i + 1)
                dve.wait_ge(acc_ready, (i + 1) * (EXPERTS - 1))
                dve.tensor_tensor(result[par][:], result[par][:], acc[par][:], ALU.add).then_inc(result_ready, 1)

            weigh_some = lambda first, last: lambda i, par: weigh(i, par, first, last)
            pipeline(dve, [(3, finish), (2, weigh_some(0, 1)), (1, choose), (2, weigh_some(1, 3)), (0, add_rnn),
                           (0, norm.bind_centre(dve)), (2, weigh_some(3, 4)), (0, norm.bind_sum(dve)),
                           (1, make_gates), (2, weigh_some(4, EXPERTS))], NBLK)

        @block.gpsimd
        def _(pool):
            norm.gpsimd_setup(pool)

            def accumulate(i, par, first, last):
                for e in range(first, last):
                    if e == 1:
                        wait_former(pool, result_ready, i)
                    pool.wait_ge(weighted_ready, i * EXPERTS + (e + 1))
                    if e > 1:
                        pool.wait_ge(acc_ready, i * (EXPERTS - 1) + (e - 1))
                    pool.tensor_tensor(acc[par][:], acc[par][:] if e > 1 else weighted[0][:], weighted[e % 2][:],
                                       ALU.add).then_inc(acc_ready, 1)

            add_some = lambda first, last: lambda i, par: accumulate(i, par, first, last)
            pipeline(pool, [(2, add_some(1, 3)), (0, norm.bind_square(pool)), (2, add_some(3, 4)),
                            (0, norm.bind_scale(pool, turned)), (2, add_some(4, EXPERTS))], NBLK)


def build(nc, d, out):
    with ExitStack() as ctx:
        hidden = ctx.enter_context(nc.sbuf_tensor("hidden", [TB, NBLK * BC], F32))
        ident = ctx.enter_context(nc.sbuf_tensor("identity", [128, 128], F32))
        bank = [ctx.enter_context(nc.psum_tensor(f"bank{k}", [128, 512], F32)) for k in range(8)]
        xt = nc.dram_tensor("normed_turned", (C, TOKENS * B), F32, kind="Internal").ap()
        rnn_out = nc.dram_tensor("rnn_out", (NBLK, TB, BC), F32, kind="Internal").ap()
        window_attention(nc, hidden, ident, bank, d)
        time_mixing(nc, hidden, ident, bank, d)
        expert_choice(nc, hidden, ident, bank, d, xt)
        recurrence(nc, ident, bank, d, xt, rnn_out)
        expert_pairs(nc, hidden, ident, bank, d, rnn_out, out)


def by_batch_diagonal(m):
    o = np.zeros((128, BC), np.float32)
    for b in range(B):
        o[b * EXPERTS:(b + 1) * EXPERTS, b * C:(b + 1) * C] = m
    return o


def lay_out(a):
    o = {"ident": np.eye(128, dtype=np.float32)}
    x = np.roll(a["x"], (-(WS // 2), -(WS // 2)), axis=(2, 3)).reshape(B, C, STRIPS, WS, WCOLS, WS)
    o["x"] = x.transpose(2, 1, 3, 5, 0, 4).reshape(STRIPS, C, WTOK * WINDOWS)
    o["w_qkv"] = np.concatenate([a["L0_tok_w1"], a["L0_tok_b1"][:, None]], 1)\
        .reshape(HEAD, NH, 3, C + 1).transpose(3, 2, 0, 1).reshape(C + 1, 3 * C)
    w2 = a["L0_tok_w2"].reshape(C, NH, HEAD).transpose(2, 1, 0).reshape(C, C)
    o["w_out"] = np.concatenate([w2, a["L0_tok_b2"][None]], 0)
    at = np.array([[i, j] for i in range(WS) for j in range(WS)])
    rel = at[None] - at[:, None] + WS - 1
    o["pos_bias"] = a["L0_tok_pos_emb"][rel[..., 0], rel[..., 1]].reshape(-1)
    low, right = at[:, 0] >= WS // 2, at[:, 1] >= WS // 2
    mask = lambda side: np.where(side[:, None] != side[None], np.float32(NEG), np.float32(0)).reshape(-1)
    o["rowmask"] = mask(low)
    o["colmask"] = np.zeros((B, WCOLS, WTOK * WTOK), np.float32)
    o["colmask"][:, -1] = mask(right)
    o["colmask"] = o["colmask"].reshape(WINDOWS, -1)
    for n in "kvr":
        o[f"w_{n}"] = a[f"L0_attn_W{n}"]
    o["w_o"] = a["L0_attn_Wo"]
    o["mix"] = np.stack([a[f"L0_attn_time_mix_{n}"].reshape(C) for n in "kvr"], 1)
    u, j, t = np.ogrid[0:TB, 0:BAND + 1, 0:TB]
    distance = j * TB + t - u
    distance[:, BAND] = MAXLEN
    o["toeplitz"] = np.where(distance < 0, np.float32(0), a["L0_attn_time_w"][np.clip(MAXLEN - 1 - distance, 0, MAXLEN - 1)])
    o["triangle"] = np.triu(np.ones((TB, TB), np.float32))
    zero = lambda *s: np.zeros(s, np.float32)
    w1 = a["L0_ffn_W1"]
    o["ffn_w1_even"] = np.concatenate([w1, zero(C, HID)])
    o["ffn_w1_odd"] = np.concatenate([zero(C, HID), w1])
    o["ffn_b1"] = a["L0_ffn_b1"].reshape(HID // 128, 128).T
    wg = a["L0_ffn_Wg"].reshape(HID // 128, 128, EXPERTS).transpose(1, 0, 2)
    o["ffn_w_gate"] = np.concatenate([wg, zero(128, HID // 128, (B - 1) * EXPERTS)], 2)
    o["ffn_gate_bias"] = np.tile(a["L0_ffn_bg"], B)
    o["order"] = np.tile(np.arange(EXPERTS, 0, -1, dtype=np.float32), B)
    o["ffn_w_down"] = a["L0_ffn_Wd"].reshape(EXPERTS, HID // 128, 128, C).transpose(2, 1, 0, 3)\
        .reshape(128, HID // 128, EXPERTS * C)
    o["ffn_b_down"] = by_batch_diagonal(a["L0_ffn_bd"])
    def unit_rows(m):
        return m.reshape(4, HID // 128, QUAD, -1).transpose(0, 2, 1, 3).reshape(128, -1)
    o["rnn_w_x"] = np.concatenate([a["L1_attn_W_ih_0"].T, a["L1_attn_b_ih_0"][None], a["L1_attn_b_hh_0"][None],
                                   zero(128 - C - 2, HID)])
    o["rnn_w_hh0"] = unit_rows(a["L1_attn_W_hh_0"].T)
    o["rnn_w_hh1"] = unit_rows(a["L1_attn_W_hh_1"].T)
    o["rnn_w_up"] = unit_rows(a["L1_attn_W_ih_1"].T)
    o["rnn_w_fc"] = unit_rows(a["L1_attn_fc_w"].T)
    o["rnn_b_ih1"], o["rnn_b_hh1"] = a["L1_attn_b_ih_1"].reshape(2, 128).T, a["L1_attn_b_hh_1"].reshape(2, 128).T
    o["rnn_fc_b"] = a["L1_attn_fc_b"]
    w1 = a["L1_ffn_W1"].transpose(1, 0, 2).reshape(C, EXPERTS * MHID)
    o["moe_w1_even"] = np.concatenate([w1, zero(C, EXPERTS * MHID)])
    o["moe_w1_odd"] = np.concatenate([zero(C, EXPERTS * MHID), w1])
    o["moe_b1"] = a["L1_ffn_b1"].T
    o["moe_w2"] = a["L1_ffn_W2"].transpose(1, 0, 2).reshape(MHID, EXPERTS * C)
    o["moe_w_gate"] = zero(PW, PW)
    for b in range(2):
        o["moe_w_gate"][b * C:(b + 1) * C, b * EXPERTS:(b + 1) * EXPERTS] = a["L1_ffn_gate_w"]
    o["moe_gate_bias"] = np.tile(a["L1_ffn_gate_b"], B)
    o["moe_b2"] = by_batch_diagonal(a["L1_ffn_b2"])
    return {k: np.ascontiguousarray(v) for k, v in o.items()}


def kernel(**inputs):
    import concourse.bacc as bacc
    from concourse.bass_utils import run_bass_kernel_spmd

    nc = bacc.Bacc("TRN2", target_bir_lowering=False, num_devices=1)
    arrays = {f"in_{n}": v for n, v in lay_out({n: np.asarray(v) for n, v in inputs.items()}).items()}
    d = {n[3:]: nc.dram_tensor(n, v.shape, mybir.dt.from_np(v.dtype), kind="ExternalInput").ap()
         for n, v in arrays.items()}
    out = nc.dram_tensor("out", (NBLK, TB, BC), F32, kind="ExternalOutput").ap()
    build(nc, d, out)
    got = run_bass_kernel_spmd(nc, [arrays], core_ids=[0]).results[0]["out"]
    return np.ascontiguousarray(got.reshape(NBLK, TB, B, C).transpose(2, 0, 1, 3).reshape(B, TOKENS, C))
```
